# Optimizing a Trainium2 kernel written in Bass

```python
import numpy as np
import jax
import jax.numpy as jnp

def _softmax(x, axis=-1):
    return jax.nn.softmax(x, axis=axis)

def _gelu(x):
    return jax.nn.gelu(x, approximate=True)

def _silu(x):
    return jax.nn.silu(x)

def _sigmoid(x):
    return jax.nn.sigmoid(x)

def _layernorm(x, axis=-1, eps=1e-05):
    m = jnp.mean(x, axis=axis, keepdims=True)
    v = jnp.var(x, axis=axis, keepdims=True)
    return (x - m) / jnp.sqrt(v + eps)

def _scatter_add(tgt, idx, src, axis=0):
    return tgt.at[idx].add(src)

def _segment_sum(src, seg, n):
    return jax.ops.segment_sum(src, seg, n)
kernel_name = 'mk_prb_d2_jaxref_r8_cfa3c7'

def setup_inputs(seed: int=0):
    np.random.seed(seed)
    _w = jnp.asarray

    def _L0_attn_setup():
        import jax, jax.numpy as jnp
        import numpy as np
        B, S, D = (2, 1024, 128)
        NH = 4
        DH = D // NH
        DHID = 2 * DH
        CHUNK = 256
        BASE_LR_INV = float(np.log(np.expm1(0.001)))
        NS_COEFFS = ((4.0848, -6.8946, 2.927), (3.9505, -6.3029, 2.6377), (3.7418, -5.5913, 2.3037), (2.8769, -3.1427, 1.2046), (2.8366, -3.0525, 1.2012))

        def rms_norm(x, w, eps=1e-06):
            return x * jax.lax.rsqrt(jnp.mean(x * x, axis=-1, keepdims=True) + eps) * w

        def l2_normalize(x):
            return x / (jnp.linalg.norm(x, axis=-1, keepdims=True) + 1e-05)

        def silu(x):
            return x * jax.nn.sigmoid(x)

        def newton_schulz5(G):
            trans = G.shape[1] > G.shape[2]
            X = jnp.swapaxes(G, 1, 2) if trans else G
            X = X / (jnp.linalg.norm(X, axis=(1, 2), keepdims=True) + 1e-07)
            for a, b, c in NS_COEFFS:
                A = X @ jnp.swapaxes(X, 1, 2)
                Bm = b * A + c * (A @ A)
                X = a * X + Bm @ X
            return jnp.swapaxes(X, 1, 2) if trans else X
        ks = jax.random.split(jax.random.key(seed), 8)
        f32 = jnp.float32
        return {'hidden_states': jax.random.normal(ks[0], (B, S, D), f32), 'qkv_w': jax.random.normal(ks[1], (3 * D, D), f32) / np.sqrt(D), 'q_norm_w': jnp.ones((D,), f32), 'k_norm_w': jnp.ones((D,), f32), 'lr_proj_w': jax.random.normal(ks[2], (3 * NH, D), f32) / np.sqrt(D), 'lr_proj_b': jnp.zeros((3 * NH,), f32), 'w0': jax.random.normal(ks[3], (NH, DHID, DH), f32) / np.sqrt(DH), 'w1': jax.random.normal(ks[4], (NH, DH, DHID), f32) / np.sqrt(DHID), 'w2': jax.random.normal(ks[5], (NH, DHID, DH), f32) / np.sqrt(DH)}
    _L0_attn_in = _L0_attn_setup()

    def _L0_ffn_setup():
        import jax, jax.numpy as jnp
        import numpy as np
        DIM = 128
        DEPTH = 2
        HEADS = 8
        DIM_HEAD = 64
        WINDOW = 64
        INNER = HEADS * DIM_HEAD
        HID = int(DIM * 4 * 2 / 3)
        B, N = (2, 1024)
        QK_SCALE = 8.0

        def shift_token(t):
            t1, t2 = jnp.split(t, 2, axis=-1)
            t2 = jnp.pad(t2, ((0, 0), (1, 0), (0, 0)))[:, :-1]
            return jnp.concatenate([t1, t2], axis=-1)

        def l2norm(t):
            return t / jnp.clip(jnp.linalg.norm(t, axis=-1, keepdims=True), 1e-12)

        def rotate_half(x):
            x1, x2 = jnp.split(x, 2, axis=-1)
            return jnp.concatenate([-x2, x1], axis=-1)

        def rotary_xpos(q, k):
            n = q.shape[-2]
            half_idx = jnp.arange(0, DIM_HEAD, 2, dtype=jnp.float32)
            inv_freq = 1.0 / 10000.0 ** (half_idx / DIM_HEAD)
            t = jnp.arange(n, dtype=jnp.float32)
            freqs = t[:, None] * inv_freq[None, :]
            freqs = jnp.concatenate([freqs, freqs], axis=-1)
            base = (half_idx + 0.4 * DIM_HEAD) / (1.4 * DIM_HEAD)
            power = (t - n // 2) / float(WINDOW // 2)
            scale = base[None, :] ** power[:, None]
            scale = jnp.concatenate([scale, scale], axis=-1)
            cos, sin = (jnp.cos(freqs), jnp.sin(freqs))
            q = q * cos * scale + rotate_half(q) * sin * scale
            k = k * cos / scale + rotate_half(k) * sin / scale
            return (q, k)

        def local_attention(q, k, v):
            b, h, n, d = q.shape
            w = n // WINDOW
            bq = q.reshape(b, h, w, WINDOW, d) * QK_SCALE
            bk = k.reshape(b, h, w, WINDOW, d)
            bv = v.reshape(b, h, w, WINDOW, d)

            def look_around(t):
                p = jnp.pad(t, ((0, 0), (0, 0), (1, 0), (0, 0), (0, 0)))
                return jnp.concatenate([p[:, :, :w], p[:, :, 1:]], axis=3)
            bk, bv = (look_around(bk), look_around(bv))
            bt = jnp.arange(n).reshape(w, WINDOW)
            btp = jnp.pad(bt, ((1, 0), (0, 0)), constant_values=-1)
            btk = jnp.concatenate([btp[:w], btp[1:]], axis=1)
            sim = jnp.einsum('bhwid,bhwjd->bhwij', bq, bk)
            i = bt[:, :, None]
            j = btk[:, None, :]
            mask = (i < j) | (i > j + WINDOW) | (j == -1)
            sim = jnp.where(mask, -jnp.finfo(sim.dtype).max, sim)
            attn = jax.nn.softmax(sim, axis=-1)
            out = jnp.einsum('bhwij,bhwjd->bhwid', attn, bv)
            return out.reshape(b, h, n, d)

        def _layer(x, wqkv, qs, ksc, wo, lg, lb, w1, b1, w2, b2):
            b, n, _ = x.shape
            h = shift_token(x)
            qkv = h @ wqkv
            q, k, v = jnp.split(qkv, 3, axis=-1)
            to_heads = lambda t: t.reshape(b, n, HEADS, DIM_HEAD).transpose(0, 2, 1, 3)
            q, k, v = (to_heads(q), to_heads(k), to_heads(v))
            q = l2norm(q) * qs
            k = l2norm(k) * ksc
            q, k = rotary_xpos(q, k)
            o = local_attention(q, k, v)
            o = o.transpose(0, 2, 1, 3).reshape(b, n, INNER)
            x = x + o @ wo
            h = shift_token(x)
            mu = h.mean(-1, keepdims=True)
            var = h.var(-1, keepdims=True)
            h = (h - mu) / jnp.sqrt(var + 1e-05) * lg + lb
            h = h @ w1 + b1
            a, g = jnp.split(h, 2, axis=-1)
            h = a * jax.nn.gelu(g, approximate=False)
            x = x + h @ w2 + b2
            return x
        key = jax.random.key(seed)
        ks = jax.random.split(key, 6)
        return {'x': jax.random.normal(ks[0], (B, N, DIM), jnp.float32), 'wqkv': jax.random.normal(ks[1], (DEPTH, DIM, 3 * INNER), jnp.float32) * 0.02, 'q_scale': jnp.ones((DEPTH, DIM_HEAD), jnp.float32), 'k_scale': jnp.ones((DEPTH, DIM_HEAD), jnp.float32), 'wo': jax.random.normal(ks[2], (DEPTH, INNER, DIM), jnp.float32) * 0.02, 'ln_g': jnp.ones((DEPTH, DIM), jnp.float32), 'ln_b': jnp.zeros((DEPTH, DIM), jnp.float32), 'w1': jax.random.normal(ks[3], (DEPTH, DIM, 2 * HID), jnp.float32) * 0.02, 'b1': jnp.zeros((DEPTH, 2 * HID), jnp.float32), 'w2': jax.random.normal(ks[4], (DEPTH, HID, DIM), jnp.float32) * 0.02, 'b2': jnp.zeros((DEPTH, DIM), jnp.float32)}
    _L0_ffn_in = _L0_ffn_setup()

    def _L1_attn_setup():
        import jax, jax.numpy as jnp
        import numpy as np
        B, S, D = (4, 256, 128)
        COMP_RATIO = 4
        TOP_K = 64
        key = jax.random.key(seed)
        ks = jax.random.split(key, 9)
        sd = 1.0 / np.sqrt(D)
        return {'x': jax.random.normal(ks[0], (B, S, D), dtype=jnp.float32), 'Wq': jax.random.normal(ks[1], (D, D), dtype=jnp.float32) * sd, 'bq': jnp.zeros((D,), dtype=jnp.float32), 'Wk': jax.random.normal(ks[2], (D, D), dtype=jnp.float32) * sd, 'bk': jnp.zeros((D,), dtype=jnp.float32), 'Wv': jax.random.normal(ks[3], (D, D), dtype=jnp.float32) * sd, 'bv': jnp.zeros((D,), dtype=jnp.float32), 'Wo': jax.random.normal(ks[4], (D, D), dtype=jnp.float32) * sd, 'bo': jnp.zeros((D,), dtype=jnp.float32)}
    _L1_attn_in = _L1_attn_setup()

    def _L1_ffn_setup():
        import jax, jax.numpy as jnp
        import numpy as np
        D_MODEL = 128
        NUM_EXPERTS = 8
        HIDDEN = 512
        TOP_K = 2
        key = jax.random.key(seed)
        ks = jax.random.split(key, 6)
        x = jax.random.normal(ks[0], (2, 128, D_MODEL), dtype=jnp.float32)
        gate_w = jax.random.normal(ks[1], (NUM_EXPERTS, D_MODEL), dtype=jnp.float32) * (1.0 / np.sqrt(D_MODEL))
        w1 = jax.random.normal(ks[2], (NUM_EXPERTS, HIDDEN, D_MODEL), dtype=jnp.float32) * (1.0 / np.sqrt(D_MODEL))
        b1 = jax.random.normal(ks[3], (NUM_EXPERTS, HIDDEN), dtype=jnp.float32) * 0.01
        w2 = jax.random.normal(ks[4], (NUM_EXPERTS, D_MODEL, HIDDEN), dtype=jnp.float32) * (1.0 / np.sqrt(HIDDEN))
        b2 = jax.random.normal(ks[5], (NUM_EXPERTS, D_MODEL), dtype=jnp.float32) * 0.01
        return {'x': x, 'gate_w': gate_w, 'w1': w1, 'b1': b1, 'w2': w2, 'b2': b2}
    _L1_ffn_in = _L1_ffn_setup()
    _d = {'L0_attn_hidden_states': _L0_attn_in['hidden_states'], 'L0_attn_qkv_w': _L0_attn_in['qkv_w'], 'L0_attn_q_norm_w': _L0_attn_in['q_norm_w'], 'L0_attn_k_norm_w': _L0_attn_in['k_norm_w'], 'L0_attn_lr_proj_w': _L0_attn_in['lr_proj_w'], 'L0_attn_lr_proj_b': _L0_attn_in['lr_proj_b'], 'L0_attn_w0': _L0_attn_in['w0'], 'L0_attn_w1': _L0_attn_in['w1'], 'L0_attn_w2': _L0_attn_in['w2'], 'L0_ffn_wqkv': _L0_ffn_in['wqkv'], 'L0_ffn_q_scale': _L0_ffn_in['q_scale'], 'L0_ffn_k_scale': _L0_ffn_in['k_scale'], 'L0_ffn_wo': _L0_ffn_in['wo'], 'L0_ffn_ln_g': _L0_ffn_in['ln_g'], 'L0_ffn_ln_b': _L0_ffn_in['ln_b'], 'L0_ffn_w1': _L0_ffn_in['w1'], 'L0_ffn_b1': _L0_ffn_in['b1'], 'L0_ffn_w2': _L0_ffn_in['w2'], 'L0_ffn_b2': _L0_ffn_in['b2'], 'L1_attn_Wq': _L1_attn_in['Wq'], 'L1_attn_bq': _L1_attn_in['bq'], 'L1_attn_Wk': _L1_attn_in['Wk'], 'L1_attn_bk': _L1_attn_in['bk'], 'L1_attn_Wv': _L1_attn_in['Wv'], 'L1_attn_bv': _L1_attn_in['bv'], 'L1_attn_Wo': _L1_attn_in['Wo'], 'L1_attn_bo': _L1_attn_in['bo'], 'L1_ffn_gate_w': _L1_ffn_in['gate_w'], 'L1_ffn_w1': _L1_ffn_in['w1'], 'L1_ffn_b1': _L1_ffn_in['b1'], 'L1_ffn_w2': _L1_ffn_in['w2'], 'L1_ffn_b2': _L1_ffn_in['b2']}
    _x0 = _d['L0_attn_hidden_states']
    _d['L0_attn_hidden_states'] = jax.random.normal(jax.random.fold_in(jax.random.key(seed), 1), (16, 256, 128), dtype=_x0.dtype)
    del _x0
    return _d

def reference(L0_attn_hidden_states, L0_attn_qkv_w, L0_attn_q_norm_w, L0_attn_k_norm_w, L0_attn_lr_proj_w, L0_attn_lr_proj_b, L0_attn_w0, L0_attn_w1, L0_attn_w2, L0_ffn_wqkv, L0_ffn_q_scale, L0_ffn_k_scale, L0_ffn_wo, L0_ffn_ln_g, L0_ffn_ln_b, L0_ffn_w1, L0_ffn_b1, L0_ffn_w2, L0_ffn_b2, L1_attn_Wq, L1_attn_bq, L1_attn_Wk, L1_attn_bk, L1_attn_Wv, L1_attn_bv, L1_attn_Wo, L1_attn_bo, L1_ffn_gate_w, L1_ffn_w1, L1_ffn_b1, L1_ffn_w2, L1_ffn_b2):

    def _L0_attn_ref(hidden_states, qkv_w, q_norm_w, k_norm_w, lr_proj_w, lr_proj_b, w0, w1, w2):
        import jax, jax.numpy as jnp
        import numpy as np
        B, S, D = (2, 1024, 128)
        NH = 4
        DH = D // NH
        DHID = 2 * DH
        CHUNK = 256
        BASE_LR_INV = float(np.log(np.expm1(0.001)))
        NS_COEFFS = ((4.0848, -6.8946, 2.927), (3.9505, -6.3029, 2.6377), (3.7418, -5.5913, 2.3037), (2.8769, -3.1427, 1.2046), (2.8366, -3.0525, 1.2012))

        def rms_norm(x, w, eps=1e-06):
            return x * jax.lax.rsqrt(jnp.mean(x * x, axis=-1, keepdims=True) + eps) * w

        def l2_normalize(x):
            return x / (jnp.linalg.norm(x, axis=-1, keepdims=True) + 1e-05)

        def silu(x):
            return x * jax.nn.sigmoid(x)

        def newton_schulz5(G):
            trans = G.shape[1] > G.shape[2]
            X = jnp.swapaxes(G, 1, 2) if trans else G
            X = X / (jnp.linalg.norm(X, axis=(1, 2), keepdims=True) + 1e-07)
            for a, b, c in NS_COEFFS:
                A = X @ jnp.swapaxes(X, 1, 2)
                Bm = b * A + c * (A @ A)
                X = a * X + Bm @ X
            return jnp.swapaxes(X, 1, 2) if trans else X
        b, s, d = hidden_states.shape
        qkv = hidden_states @ qkv_w.T
        q, k, v = jnp.split(qkv, 3, axis=-1)
        q = rms_norm(q, q_norm_w)
        k = rms_norm(k, k_norm_w)

        def to_heads(x):
            return x.reshape(b, s, NH, DH).transpose(0, 2, 1, 3).reshape(b * NH, s, DH)
        q = l2_normalize(to_heads(q))
        k = l2_normalize(to_heads(k))
        v = to_heads(v)
        lr = jax.nn.softplus(hidden_states @ lr_proj_w.T + lr_proj_b + BASE_LR_INV)
        lr = lr.reshape(b, s, NH, 3).transpose(0, 2, 1, 3).reshape(b * NH, s, 3)
        W0 = jnp.tile(w0, (b, 1, 1))
        W1 = jnp.tile(w1, (b, 1, 1))
        W2 = jnp.tile(w2, (b, 1, 1))
        n0 = jnp.linalg.norm(W0, axis=2, keepdims=True)
        n1 = jnp.linalg.norm(W1, axis=2, keepdims=True)
        n2 = jnp.linalg.norm(W2, axis=2, keepdims=True)
        nc = s // CHUNK

        def chunked(x):
            return x.reshape(b * NH, nc, CHUNK, -1).transpose(1, 0, 2, 3)
        qc, kc, vc, lrc = (chunked(q), chunked(k), chunked(v), chunked(lr))

        def renorm(w, n):
            return w / (jnp.linalg.norm(w, axis=2, keepdims=True) + 1e-05) * n

        def step(carry, xs):
            W0, W1, W2 = carry
            qi, ki, vi, li = xs
            l0, l1, l2 = (li[..., 0], li[..., 1], li[..., 2])
            gq = silu(jnp.einsum('bhd,bcd->bhc', W0, qi))
            hq = jnp.einsum('bhd,bcd->bhc', W2, qi)
            o = jnp.einsum('boh,bhc->bco', W1, gq * hq)
            gba = jnp.einsum('bhd,bcd->bhc', W0, ki)
            hbm = jnp.einsum('bhd,bcd->bhc', W2, ki)
            sg = silu(gba)
            hidden = sg * hbm
            dhid = jnp.einsum('boh,bco->bhc', W1, vi)
            dhbm = dhid * sg
            dgate = dhid * hbm
            sig = jax.nn.sigmoid(gba)
            dgba = dgate * sig * (1 + gba * (1 - sig))
            dw1 = jnp.einsum('bco,bhc,bc->boh', vi, hidden, l1)
            dw0 = jnp.einsum('bhc,bcd,bc->bhd', dgba, ki, l0)
            dw2 = jnp.einsum('bhc,bcd,bc->bhd', dhbm, ki, l2)
            dw0, dw1, dw2 = (newton_schulz5(dw0), newton_schulz5(dw1), newton_schulz5(dw2))
            W0 = renorm(W0 + dw0, n0)
            W1 = renorm(W1 + dw1, n1)
            W2 = renorm(W2 + dw2, n2)
            return ((W0, W1, W2), o)
        _, os_ = jax.lax.scan(step, (W0, W1, W2), (qc, kc, vc, lrc))
        out = os_.transpose(1, 0, 2, 3).reshape(b * NH, s, DH)
        return out.reshape(b, NH, s, DH).transpose(0, 2, 1, 3).reshape(b, s, d)

    def _L0_ffn_ref(x, wqkv, q_scale, k_scale, wo, ln_g, ln_b, w1, b1, w2, b2):
        import jax, jax.numpy as jnp
        import numpy as np
        DIM = 128
        DEPTH = 2
        HEADS = 8
        DIM_HEAD = 64
        WINDOW = 64
        INNER = HEADS * DIM_HEAD
        HID = int(DIM * 4 * 2 / 3)
        B, N = (2, 1024)
        QK_SCALE = 8.0

        def shift_token(t):
            t1, t2 = jnp.split(t, 2, axis=-1)
            t2 = jnp.pad(t2, ((0, 0), (1, 0), (0, 0)))[:, :-1]
            return jnp.concatenate([t1, t2], axis=-1)

        def l2norm(t):
            return t / jnp.clip(jnp.linalg.norm(t, axis=-1, keepdims=True), 1e-12)

        def rotate_half(x):
            x1, x2 = jnp.split(x, 2, axis=-1)
            return jnp.concatenate([-x2, x1], axis=-1)

        def rotary_xpos(q, k):
            n = q.shape[-2]
            half_idx = jnp.arange(0, DIM_HEAD, 2, dtype=jnp.float32)
            inv_freq = 1.0 / 10000.0 ** (half_idx / DIM_HEAD)
            t = jnp.arange(n, dtype=jnp.float32)
            freqs = t[:, None] * inv_freq[None, :]
            freqs = jnp.concatenate([freqs, freqs], axis=-1)
            base = (half_idx + 0.4 * DIM_HEAD) / (1.4 * DIM_HEAD)
            power = (t - n // 2) / float(WINDOW // 2)
            scale = base[None, :] ** power[:, None]
            scale = jnp.concatenate([scale, scale], axis=-1)
            cos, sin = (jnp.cos(freqs), jnp.sin(freqs))
            q = q * cos * scale + rotate_half(q) * sin * scale
            k = k * cos / scale + rotate_half(k) * sin / scale
            return (q, k)

        def local_attention(q, k, v):
            b, h, n, d = q.shape
            w = n // WINDOW
            bq = q.reshape(b, h, w, WINDOW, d) * QK_SCALE
            bk = k.reshape(b, h, w, WINDOW, d)
            bv = v.reshape(b, h, w, WINDOW, d)

            def look_around(t):
                p = jnp.pad(t, ((0, 0), (0, 0), (1, 0), (0, 0), (0, 0)))
                return jnp.concatenate([p[:, :, :w], p[:, :, 1:]], axis=3)
            bk, bv = (look_around(bk), look_around(bv))
            bt = jnp.arange(n).reshape(w, WINDOW)
            btp = jnp.pad(bt, ((1, 0), (0, 0)), constant_values=-1)
            btk = jnp.concatenate([btp[:w], btp[1:]], axis=1)
            sim = jnp.einsum('bhwid,bhwjd->bhwij', bq, bk)
            i = bt[:, :, None]
            j = btk[:, None, :]
            mask = (i < j) | (i > j + WINDOW) | (j == -1)
            sim = jnp.where(mask, -jnp.finfo(sim.dtype).max, sim)
            attn = jax.nn.softmax(sim, axis=-1)
            out = jnp.einsum('bhwij,bhwjd->bhwid', attn, bv)
            return out.reshape(b, h, n, d)

        def _layer(x, wqkv, qs, ksc, wo, lg, lb, w1, b1, w2, b2):
            b, n, _ = x.shape
            h = shift_token(x)
            qkv = h @ wqkv
            q, k, v = jnp.split(qkv, 3, axis=-1)
            to_heads = lambda t: t.reshape(b, n, HEADS, DIM_HEAD).transpose(0, 2, 1, 3)
            q, k, v = (to_heads(q), to_heads(k), to_heads(v))
            q = l2norm(q) * qs
            k = l2norm(k) * ksc
            q, k = rotary_xpos(q, k)
            o = local_attention(q, k, v)
            o = o.transpose(0, 2, 1, 3).reshape(b, n, INNER)
            x = x + o @ wo
            h = shift_token(x)
            mu = h.mean(-1, keepdims=True)
            var = h.var(-1, keepdims=True)
            h = (h - mu) / jnp.sqrt(var + 1e-05) * lg + lb
            h = h @ w1 + b1
            a, g = jnp.split(h, 2, axis=-1)
            h = a * jax.nn.gelu(g, approximate=False)
            x = x + h @ w2 + b2
            return x
        for l in range(DEPTH):
            x = _layer(x, wqkv[l], q_scale[l], k_scale[l], wo[l], ln_g[l], ln_b[l], w1[l], b1[l], w2[l], b2[l])
        return x

    def _L1_attn_ref(x, Wq, bq, Wk, bk, Wv, bv, Wo, bo):
        import jax, jax.numpy as jnp
        import numpy as np
        B, S, D = (4, 256, 128)
        COMP_RATIO = 4
        TOP_K = 64
        b, s, d = x.shape
        scale = 1.0 / jnp.sqrt(jnp.asarray(d, x.dtype))
        Q = x @ Wq + bq
        K = x @ Wk + bk
        V = x @ Wv + bv
        raw = jnp.einsum('bqd,bkd->bqk', Q, K) * scale
        causal = jnp.triu(jnp.ones((s, s), dtype=bool), k=1)
        w_scores = jnp.where(causal, jnp.asarray(-jnp.inf, raw.dtype), raw)
        w_attn = jax.nn.softmax(w_scores, axis=-1) @ V
        sc = s // COMP_RATIO
        Kc = K.reshape(b, sc, COMP_RATIO, d).mean(axis=2)
        Vc = V.reshape(b, sc, COMP_RATIO, d).mean(axis=2)
        c_scores = jnp.einsum('bqd,bkd->bqk', Q, Kc) * scale
        c_attn = jax.nn.softmax(c_scores, axis=-1) @ Vc
        top_vals, top_idx = jax.lax.top_k(raw, TOP_K)
        bi = jnp.arange(b)[:, None, None]
        si = jnp.arange(s)[None, :, None]
        sparse = jnp.zeros_like(raw).at[bi, si, top_idx].set(top_vals)
        s_attn = jax.nn.softmax(sparse, axis=-1) @ V
        out = (w_attn + c_attn + s_attn) / 3.0
        return out @ Wo + bo

    def _L1_ffn_ref(x, gate_w, w1, b1, w2, b2):
        import jax, jax.numpy as jnp
        import numpy as np
        D_MODEL = 128
        NUM_EXPERTS = 8
        HIDDEN = 512
        TOP_K = 2
        B, S, D = x.shape
        xf = x.reshape(-1, D)
        T = xf.shape[0]
        gate_logits = xf @ gate_w.T
        gate_probs = jax.nn.softmax(gate_logits, axis=-1)
        topk_scores, topk_idx = jax.lax.top_k(gate_probs, TOP_K)
        topk_scores = topk_scores / jnp.sum(topk_scores, axis=-1, keepdims=True)
        combine = jnp.zeros((T, NUM_EXPERTS), dtype=x.dtype)
        combine = combine.at[jnp.arange(T)[:, None], topk_idx].set(topk_scores)
        h = jax.nn.relu(jnp.einsum('td,ehd->teh', xf, w1) + b1)
        expert_out = jnp.einsum('teh,edh->ted', h, w2) + b2
        out = jnp.einsum('ted,te->td', expert_out, combine)
        return out.reshape(B, S, D)
    x = L0_attn_hidden_states
    xn = _layernorm(x, axis=-1)
    x = x + _L0_attn_ref(xn, L0_attn_qkv_w, L0_attn_q_norm_w, L0_attn_k_norm_w, L0_attn_lr_proj_w, L0_attn_lr_proj_b, L0_attn_w0, L0_attn_w1, L0_attn_w2) + _L0_ffn_ref(xn, L0_ffn_wqkv, L0_ffn_q_scale, L0_ffn_k_scale, L0_ffn_wo, L0_ffn_ln_g, L0_ffn_ln_b, L0_ffn_w1, L0_ffn_b1, L0_ffn_w2, L0_ffn_b2)
    xn = _layernorm(x, axis=-1)
    x = x + _L1_attn_ref(xn, L1_attn_Wq, L1_attn_bq, L1_attn_Wk, L1_attn_bk, L1_attn_Wv, L1_attn_bv, L1_attn_Wo, L1_attn_bo) + _L1_ffn_ref(xn, L1_ffn_gate_w, L1_ffn_w1, L1_ffn_b1, L1_ffn_w2, L1_ffn_b2)
    return x

_drawn_inputs = setup_inputs


def setup_inputs(seed=0):
    import zlib

    import numpy as np

    out = dict(_drawn_inputs(seed))
    spreads = {'L0_attn_q_norm_w': (1.0, 0.6),
     'L0_attn_k_norm_w': (1.0, 0.2),
     'L0_attn_lr_proj_b': (0.0, 0.1),
     'L0_ffn_q_scale': (1.0, 0.6),
     'L0_ffn_k_scale': (1.0, 0.6),
     'L0_ffn_ln_g': (1.0, 0.6),
     'L0_ffn_ln_b': (0.0, 0.8),
     'L0_ffn_b1': (0.0, 0.64),
     'L0_ffn_b2': (0.0, 0.1),
     'L1_attn_bq': (0.0, 2.0),
     'L1_attn_bk': (0.0, 2.0),
     'L1_attn_bv': (0.0, 0.1),
     'L1_attn_bo': (0.0, 0.1)}
    factors = {'L0_attn_qkv_w': 3.461,
     'L0_attn_w0': 3.615,
     'L0_attn_w1': 3.483,
     'L0_attn_w2': 3.56,
     'L0_ffn_w1': 3.222,
     'L0_ffn_w2': 3.257,
     'L1_ffn_b1': 32.625,
     'L1_ffn_b2': 22.29}
    for name, (base, spread) in spreads.items():
        noise = np.random.default_rng([zlib.crc32(name.encode()), seed]).standard_normal(out[name].shape)
        drawn = base * np.exp(spread * noise) if base else spread * noise
        out[name] = jnp.asarray(drawn.astype(out[name].dtype))
    for name, factor in factors.items():
        out[name] = (out[name] * factor).astype(out[name].dtype)
    return out
```

```python
import math
from contextlib import ExitStack

import concourse.bass as bass
from concourse import mybir

F32 = mybir.dt.float32
BF16 = mybir.dt.bfloat16
U32 = mybir.dt.uint32
ALU = mybir.AluOpType
ACT = mybir.ActivationFunctionType
AX_X = mybir.AxisListType.X

P = 128
B, S, D = 16, 256, 128
TILES = S // P
SLOTS = 2
PAIRS = B // SLOTS
NT = SLOTS * TILES
NH, DH, DHID = 4, 32, 64
DEPTH, HEADS, DIM_HEAD, WINDOW = 2, 8, 64, 64
INNER = HEADS * DIM_HEAD
HID = int(D * 4 * 2 / 3)
CH = [(c * P, min(P, HID - c * P)) for c in range((HID + P - 1) // P)]
EXPERTS, HIDDEN = 8, 512
EC = HIDDEN // P
COMP, TOP_K = 4, 64
SC = S // COMP
BIG = 3.0e38
DVE_LINKS = 208
POOL_LINKS = 16
ACT_LINKS = 18
LN_SCALE = 2.0 ** 16


def count(i, per_pair, k):
    return (i - 1) * per_pair + k + 1


def build(nc, x_d, out_d, w):
    ctx = ExitStack()
    with ctx:
        def sb(name, shape, dt=F32):
            return ctx.enter_context(nc.sbuf_tensor(name, shape, dt))

        def sem(name):
            return ctx.enter_context(nc.semaphore(name))

        ident = sb("ident", [P, P])
        identb = sb("identb", [P, P], BF16)
        band = sb("band", [P, TILES, P])
        bandb = sb("bandb", [P, TILES, P], BF16)
        causal = sb("causal", [P, P])
        rot_cos = sb("rot_cos", [P, TILES, 2, DIM_HEAD])
        rot_sin = sb("rot_sin", [P, TILES, 2, DIM_HEAD])
        qk_scale = sb("qk_scale", [P, DEPTH, 2, DIM_HEAD])
        tab_cos = sb("tab_cos", [P, DEPTH, TILES, 2, DIM_HEAD])
        tab_sin = sb("tab_sin", [P, DEPTH, TILES, 2, DIM_HEAD])
        iota8 = sb("iota8", [P, EXPERTS])
        third = sb("third", [P, 3])
        fw_q = sb("fw_q", [P, P])
        fw_gate = sb("fw_gate", [P, P])
        fw_up = sb("fw_up", [P, P])
        fw_down = sb("fw_down", [P, 2, 2 * DH])
        q_norm = sb("q_norm", [P, P])
        wqkv = sb("wqkv", [P, DEPTH, 3 * INNER])
        wo = sb("wo", [P, DEPTH, INNER // P, P])
        w1 = sb("w1", [P, DEPTH, 2 * HID])
        w2 = sb("w2", [P, DEPTH, len(CH), P])
        a_wq = sb("a_wq", [P, P])
        a_wk = sb("a_wk", [P, P])
        a_wv = sb("a_wv", [P, P])
        a_wo = sb("a_wo", [P, P])
        a_bqs = sb("a_bqs", [P, 1])
        a_bv = sb("a_bv", [P, P])
        a_bo = sb("a_bo", [P, P])
        m_gate = sb("m_gate", [P, EXPERTS])
        m_w1 = sb("m_w1", [P, EXPERTS, HIDDEN])
        m_w2 = sb("m_w2", [P, EXPERTS, EC, P])
        m_b2 = sb("m_b2", [EXPERTS, P])
        cols = sb("cols", [P, 2 * DEPTH * len(CH) + 3 * DEPTH + 2 + EXPERTS * EC])
        b1a = cols[:, 0:6].rearrange("p (l c) -> p l c", l=DEPTH)
        b1g = cols[:, 6:12].rearrange("p (l c) -> p l c", l=DEPTH)
        b2, ln_g, ln_b = cols[:, 12:14], cols[:, 14:16], cols[:, 16:18]
        a_bq, a_bk = cols[:, 18:19], cols[:, 19:20]
        m_b1 = cols[:, 20:52].rearrange("p (e c) -> p e c", e=EXPERTS)

        x0 = sb("x0", [P, NT, P])
        y_out = sb("y_out", [P, NT, P])
        stats = sb("stats", [P, NT, 6])
        meanvar = sb("meanvar", [P, NT, 2])
        rstd = sb("rstd", [P, NT])
        vareps = sb("vareps", [P, NT])
        newt = sb("newt", [P, NT, 16])
        ln_root = sb("ln_root", [P, 1])
        fw_n = sb("fw_n", [P, SLOTS, TILES + TILES * NH])
        fw_r = sb("fw_r", [P, SLOTS, TILES + TILES * NH])
        qk_n = sb("qk_n", [P, NT, 16])
        xn = sb("xn", [P, NT, P])
        xT = sb("xT", [P, SLOTS, S])
        x1T = sb("x1T", [P, SLOTS, S])
        hT = sb("hT", [P, SLOTS, S + 1])
        res = sb("res", [P, NT, P])
        ms0 = sb("ms0", [P, NT])
        hs0 = sb("hs0", [P, NT, NH])
        hr0 = sb("hr0", [P, NT, NH])
        q0 = sb("q0", [P, NT, P])
        q0s = sb("q0s", [P, NT, P])
        q0T = sb("q0T", [P, SLOTS, S])
        th = sb("th", [P, SLOTS, 2, S])
        bufA = sb("bufA", [P, NT, 16, DIM_HEAD])
        bufB = sb("bufB", [P, NT, 16, DIM_HEAD])
        bufC = sb("bufC", [P, NT, 16, DIM_HEAD])
        bufD = sb("bufD", [P, NT, 16, DIM_HEAD])
        ssq = sb("ssq", [P, NT, 16])
        qkT = sb("qkT", [P, SLOTS, 8, S])
        hnT = sb("hnT", [P, SLOTS, S])
        ge = sb("ge", [P, SLOTS, len(CH), S])
        yT = sb("yT", [P, SLOTS, S])
        g_l = sb("g_l", [P, NT, EXPERTS])
        g_m = sb("g_m", [P, NT, EXPERTS])
        g_i = sb("g_i", [P, NT, EXPERTS], U32)
        g_f = sb("g_f", [P, NT, EXPERTS])
        g_e = sb("g_e", [P, NT, EXPERTS])
        g_s = sb("g_s", [P, NT])
        comb = sb("comb", [P, NT, EXPERTS])
        combT = sb("combT", [EXPERTS, NT * P])
        top8 = sb("top8", [P, NT, 8])
        nmax = sb("nmax", [P, NT, 3])
        lsum = sb("lsum", [P, NT, 3])
        kcs = sb("kcs", [P, SLOTS, SC])

        v = bufD[:].rearrange("p (s t) a b -> p s (t a b)", s=SLOTS)[:, :, 0:3 * INNER].rearrange("p s (k n) -> p s k n", k=3)
        oT = bufA[:].rearrange("p (s t) a b -> p s (t a b)", s=SLOTS)[:, :, 0:4 * S].rearrange("p s (k n) -> p s k n", k=4)
        raw = [bufA[:, j].rearrange("p a b -> p (a b)") for j in range(NT)]
        wrk = [bufB[:, j].rearrange("p a b -> p (a b)") for j in range(NT)]
        a_qT = qkT[:, :, 0, :]
        a_kT = th[:].rearrange("p s a b -> p s (a b)")
        a_v = q0[:].rearrange("p (s t) n -> p s t n", s=SLOTS)
        a_pT = ge[:, :, 0:2, :]
        a_oT = xT
        hbuf = bufC[:, :, :, :].rearrange("p n a b -> p (n a b)").rearrange("p (e c n) -> p e c n", e=2, c=EC)

        ps = [ctx.enter_context(nc.psum_tensor(f"ps{s}", [P, 4, 512], F32)) for s in range(SLOTS)]

        loaded = sem("weights_loaded")
        x_loaded = sem("x_loaded")
        x_used = sem("x_used")
        stored = sem("stored")
        consts = sem("consts_ready")
        prep_a = sem("dve_prep")
        dlink = sem("dve_link")
        plink = sem("pool_link")
        alink = sem("act_link")
        names = """xn_ready xnT_done h0_ready q0_done q0_sq qn0_ready qT0_done qT0_ready gu_done th_ready hid_ready o0_done
        qk_done qk_sq qn_ready u_ready s_ready qkT_done qkT_ready v_done v_ready sim_done d_ready p_ready rl_ready pn_ready
        pT_done pT_ready oT_done oT_ready x1T_done h2_ready h2tok_done hn_ready hnT_done hnT_ready w1_done gelu_ready
        u2_ready x2T_done h1_ready x2T_ready x2_done y_ready yTp_done yT_ready proj_done qk1_ready kc_ready logit_ready
        e_ready comb_ready combT_done combT_ready b2_done acc0_ready sc_done raw_ready top_ready cm_ready cmax_ready
        sp_ready ex_ready pw_ready pwT_done pwT_ready at_done at_ready wo_done out_ready h_done relu_done eo_done
        acc_done var_ready rstd_ready fwn_ready fwr_ready qkn_ready qkr_ready""".split()
        g = {n: sem(n) for n in names}

        block = ctx.enter_context(nc.Block())
        NLOAD = 0

        @block.sync
        def _(sp):
            nonlocal NLOAD

            def load(dst, src):
                nonlocal NLOAD
                NLOAD += 1
                sp.dma_start(dst, src).then_inc(loaded, 16)

            xv = x_d.rearrange("b (t p) d -> p (b t) d", p=P)
            ov = out_d.rearrange("b (t p) d -> p (b t) d", p=P)
            sp.dma_start(x0[:], xv[:, 0:NT, :]).then_inc(x_loaded, 16)
            sp.wait_ge(consts, 1)
            load(ident[:], w["ident"])
            load(band[:], w["band"].rearrange("t p n -> p t n"))
            load(causal[:], w["causal"])
            load(rot_cos[:], w["rot_cos"].rearrange("(t p) a n -> p t a n", p=P))
            load(rot_sin[:], w["rot_sin"].rearrange("(t p) a n -> p t a n", p=P))
            load(qk_scale[:, :, 0, :], w["q_scale"].partition_broadcast(P))
            load(qk_scale[:, :, 1, :], w["k_scale"].partition_broadcast(P))
            load(iota8[:], w["iota8"].partition_broadcast(P))
            load(fw_q[:], w["fw_q"])
            load(q_norm[:], w["q_norm_w"].partition_broadcast(P))
            for h in range(NH):
                a, o = DH * h, DHID * (h % 2)
                load(fw_gate[a:a + DH, o:o + DHID], w["fw_w0"][h])
                load(fw_up[a:a + DH, o:o + DHID], w["fw_w2"][h])
                load(fw_down[o:o + DHID, h // 2, DH * (h % 2):DH * (h % 2 + 1)], w["fw_w1"][h])
            load(wqkv[:], w["wqkv"].rearrange("l p n -> p l n"))
            load(wo[:], w["wo"].rearrange("l (j p) n -> p l j n", p=P))
            load(w1[:], w["w1"].rearrange("l p n -> p l n"))
            for c, (o, n) in enumerate(CH):
                load(w2[0:n, :, c, :], w["w2"][:, o:o + n, :].rearrange("l p n -> p l n"))
            load(cols[:], w["cols"])
            for t, n in ((a_wq, "a_wq"), (a_wk, "a_wk"), (a_wv, "a_wv"), (a_wo, "a_wo"), (m_gate, "m_gate"),
                         (m_b2, "m_b2")):
                load(t[:], w[n])
            load(a_bv[:], w["a_bv"].partition_broadcast(P))
            load(a_bo[:], w["a_bo"].partition_broadcast(P))
            load(m_w1[:], w["m_w1"])
            load(m_w2[:], w["m_w2"])
            sp.sem_inc(stored, 16)
            with sp.Fori(1, PAIRS) as i:
                sp.wait_ge(x_used, count(i, SLOTS, SLOTS - 1))
                sp.dma_start(x0[:], xv[:, bass.ds(i * NT, NT), :]).then_inc(x_loaded, 16)
                sp.wait_ge(g["out_ready"], count(i, 1, 0))
                sp.dma_start(ov[:, bass.ds((i - 1) * NT, NT), :], y_out[:]).then_inc(stored, 16)
            sp.wait_ge(g["out_ready"], PAIRS)
            sp.dma_start(ov[:, (PAIRS - 1) * NT:PAIRS * NT, :], y_out[:]).then_inc(stored, 16)
            sp.wait_ge(stored, 16 * (PAIRS + 1))

        slots = range(SLOTS)
        tiles = range(TILES)

        def tok(t):
            return slice(t * P, (t + 1) * P)

        @block.gpsimd
        def _(pool):
            with pool.Fori(1, PAIRS + 1) as i:
                n_link = 0

                def link(ins):
                    nonlocal n_link
                    ins.then_inc(plink, 1)
                    n_link += 1
                    pool.wait_ge(plink, count(i, POOL_LINKS, n_link - 1))

                for l in range(DEPTH):
                    for s in slots:
                        for t in tiles:
                            j, k = 2 * s + t, 4 * l + 2 * s + t
                            pool.wait_ge(g["qn_ready"], count(i, 8, k))
                            for h in range(2):
                                src = bufB[:, j].rearrange("p (a h) n -> p a h n", a=2)[:, :, :, 32 * (1 - h):32 * (2 - h)]
                                dst = bufD[:, j].rearrange("p (a h) n -> p a h n", a=2)[:, :, :, 32 * h:32 * h + 32]
                                tab = tab_sin[:, l, t, :, 32 * h:32 * h + 32].unsqueeze(2).to_broadcast([P, 2, HEADS, 32])
                                last = nc.gpsimd.tensor_tensor(dst, src, tab, ALU.mult)
                            link(last)
                            pool.wait_ge(g["u_ready"], count(i, 8, k))
                            nc.gpsimd.tensor_tensor(bufC[:, j], bufC[:, j], bufD[:, j], ALU.add).then_inc(g["s_ready"], 1)
                    for s in slots:
                        for t in tiles:
                            j, k = 2 * s + t, 4 * l + 2 * s + t
                            pool.wait_ge(g["rl_ready"], count(i, 8, k))
                            pv = bufB[:, j].rearrange("p a b -> p (a b)").rearrange("p (h n) -> p h n", h=HEADS)
                            nc.gpsimd.tensor_tensor(pv, pv, ssq[:, j, 0:8].unsqueeze(2).to_broadcast([P, HEADS, P]),
                                                    ALU.mult).then_inc(g["pn_ready"], 1)
                for j in range(NT):
                    t = j % 2
                    pool.wait_ge(g["raw_ready"], count(i, NT, j))
                    cm = wrk[j][:, 512:512 + S]
                    pool.nop(nofuse=True)
                    if t == 1:
                        nc.gpsimd.tensor_copy(cm[:, 0:P], raw[j][:, 0:P])
                    nc.gpsimd.tensor_tensor(cm[:, tok(t)], raw[j][:, tok(t)], causal[:], ALU.add).then_inc(g["cm_ready"], 1)
                for j in range(NT):
                    pool.wait_ge(g["top_ready"], count(i, NT, j))
                    sel = bufD[:, j].rearrange("p a b -> p (a b)")[:, 0:S]
                    link(nc.gpsimd.tensor_tensor(sel, wrk[j][:, 0:S], raw[j][:, 0:S], ALU.subtract))
                    pool.nop(nofuse=True)
                    link(nc.gpsimd.tensor_scalar(sel, sel, 0.0, None, ALU.is_lt))
                    nc.gpsimd.tensor_tensor(sel, sel, raw[j][:, 0:S], ALU.mult).then_inc(g["sp_ready"], 1)
                assert n_link <= POOL_LINKS
                if n_link < POOL_LINKS:
                    pool.sem_inc(plink, POOL_LINKS - n_link)

        @block.scalar
        def _(act):
            act.wait_ge(prep_a, 3)
            with act.Fori(1, PAIRS + 1) as i:
                n_link = 0

                def rsqrt(out, x, scale, bias, ready):
                    nonlocal n_link
                    nc.scalar.activation(out, x, ACT.Ln, scale=scale).then_inc(alink, 1)
                    n_link += 1
                    act.wait_ge(alink, count(i, ACT_LINKS, n_link - 1))
                    nc.scalar.activation(out, out, ACT.Exp, scale=-0.5, bias=bias).then_inc(ready, 1)

                def ln_root_of(k):
                    s = k % 2
                    act.wait_ge(g["var_ready"], count(i, 8, k))
                    rsqrt(rstd[:, 2 * s:2 * s + 2], vareps[:, 2 * s:2 * s + 2], 1.0, 0.0, g["rstd_ready"])

                ln_root_of(0)
                ln_root_of(1)
                for s in slots:
                    act.wait_ge(g["xnT_done"], count(i, 2, s))
                    nc.scalar.copy(xT[:, s, :], ps[s][:, 0, 0:S])
                    nc.scalar.copy(hT[0:64, s, 0:S], ps[s][0:64, 0, 0:S])
                    nc.scalar.copy(hT[64:128, s, 1:S + 1], ps[s][64:128, 0, 0:S]).then_inc(g["h0_ready"], 1)
                for s in slots:
                    act.wait_ge(g["q0_done"], count(i, 2, s))
                    for t in tiles:
                        last = nc.scalar.activation(q0s[:, 2 * s + t], ps[s][:, 1, tok(t)], ACT.Square,
                                                    scale=float(D) ** -0.5, accum_out=ms0[:, 2 * s + t:2 * s + t + 1])
                    last.then_inc(g["q0_sq"], 1)
                for s in slots:
                    act.wait_ge(g["fwn_ready"], count(i, 2, s))
                    rsqrt(fw_r[:, s], fw_n[:, s], LN_SCALE, ln_root[:], g["fwr_ready"])
                for s in slots:
                    act.wait_ge(g["qT0_done"], count(i, 2, s))
                    nc.scalar.copy(q0T[:, s, :], ps[s][:, 0, 0:S]).then_inc(g["qT0_ready"], 1)
                for s in slots:
                    act.wait_ge(g["gu_done"], count(i, 2, s))
                    for p in range(2):
                        last = nc.scalar.activation(th[:, s, p, :], ps[s][:, 1 + p, 0:S], ACT.Tanh, scale=0.5)
                    last.then_inc(g["th_ready"], 1)
                for l in range(DEPTH):
                    for s in slots:
                        for t in tiles:
                            act.wait_ge(g["qk_done"], count(i, 8, 4 * l + 2 * s + t))
                            nc.scalar.activation(bufA[:, 2 * s + t].rearrange("p (a h) n -> p a (h n)", a=2),
                                                 ps[s][:, 2 * t:2 * t + 2, :], ACT.Square).then_inc(g["qk_sq"], 1)
                    for s in slots:
                        for t in tiles:
                            act.wait_ge(g["qkn_ready"], count(i, 8, 4 * l + 2 * s + t))
                            rsqrt(ssq[:, 2 * s + t], qk_n[:, 2 * s + t], LN_SCALE, ln_root[:], g["qkr_ready"])
                    for s in slots:
                        for t in tiles:
                            act.wait_ge(g["qkT_done"], count(i, 8, 4 * l + 2 * s + t))
                            nc.scalar.copy(qkT[:, s, :, tok(t)],
                                           ps[s][:, 2 * t:2 * t + 2, :].rearrange("p a (b n) -> p (a b) n", n=P)
                                           ).then_inc(g["qkT_ready"], 1)
                    for s in slots:
                        act.wait_ge(g["v_done"], count(i, 4, 2 * l + s))
                        nc.scalar.copy(v[:, s, 0:2, :], ps[s][:, 2:4, :])
                        nc.scalar.copy(v[0:64, s, 2, :], ps[s][0:64, 3, :])
                        nc.scalar.copy(v[64:128, s, 2, :], ps[s][64:128, 2, :]).then_inc(g["v_ready"], 1)
                    for s in slots:
                        for t in tiles:
                            j = 2 * s + t
                            act.wait_ge(g["d_ready"], count(i, 8, 4 * l + j))
                            nc.scalar.activation(bufB[:, j].rearrange("p a b -> p (a b)"), bufA[:, j].rearrange("p a b -> p (a b)"),
                                                 ACT.Exp, scale=8.0).then_inc(g["p_ready"], 1)
                    for s in slots:
                        for t in tiles:
                            j = 2 * s + t
                            act.wait_ge(g["pT_done"], count(i, 8, 4 * l + j))
                            nc.scalar.copy(bufC[:, j].rearrange("p (a h) n -> p a (h n)", a=2), ps[s][:, 2 * t:2 * t + 2, :]
                                           ).then_inc(g["pT_ready"], 1)
                    for s in slots:
                        for t in tiles:
                            act.wait_ge(g["oT_done"], count(i, 8, 4 * l + 2 * s + t))
                            nc.scalar.copy(oT[:, s, :, tok(t)], ps[s][:, 2 * t, :].rearrange("p (b n) -> p b n", n=P)
                                           ).then_inc(g["oT_ready"], 1)
                    for s in slots:
                        ln_root_of(2 + 2 * l + s)
                    for s in slots:
                        act.wait_ge(g["hnT_done"], count(i, 4, 2 * l + s))
                        nc.scalar.activation(hnT[:, s, :], ps[s][:, 2, 0:S], ACT.Identity, bias=ln_b[:, l:l + 1],
                                             scale=ln_g[:, l:l + 1]).then_inc(g["hnT_ready"], 1)
                    for s in slots:
                        act.wait_ge(g["w1_done"], count(i, 4, 2 * l + s))
                        for c, (o, n) in enumerate(CH):
                            src = ps[s][0:n, 3, c * S:(c + 1) * S] if c < 2 else ps[s][0:n, 2, 0:S]
                            last = nc.scalar.activation(ge[0:n, s, c, :], src, ACT.Gelu, bias=b1g[0:n, l, c:c + 1])
                        last.then_inc(g["gelu_ready"], 1)
                for s in slots:
                    ln_root_of(6 + s)
                for s in slots:
                    act.wait_ge(g["yTp_done"], count(i, 2, s))
                    nc.scalar.copy(yT[:, s, :], ps[s][:, 2, 0:S]).then_inc(g["yT_ready"], 1)
                for s in slots:
                    act.wait_ge(g["proj_done"], count(i, 2, s))
                    nc.scalar.activation(a_qT[:, s, :], ps[s][:, 0, 0:S], ACT.Identity, bias=a_bqs[:], scale=float(D) ** -0.5)
                    nc.scalar.activation(a_kT[:, s, 0:S], ps[s][:, 0, S:2 * S], ACT.Identity, bias=a_bk
                                         ).then_inc(g["qk1_ready"], 1)
                for s in slots:
                    act.wait_ge(g["logit_ready"], count(i, 2, s))
                    nc.scalar.activation(g_e[:, 2 * s:2 * s + 2, :], g_l[:, 2 * s:2 * s + 2, :], ACT.Exp).then_inc(g["e_ready"], 1)
                for j in range(NT):
                    s, t = j // 2, j % 2
                    act.wait_ge(g["sc_done"], count(i, NT, j))
                    nc.scalar.copy(raw[j][:, 0:S + SC], ps[s][:, t, 0:S + SC]).then_inc(g["raw_ready"], 1)
                act.wait_ge(g["combT_done"], count(i, 1, 0))
                nc.scalar.copy(combT[:], ps[1][0:EXPERTS, 3, :]).then_inc(g["combT_ready"], 1)

                def softmaxes(j):
                    act.wait_ge(g["sp_ready"], count(i, NT, j))
                    act.wait_ge(g["cmax_ready"], count(i, NT, j))
                    n = P * (j % 2 + 1)
                    sel = bufD[:, j].rearrange("p a b -> p (a b)")
                    nc.scalar.activation(sel[:, 256:512], sel[:, 0:S], ACT.Exp, bias=nmax[:, j, 0:1], accum_out=lsum[:, j, 0:1])
                    nc.scalar.activation(sel[:, 512:512 + n], wrk[j][:, 512:512 + n], ACT.Exp, bias=nmax[:, j, 1:2],
                                         accum_out=lsum[:, j, 1:2])
                    nc.scalar.activation(sel[:, 768:768 + SC], raw[j][:, S:S + SC], ACT.Exp, bias=nmax[:, j, 2:3],
                                         accum_out=lsum[:, j, 2:3]).then_inc(g["ex_ready"], 1)

                for e in range(EXPERTS):
                    for c in range(EC):
                        if c == 0 and e >= 2:
                            act.wait_ge(g["eo_done"], count(i, EXPERTS, e - 2))
                        k = EC * e + c
                        act.wait_ge(g["h_done"], count(i, EXPERTS * EC, k))
                        sl, bk = ((0, 2), (0, 3), (1, 2))[k % 3]
                        nc.scalar.activation(hbuf[:, e % 2, c, :], ps[sl][:, bk, :], ACT.Relu, bias=m_b1[:, e, c:c + 1]
                                             ).then_inc(g["relu_done"], 1)
                    if e % 2 == 1 and e >= 3:
                        softmaxes((e - 3) // 2)
                softmaxes(3)
                for s in slots:
                    for t in tiles:
                        act.wait_ge(g["pwT_done"], count(i, NT, 2 * s + t))
                        nc.scalar.copy(a_pT[:, s, :, tok(t)], ps[s][:, t, 0:S].rearrange("p (a n) -> p a n", n=P)
                                       ).then_inc(g["pwT_ready"], 1)
                    act.wait_ge(g["at_done"], count(i, 2, s))
                    nc.scalar.copy(a_oT[:, s, :], ps[s][:, 0, 0:S]).then_inc(g["at_ready"], 1)
                assert n_link == ACT_LINKS

        @block.vector
        def _(dve):
            def vt(out, a, b, op):
                return nc.vector.tensor_tensor(out, a, b, op)

            nc.vector.memset(fw_gate[:], 0.0)
            nc.vector.memset(fw_up[:], 0.0)
            nc.vector.memset(fw_down[:], 0.0)
            nc.vector.memset(hT[64:128, :, 0:1], 0.0)
            nc.vector.memset(ln_root[:], 0.5 * math.log(LN_SCALE))
            nc.vector.memset(third[:, 0:2], 1.0 / 3.0)
            nc.vector.memset(third[:, 2:3], 1.0 / (3.0 * COMP)).then_inc(consts, 1)
            dve.wait_ge(loaded, 16 * NLOAD)
            nc.vector.tensor_copy(identb[:], ident[:])
            nc.vector.tensor_copy(bandb[:], band[:])
            nc.vector.tensor_scalar_mul(a_bqs[:], a_bq, float(D) ** -0.5).then_inc(prep_a, 1)
            for l in range(DEPTH):
                for t in tiles:
                    vt(tab_cos[:, l, t], rot_cos[:, t], qk_scale[:, l], ALU.mult)
                    for h in range(2):
                        last = vt(tab_sin[:, l, t, :, 32 * h:32 * h + 32], rot_sin[:, t, :, 32 * h:32 * h + 32],
                                  qk_scale[:, l, :, 32 * (1 - h):32 * (2 - h)], ALU.mult)
                last.then_inc(prep_a, 1)
            dve.wait_ge(prep_a, 3)

            with dve.Fori(1, PAIRS + 1) as i:
                n_link = 0

                def link(ins):
                    nonlocal n_link
                    ins.then_inc(dlink, 1)
                    n_link += 1
                    dve.wait_ge(dlink, count(i, DVE_LINKS, n_link - 1))

                def after_wait(op, *args, **kw):
                    dve.nop(nofuse=True)
                    return op(*args, **kw)

                def newton(y, x, t):
                    link(nc.vector.scalar_tensor_tensor(t, y, -0.5, y, ALU.mult, ALU.mult))
                    link(vt(t, t, x, ALU.mult))
                    return nc.vector.scalar_tensor_tensor(y, t, 1.5, y, ALU.add, ALU.mult)

                def moments(s, src):
                    for t in tiles:
                        last = nc.vector.bn_stats(stats[:, 2 * s + t, :], src(t))
                    link(last)
                    for t in tiles:
                        last = after_wait(nc.vector.bn_aggr, meanvar[:, 2 * s + t, :], stats[:, 2 * s + t, :])
                    link(last)
                    nc.vector.tensor_scalar(vareps[:, 2 * s:2 * s + 2], meanvar[:, 2 * s:2 * s + 2, 1], 1e-5, None, ALU.add
                                            ).then_inc(g["var_ready"], 1)

                def normalise(s, k, src, ready):
                    dve.wait_ge(g["rstd_ready"], count(i, 8, k))
                    js = slice(2 * s, 2 * s + 2)
                    link(newton(rstd[:, js], vareps[:, js], newt[:, js, 0]))
                    for t in tiles:
                        j = 2 * s + t
                        last = nc.vector.tensor_scalar(xn[:, j], src(t), meanvar[:, j, 0:1], rstd[:, j:j + 1],
                                                       ALU.subtract, ALU.mult)
                    last.then_inc(ready, 1)

                dve.wait_ge(x_loaded, 16 * i)
                for s in slots:
                    moments(s, lambda t: x0[:, 2 * s + t])
                for s in slots:
                    normalise(s, s, lambda t: x0[:, 2 * s + t], g["xn_ready"])
                for s in slots:
                    dve.wait_ge(g["q0_done"], count(i, 2, s))
                    dve.wait_ge(g["q0_sq"], count(i, 2, s))
                    js = slice(2 * s, 2 * s + 2)
                    link(vt(q0[:, js], ps[s][:, 1, 0:S].rearrange("p (t n) -> p t n", t=2),
                            q_norm[:].unsqueeze(1).to_broadcast([P, 2, P]), ALU.mult))
                    link(vt(q0s[:, js], q0[:, js], q0[:, js], ALU.mult))
                    link(nc.vector.tensor_reduce(hs0[:, js], q0s[:, js].rearrange("p t (h n) -> p t h n", h=NH), AX_X, ALU.add))
                    nc.vector.tensor_scalar(fw_n[:, s, 0:TILES], ms0[:, js], 1e-6, None, ALU.add)
                    nc.vector.tensor_scalar(fw_n[:, s, TILES:], hs0[:, js].rearrange("p t h -> p (t h)"), 1e-24, None, ALU.max
                                            ).then_inc(g["fwn_ready"], 1)
                for s in slots:
                    js = slice(2 * s, 2 * s + 2)
                    dve.wait_ge(g["fwr_ready"], count(i, 2, s))
                    dve.wait_ge(g["fwn_ready"], count(i, 2, s))
                    link(newton(fw_r[:, s], fw_n[:, s], newt[:, 2 * s, 0:TILES + TILES * NH]))
                    rrb = fw_r[:, s, 0:TILES].unsqueeze(2).to_broadcast([P, 2, NH])
                    link(vt(hs0[:, js], hs0[:, js], fw_r[:, s, TILES:].rearrange("p (t h) -> p t h", t=TILES), ALU.mult))
                    link(vt(hs0[:, js], hs0[:, js], rrb, ALU.mult))
                    link(nc.vector.tensor_scalar(hs0[:, js], hs0[:, js], 1e-5, None, ALU.add))
                    link(after_wait(nc.vector.reciprocal, hr0[:, js], hs0[:, js]))
                    link(vt(hr0[:, js], hr0[:, js], rrb, ALU.mult))
                    vt(q0s[:, js].rearrange("p t (h n) -> p (t h) n", h=NH), q0[:, js].rearrange("p t (h n) -> p (t h) n", h=NH),
                       hr0[:, js].rearrange("p t h -> p (t h)").unsqueeze(2).to_broadcast([P, 2 * NH, DH]), ALU.mult
                       ).then_inc(g["qn0_ready"], 1)
                for s in slots:
                    dve.wait_ge(g["th_ready"], count(i, 2, s))
                    for p in range(2):
                        last = nc.vector.scalar_tensor_tensor(th[:, s, p], th[:, s, p], 1.0, ps[s][:, 1 + p, 0:S], ALU.add, ALU.mult)
                    link(last)
                    for p in range(2):
                        last = nc.vector.scalar_tensor_tensor(th[:, s, p], th[:, s, p], 0.5, ps[s][:, 1 + p, S:2 * S], ALU.mult, ALU.mult)
                    last.then_inc(g["hid_ready"], 1)
                for s in slots:
                    dve.wait_ge(g["o0_done"], count(i, 2, s))
                    vt(res[:, 2 * s:2 * s + 2], ps[s][:, 3, 0:S].rearrange("p (t n) -> p t n", t=2), x0[:, 2 * s:2 * s + 2],
                       ALU.add).then_inc(x_used, 1)

                for l in range(DEPTH):
                    for s in slots:
                        for t in tiles:
                            j, k = 2 * s + t, 4 * l + 2 * s + t
                            dve.wait_ge(g["qk_sq"], count(i, 8, k))
                            link(nc.vector.tensor_reduce(qk_n[:, j], bufA[:, j], AX_X, ALU.add))
                            nc.vector.tensor_scalar(qk_n[:, j], qk_n[:, j], 1e-24, None, ALU.max).then_inc(g["qkn_ready"], 1)
                    for s in slots:
                        for t in tiles:
                            j, k = 2 * s + t, 4 * l + 2 * s + t
                            dve.wait_ge(g["qkr_ready"], count(i, 8, k))
                            dve.wait_ge(g["qkn_ready"], count(i, 8, k))
                            link(newton(ssq[:, j], qk_n[:, j], newt[:, j]))
                            vt(bufB[:, j], ps[s][:, 2 * t:2 * t + 2, :].rearrange("p a (h n) -> p (a h) n", n=DIM_HEAD),
                               ssq[:, j].unsqueeze(2).to_broadcast([P, 16, DIM_HEAD]), ALU.mult).then_inc(g["qn_ready"], 1)
                            dve.wait_ge(g["qn_ready"], count(i, 8, k))
                            vt(bufC[:, j].rearrange("p (a h) n -> p a h n", a=2), bufB[:, j].rearrange("p (a h) n -> p a h n", a=2),
                               tab_cos[:, l, t].unsqueeze(2).to_broadcast([P, 2, HEADS, DIM_HEAD]), ALU.mult
                               ).then_inc(g["u_ready"], 1)
                    for s in slots:
                        for t in tiles:
                            j, k = 2 * s + t, 4 * l + 2 * s + t
                            dve.wait_ge(g["sim_done"], count(i, 8, k))
                            sim = ps[s][:, 2 * t:2 * t + 2, :].rearrange("p a (h n) -> p (a h) n", n=P)
                            link(nc.vector.tensor_reduce(ssq[:, j, 8:16], sim, AX_X, ALU.max))
                            vt(bufA[:, j].rearrange("p a b -> p (a b)").rearrange("p (h n) -> p h n", h=HEADS), sim,
                               ssq[:, j, 8:16].unsqueeze(2).to_broadcast([P, HEADS, P]), ALU.subtract).then_inc(g["d_ready"], 1)
                    for s in slots:
                        for t in tiles:
                            j, k = 2 * s + t, 4 * l + 2 * s + t
                            dve.wait_ge(g["p_ready"], count(i, 8, k))
                            link(nc.vector.tensor_reduce(ssq[:, j, 0:8], bufB[:, j].rearrange("p a b -> p (a b)").rearrange(
                                "p (h n) -> p h n", h=HEADS), AX_X, ALU.add))
                            after_wait(nc.vector.reciprocal, ssq[:, j, 0:8], ssq[:, j, 0:8]).then_inc(g["rl_ready"], 1)
                    for s in slots:
                        k = 2 * l + s
                        dve.wait_ge(g["x1T_done"], count(i, 4, k))
                        pr = ps[s][:, 1, 0:S]
                        vt(x1T[:, s], pr, xT[:, s], ALU.add)
                        vt(hT[0:64, s, 0:S], pr[0:64], xT[0:64, s], ALU.add)
                        vt(hT[64:128, s, 1:S + 1], pr[64:128], xT[64:128, s], ALU.add).then_inc(g["h2_ready"], 1)
                    for s in slots:
                        dve.wait_ge(g["h2tok_done"], count(i, 4, 2 * l + s))
                        moments(s, lambda t: ps[s][:, 0, tok(t)])
                    for s in slots:
                        normalise(s, 2 + 2 * l + s, lambda t: ps[s][:, 0, tok(t)], g["hn_ready"])
                    for s in slots:
                        dve.wait_ge(g["w1_done"], count(i, 4, 2 * l + s))
                        dve.wait_ge(g["gelu_ready"], count(i, 4, 2 * l + s))
                        for c, (o, n) in enumerate(CH):
                            src = ps[s][0:n, 0, c * S:(c + 1) * S] if c < 2 else ps[s][0:n, 1, 0:S]
                            last = nc.vector.scalar_tensor_tensor(ge[0:n, s, c], src, b1a[0:n, l, c:c + 1], ge[0:n, s, c],
                                                                  ALU.add, ALU.mult)
                        last.then_inc(g["u2_ready"], 1)
                    for s in slots:
                        dve.wait_ge(g["x2T_done"], count(i, 4, 2 * l + s))
                        pr = ps[s][:, 1, 0:S]
                        last = nc.vector.scalar_tensor_tensor(xT[:, s], pr, b2[:, l:l + 1], x1T[:, s], ALU.add, ALU.add)
                        if l == 0:
                            nc.vector.scalar_tensor_tensor(hT[0:64, s, 0:S], pr[0:64], b2[0:64, l:l + 1], x1T[0:64, s],
                                                           ALU.add, ALU.add)
                            nc.vector.scalar_tensor_tensor(hT[64:128, s, 1:S + 1], pr[64:128], b2[64:128, l:l + 1],
                                                           x1T[64:128, s], ALU.add, ALU.add).then_inc(g["h1_ready"], 1)
                        else:
                            last.then_inc(g["x2T_ready"], 1)
                for s in slots:
                    dve.wait_ge(g["x2_done"], count(i, 2, s))
                    link(vt(res[:, 2 * s:2 * s + 2], ps[s][:, 0, 0:S].rearrange("p (t n) -> p t n", t=2),
                            res[:, 2 * s:2 * s + 2], ALU.add))
                    moments(s, lambda t: res[:, 2 * s + t])
                for s in slots:
                    normalise(s, 6 + s, lambda t: res[:, 2 * s + t], g["y_ready"])
                    dve.wait_ge(g["y_ready"], count(i, 2, s))
                    vt(res[:, 2 * s:2 * s + 2], res[:, 2 * s:2 * s + 2], a_bo[:].unsqueeze(1).to_broadcast([P, 2, P]), ALU.add)
                for s in slots:
                    js = slice(2 * s, 2 * s + 2)
                    dve.wait_ge(g["proj_done"], count(i, 2, s))
                    vt(a_v[:, s], ps[s][:, 1, 0:S].rearrange("p (t n) -> p t n", t=2),
                       a_bv[:].unsqueeze(1).to_broadcast([P, 2, P]), ALU.add)
                    link(nc.vector.tensor_copy(g_l[:, js], ps[s][:, 3, 0:2 * EXPERTS].rearrange("p (t e) -> p t e", t=2)))
                    for t in tiles:
                        last = after_wait(nc.vector.max, g_m[:, 2 * s + t], g_l[:, 2 * s + t])
                    link(last)
                    for t in tiles:
                        last = after_wait(nc.vector.max_index, g_i[:, 2 * s + t], g_m[:, 2 * s + t], g_l[:, 2 * s + t])
                    link(last)
                    nc.vector.tensor_copy(g_f[:, js], g_i[:, js])
                    vt(g_l[:, js], g_l[:, js], g_m[:, js, 0:1].to_broadcast([P, 2, EXPERTS]), ALU.subtract
                       ).then_inc(g["logit_ready"], 1)
                    dve.wait_ge(g["qk1_ready"], count(i, 2, s))
                    link(nc.vector.tensor_reduce(kcs[:, s], a_kT[:, s, 0:S].rearrange("p (c n) -> p c n", n=COMP), AX_X, ALU.add))
                    nc.vector.tensor_scalar_mul(a_kT[:, s, S:S + SC], kcs[:, s], 1.0 / COMP).then_inc(g["kc_ready"], 1)
                for s in slots:
                    js = slice(2 * s, 2 * s + 2)
                    dve.wait_ge(g["e_ready"], count(i, 2, s))
                    io = iota8[:].unsqueeze(1).to_broadcast([P, 2, EXPERTS])
                    vt(comb[:, js], io, g_f[:, js, 0:1].to_broadcast([P, 2, EXPERTS]), ALU.is_equal)
                    link(vt(g_m[:, js], io, g_f[:, js, 1:2].to_broadcast([P, 2, EXPERTS]), ALU.is_equal))
                    link(vt(comb[:, js], comb[:, js], g_m[:, js], ALU.add))
                    link(vt(comb[:, js], comb[:, js], g_e[:, js], ALU.mult))
                    link(nc.vector.tensor_reduce(g_s[:, js], comb[:, js], AX_X, ALU.add))
                    link(after_wait(nc.vector.reciprocal, g_s[:, js], g_s[:, js]))
                    vt(comb[:, js], comb[:, js], g_s[:, js].unsqueeze(2).to_broadcast([P, 2, EXPERTS]), ALU.mult
                       ).then_inc(g["comb_ready"], 1)
                dve.wait_ge(g["b2_done"], count(i, 1, 0))
                dve.wait_ge(stored, 16 * i)
                vt(y_out[:], ps[1][:, 3, :].rearrange("p (j n) -> p j n", n=P), res[:], ALU.add).then_inc(g["acc0_ready"], 1)

                def expert(e):
                    dve.wait_ge(g["eo_done"], count(i, EXPERTS, e))
                    if e == 0:
                        dve.wait_ge(g["acc0_ready"], count(i, 1, 0))
                    else:
                        dve.wait_ge(g["acc_done"], count(i, EXPERTS, e - 1))
                    for j in range(NT):
                        last = nc.vector.scalar_tensor_tensor(y_out[:, j], ps[1][:, 3, tok(j)], comb[:, j, e:e + 1], y_out[:, j],
                                                              ALU.mult, ALU.add)
                    last.then_inc(g["acc_done"], 1)

                def rounds(j, a, b):
                    for r in range(a, b):
                        src = raw[j][:, 0:S] if r == 0 else wrk[j][:, 0:S]
                        link(after_wait(nc.vector.max, top8[:, j], src))
                        if r == 0:
                            nc.vector.tensor_scalar(nmax[:, j, 0:1], top8[:, j, 0:1], 0.0, -1.0, ALU.max, ALU.mult)
                        last = after_wait(nc.vector.match_replace, wrk[j][:, 0:S], top8[:, j], src, -BIG)
                        if r < TOP_K // 8 - 1:
                            link(last)
                    if b == TOP_K // 8:
                        last.then_inc(g["top_ready"], 1)

                def combine(j):
                    n = P * (j % 2 + 1)
                    sel = bufD[:, j].rearrange("p a b -> p (a b)")
                    dve.wait_ge(g["ex_ready"], count(i, NT, j))
                    link(after_wait(nc.vector.reciprocal, lsum[:, j], lsum[:, j]))
                    link(vt(lsum[:, j], lsum[:, j], third[:], ALU.mult))
                    link(nc.vector.tensor_scalar(wrk[j][:, 0:S], sel[:, 256:512], lsum[:, j, 0:1], None, ALU.mult))
                    link(nc.vector.scalar_tensor_tensor(wrk[j][:, 0:n], sel[:, 512:512 + n], lsum[:, j, 1:2], wrk[j][:, 0:n],
                                                        ALU.mult, ALU.add))
                    w4 = wrk[j][:, 0:S].rearrange("p (c n) -> p c n", n=COMP)
                    nc.vector.scalar_tensor_tensor(w4, sel[:, 768:768 + SC].unsqueeze(2).to_broadcast([P, SC, COMP]),
                                                   lsum[:, j, 2:3], w4, ALU.mult, ALU.add).then_inc(g["pw_ready"], 1)

                for j in range(NT):
                    dve.wait_ge(g["raw_ready"], count(i, NT, j))
                    rounds(j, 0, 4)
                    expert(2 * j)
                    rounds(j, 4, 8)
                    dve.wait_ge(g["cm_ready"], count(i, NT, j))
                    nc.vector.tensor_reduce(nmax[:, j, 1:2], wrk[j][:, 512:512 + P * (j % 2 + 1)], AX_X, ALU.max, negate=True)
                    nc.vector.tensor_reduce(nmax[:, j, 2:3], raw[j][:, S:S + SC], AX_X, ALU.max, negate=True
                                            ).then_inc(g["cmax_ready"], 1)
                    expert(2 * j + 1)
                    if j >= 2:
                        combine(j - 2)
                combine(2)
                combine(3)
                dve.wait_ge(g["acc_done"], count(i, EXPERTS, EXPERTS - 1))
                for s in slots:
                    js = slice(2 * s, 2 * s + 2)
                    dve.wait_ge(g["wo_done"], count(i, 2, s))
                    last = vt(y_out[:, js], ps[s][:, 1, 0:S].rearrange("p (t n) -> p t n", t=2), y_out[:, js], ALU.add)
                last.then_inc(g["out_ready"], 1)
                assert n_link <= DVE_LINKS
                if n_link < DVE_LINKS:
                    dve.sem_inc(dlink, DVE_LINKS - n_link)

        @block.tensor
        def _(pe):
            def mm(out, a, b, start=True, stop=True):
                return nc.tensor.matmul(out, a, b, start=start, stop=stop)

            pe.wait_ge(prep_a, 3)
            with pe.Fori(1, PAIRS + 1) as i:
                for s in slots:
                    pe.wait_ge(g["xn_ready"], count(i, 2, s))
                    for t in tiles:
                        last = nc.tensor.transpose(ps[s][:, 0, tok(t)], xn[:, 2 * s + t], ident[:])
                    last.then_inc(g["xnT_done"], 1)
                for s in slots:
                    pe.wait_ge(g["h0_ready"], count(i, 2, s))
                    for t in tiles:
                        last = mm(ps[s][:, 1, tok(t)], xT[:, s, tok(t)], fw_q[:])
                    last.then_inc(g["q0_done"], 1)
                for s in slots:
                    pe.wait_ge(g["qn0_ready"], count(i, 2, s))
                    for t in tiles:
                        last = nc.tensor.transpose(ps[s][:, 0, tok(t)], q0s[:, 2 * s + t], ident[:])
                    last.then_inc(g["qT0_done"], 1)
                for s in slots:
                    pe.wait_ge(g["qT0_ready"], count(i, 2, s))
                    for p in range(2):
                        r = slice(64 * p, 64 * p + 64)
                        mm(ps[s][:, 1 + p, 0:S], fw_gate[r, :], q0T[r, s, :])
                        last = mm(ps[s][:, 1 + p, S:2 * S], fw_up[r, :], q0T[r, s, :])
                    last.then_inc(g["gu_done"], 1)
                for s in slots:
                    pe.wait_ge(g["hid_ready"], count(i, 2, s))
                    for t in tiles:
                        for p in range(2):
                            last = mm(ps[s][:, 3, P * t + 64 * p:P * t + 64 * p + 64], th[:, s, p, tok(t)], fw_down[:, p, :])
                    last.then_inc(g["o0_done"], 1)

                for l in range(DEPTH):
                    for s in slots:
                        if l == 0:
                            pe.wait_ge(x_used, count(i, 2, s))
                        else:
                            pe.wait_ge(g["h1_ready"], count(i, 2, s))
                        for t in tiles:
                            mm(ps[s][:, 2 * t, :], hT[:, s, tok(t)], wqkv[:, l, 0:INNER])
                            mm(ps[s][:, 2 * t + 1, :], hT[:, s, tok(t)], wqkv[:, l, INNER:2 * INNER]).then_inc(g["qk_done"], 1)
                    for s in slots:
                        for t in tiles:
                            j = 2 * s + t
                            pe.wait_ge(g["s_ready"], count(i, 8, 4 * l + j))
                            for a in range(8):
                                last = nc.tensor.transpose(ps[s][:, 2 * t + a // 4, P * (a % 4):P * (a % 4) + P],
                                                           bufC[:, j].rearrange("p a b -> p (a b)")[:, a * P:(a + 1) * P], ident[:])
                            last.then_inc(g["qkT_done"], 1)
                    for s in slots:
                        pe.wait_ge(g["qkT_ready"], count(i, 8, 4 * l + 2 * s + 1))
                        for t in tiles:
                            last = mm(ps[s][:, 2 + t, :], hT[:, s, tok(t)], wqkv[:, l, 2 * INNER:3 * INNER])
                        last.then_inc(g["v_done"], 1)
                        for h in range(2):
                            mm(ps[s][:, h, :], identb[:], bandb[:, 0, :].unsqueeze(1).to_broadcast([P, 4, P]), stop=False)
                            r = slice(64 * h, 64 * h + 64)
                            for a in range(4):
                                last = mm(ps[s][:, h, a * P:(a + 1) * P], qkT[r, s, a, 0:P], qkT[r, s, 4 + a, 0:P], start=False, stop=(a == 3))
                        last.then_inc(g["sim_done"], 1)
                        pe.wait_ge(g["v_ready"], count(i, 4, 2 * l + s))
                        for h in range(2):
                            mm(ps[s][:, 2 + h, :], identb[:], bandb[:, 1, :].unsqueeze(1).to_broadcast([P, 4, P]), stop=False)
                            r = slice(64 * h, 64 * h + 64)
                            for a in range(4):
                                c = a * P
                                mm(ps[s][:, 2 + h, c:c + 64], qkT[r, s, a, P:2 * P], qkT[r, s, 4 + a, P:P + 64], start=False, stop=False)
                                mm(ps[s][0:64, 2 + h, c + 64:c + P], qkT[r, s, a, P:P + 64], qkT[r, s, 4 + a, 64:P], start=False, stop=(a == 3))
                                last = mm(ps[s][64:128, 2 + h, c + 64:c + P], qkT[r, s, a, P + 64:2 * P],
                                          qkT[r, s, 4 + a, P + 64:2 * P], start=False, stop=(a == 3))
                        last.then_inc(g["sim_done"], 1)
                    for s in slots:
                        for t in tiles:
                            j = 2 * s + t
                            pe.wait_ge(g["pn_ready"], count(i, 8, 4 * l + j))
                            for a in range(8):
                                last = nc.tensor.transpose(ps[s][:, 2 * t + a // 4, P * (a % 4):P * (a % 4) + P],
                                                           bufB[:, j].rearrange("p a b -> p (a b)")[:, a * P:(a + 1) * P], ident[:])
                            last.then_inc(g["pT_done"], 1)
                    for s in slots:
                        for t in tiles:
                            j = 2 * s + t
                            pe.wait_ge(g["pT_ready"], count(i, 8, 4 * l + j))
                            pT = bufC[:, j].rearrange("p a b -> p (a b)").rearrange("p (h n) -> p h n", n=P)
                            for a in range(4):
                                for h in range(2):
                                    o = ps[s][64 * h:64 * h + 64, 2 * t, a * P:(a + 1) * P]
                                    hd = slice(64 * (2 * a + h), 64 * (2 * a + h) + 64)
                                    if t == 0:
                                        last = mm(o, v[:, s, 0, hd], pT[:, 4 * h + a, :])
                                    else:
                                        mm(o[:, 0:64], v[:, s, 2, hd], pT[:, 4 * h + a, 0:64])
                                        last = mm(o[:, 64:128], v[:, s, 1, hd], pT[:, 4 * h + a, 64:128])
                            last.then_inc(g["oT_done"], 1)
                    for s in slots:
                        pe.wait_ge(g["oT_ready"], count(i, 8, 4 * l + 2 * s + 1))
                        for a in range(4):
                            last = mm(ps[s][:, 1, 0:S], wo[:, l, a, :], oT[:, s, a, :], start=(a == 0), stop=(a == 3))
                        last.then_inc(g["x1T_done"], 1)
                    for s in slots:
                        pe.wait_ge(g["h2_ready"], count(i, 4, 2 * l + s))
                        for t in tiles:
                            last = nc.tensor.transpose(ps[s][:, 0, tok(t)], hT[:, s, tok(t)], ident[:])
                        last.then_inc(g["h2tok_done"], 1)
                    for s in slots:
                        pe.wait_ge(g["hn_ready"], count(i, 4, 2 * l + s))
                        for t in tiles:
                            last = nc.tensor.transpose(ps[s][:, 2, tok(t)], xn[:, 2 * s + t], ident[:])
                        last.then_inc(g["hnT_done"], 1)
                    for s in slots:
                        pe.wait_ge(g["hnT_ready"], count(i, 4, 2 * l + s))
                        for half, banks in ((1, (3, 3, 2)), (0, (0, 0, 1))):
                            for c, (o, n) in enumerate(CH):
                                at = (c % 2) * S
                                last = mm(ps[s][0:n, banks[c], at:at + S], w1[:, l, half * HID + o:half * HID + o + n], hnT[:, s, :])
                        last.then_inc(g["w1_done"], 1)
                    for s in slots:
                        pe.wait_ge(g["u2_ready"], count(i, 4, 2 * l + s))
                        for c, (o, n) in enumerate(CH):
                            last = mm(ps[s][:, 1, 0:S], w2[0:n, l, c, :], ge[0:n, s, c, :], start=(c == 0), stop=(c == len(CH) - 1))
                        last.then_inc(g["x2T_done"], 1)
                for s in slots:
                    pe.wait_ge(g["x2T_ready"], count(i, 2, s))
                    for t in tiles:
                        last = nc.tensor.transpose(ps[s][:, 0, tok(t)], xT[:, s, tok(t)], ident[:])
                    last.then_inc(g["x2_done"], 1)

                for s in slots:
                    pe.wait_ge(g["y_ready"], count(i, 2, s))
                    for t in tiles:
                        last = nc.tensor.transpose(ps[s][:, 2, tok(t)], xn[:, 2 * s + t], ident[:])
                    last.then_inc(g["yTp_done"], 1)
                for s in slots:
                    pe.wait_ge(g["yT_ready"], count(i, 2, s))
                    mm(ps[s][:, 0, 0:S], a_wq[:], yT[:, s, :])
                    mm(ps[s][:, 0, S:2 * S], a_wk[:], yT[:, s, :])
                    for t in tiles:
                        mm(ps[s][:, 1, tok(t)], yT[:, s, tok(t)], a_wv[:])
                    for t in tiles:
                        last = mm(ps[s][:, 3, EXPERTS * t:EXPERTS * (t + 1)], yT[:, s, tok(t)], m_gate[:])
                    last.then_inc(g["proj_done"], 1)
                for s in slots:
                    pe.wait_ge(g["kc_ready"], count(i, 2, s))
                    for t in tiles:
                        mm(ps[s][:, t, 0:S + SC], a_qT[:, s, tok(t)], a_kT[:, s, 0:S + SC]).then_inc(g["sc_done"], 1)

                pe.wait_ge(g["comb_ready"], count(i, 2, 1))
                for j in range(NT):
                    last = nc.tensor.transpose(ps[1][0:EXPERTS, 3, tok(j)], comb[:, j, :], ident[:])
                last.then_inc(g["combT_done"], 1)
                pe.wait_ge(g["combT_ready"], count(i, 1, 0))
                for j in range(NT):
                    last = mm(ps[1][:, 3, tok(j)], combT[:, tok(j)], m_b2[:])
                last.then_inc(g["b2_done"], 1)

                def down(e):
                    pe.wait_ge(g["relu_done"], count(i, EXPERTS * EC, EC * e + EC - 1))
                    if e == 0:
                        pe.wait_ge(g["acc0_ready"], count(i, 1, 0))
                    else:
                        pe.wait_ge(g["acc_done"], count(i, EXPERTS, e - 1))
                    for j in range(NT):
                        for c in range(EC):
                            last = mm(ps[1][:, 3, tok(j)], hbuf[:, e % 2, c, tok(j)], m_w2[:, e, c, :], start=(c == 0), stop=(c == EC - 1))
                    last.then_inc(g["eo_done"], 1)

                for e in range(EXPERTS):
                    for c in range(EC):
                        k = EC * e + c
                        sl, bk = ((0, 2), (0, 3), (1, 2))[k % 3]
                        if k >= 3:
                            pe.wait_ge(g["relu_done"], count(i, EXPERTS * EC, k - 3))
                        mm(ps[sl][:, bk, :], m_w1[:, e, c * P:(c + 1) * P], yT[:].rearrange("p s n -> p (s n)")
                           ).then_inc(g["h_done"], 1)
                    if e >= 1:
                        down(e - 1)
                down(EXPERTS - 1)

                for s in slots:
                    for t in tiles:
                        j = 2 * s + t
                        pe.wait_ge(g["pw_ready"], count(i, NT, j))
                        for a in range(2):
                            last = nc.tensor.transpose(ps[s][:, t, a * P:(a + 1) * P], wrk[j][:, a * P:(a + 1) * P], ident[:])
                        last.then_inc(g["pwT_done"], 1)
                    pe.wait_ge(g["pwT_ready"], count(i, NT, 2 * s + 1))
                    for a in range(2):
                        last = mm(ps[s][:, 0, 0:S], a_v[:, s, a, :], a_pT[:, s, a, :], start=(a == 0), stop=(a == 1))
                    last.then_inc(g["at_done"], 1)
                    pe.wait_ge(g["at_ready"], count(i, 2, s))
                    for t in tiles:
                        last = mm(ps[s][:, 1, tok(t)], a_oT[:, s, tok(t)], a_wo[:])
                    last.then_inc(g["wo_done"], 1)


def shape_constants():
    import numpy as np
    f = np.float32
    half = np.arange(0, DIM_HEAD, 2, dtype=f)
    inv = (f(1.0) / f(10000.0) ** (half / f(DIM_HEAD))).astype(f)
    t = np.arange(S, dtype=f)
    fr = (t[:, None] * inv[None, :]).astype(f)
    fr = np.concatenate([fr, fr], -1)
    base = ((half + f(0.4 * DIM_HEAD)) / f(1.4 * DIM_HEAD)).astype(f)
    power = ((t - S // 2) / f(WINDOW // 2)).astype(f)
    sc = (base[None, :] ** power[:, None]).astype(f)
    sc = np.concatenate([sc, sc], -1)
    cos, sin = np.cos(fr).astype(f), np.sin(fr).astype(f)
    sgn = np.concatenate([-np.ones(DIM_HEAD // 2, f), np.ones(DIM_HEAD // 2, f)])
    rot_cos = np.stack([cos * sc, cos / sc], 1).astype(f)
    rot_sin = np.stack([sin * sc * sgn, sin / sc * sgn], 1).astype(f)
    q, c = np.arange(P)[:, None], np.arange(P)[None, :]
    ok0 = (c <= q) & (c >= q - WINDOW)
    qi, ci = q % WINDOW, c % WINDOW
    own = (q // WINDOW == 0) == (c // WINDOW == 0)
    ok1 = np.where(own, ci <= qi, ci >= qi)
    band = np.where(np.stack([ok0, ok1]), f(0), f(-1e30)).astype(f)
    causal = np.where(c <= q, f(0), f(-BIG)).astype(f)
    return {"ident": np.eye(P, dtype=f), "band": band, "causal": causal, "rot_cos": rot_cos, "rot_sin": rot_sin,
            "iota8": np.arange(EXPERTS, dtype=f)}


def kernel(**inputs):
    import numpy as np
    import concourse.bacc as bacc
    from concourse import mybir
    from concourse.bass_utils import run_bass_kernel_spmd as run

    a = {k: np.asarray(v) for k, v in inputs.items()}
    w = shape_constants()
    w["fw_q"] = a["L0_attn_qkv_w"][0:D].T
    w["q_norm_w"] = a["L0_attn_q_norm_w"]
    for n in ("w0", "w1", "w2"):
        w["fw_" + n] = a["L0_attn_" + n].transpose(0, 2, 1)
    for n in ("wqkv", "q_scale", "k_scale", "wo", "w1", "w2"):
        w[n] = a["L0_ffn_" + n]
    for n in ("Wq", "Wk", "Wv", "Wo", "bv", "bo"):
        w["a_" + n.lower()] = a["L1_attn_" + n]
    w["m_gate"] = a["L1_ffn_gate_w"].T
    w["m_w1"] = a["L1_ffn_w1"].transpose(2, 0, 1)
    w["m_w2"] = a["L1_ffn_w2"].reshape(EXPERTS, D, EC, P).transpose(3, 0, 2, 1)
    b1, columns = a["L0_ffn_b1"], np.zeros((P, 52), np.float32)
    for l in range(DEPTH):
        for c, (o, n) in enumerate(CH):
            columns[0:n, 3 * l + c] = b1[l, o:o + n]
            columns[0:n, 6 + 3 * l + c] = b1[l, HID + o:HID + o + n]
        columns[:, 12 + l], columns[:, 14 + l], columns[:, 16 + l] = (
            a["L0_ffn_b2"][l], a["L0_ffn_ln_g"][l], a["L0_ffn_ln_b"][l])
    columns[:, 18], columns[:, 19] = a["L1_attn_bq"], a["L1_attn_bk"]
    columns[:, 20:52] = a["L1_ffn_b1"].reshape(EXPERTS * EC, P).T
    w["cols"] = columns
    w["m_b2"] = a["L1_ffn_b2"]
    x = np.ascontiguousarray(a["L0_attn_hidden_states"])

    nc = bacc.Bacc("TRN2", target_bir_lowering=False, num_devices=1)
    arrays, aps = {"x": x}, {}
    for name, value in w.items():
        arrays["in_" + name] = np.ascontiguousarray(value)
        aps[name] = nc.dram_tensor("in_" + name, value.shape, mybir.dt.from_np(value.dtype), kind="ExternalInput").ap()
    x_d = nc.dram_tensor("x", x.shape, mybir.dt.float32, kind="ExternalInput").ap()
    out_d = nc.dram_tensor("out", x.shape, mybir.dt.float32, kind="ExternalOutput").ap()
    build(nc, x_d, out_d, aps)
    r = run(nc, [arrays], core_ids=[0])
    return r.results[0]["out"]
```

```python
import math
from contextlib import ExitStack

import concourse.bass as bass
from concourse import mybir

F32 = mybir.dt.float32
BF16 = mybir.dt.bfloat16
U32 = mybir.dt.uint32
ALU = mybir.AluOpType
ACT = mybir.ActivationFunctionType
AX_X = mybir.AxisListType.X

P = 128
B, S, D = 16, 256, 128
TILES = S // P
SLOTS = 2
PAIRS = B // SLOTS
NT = SLOTS * TILES
NH, DH, DHID = 4, 32, 64
DEPTH, HEADS, DIM_HEAD, WINDOW = 2, 8, 64, 64
INNER = HEADS * DIM_HEAD
HID = int(D * 4 * 2 / 3)
CH = [(c * P, min(P, HID - c * P)) for c in range((HID + P - 1) // P)]
EXPERTS, HIDDEN = 8, 512
EC = HIDDEN // P
COMP, TOP_K = 4, 64
SC = S // COMP
BIG = 3.0e38
DVE_LINKS = (98, 92)
POOL_LINKS = (4, 8)
ACT_LINKS = 18

HEAD_STEPS, LAYER_STEPS = 7, 14
BLOCK = [HEAD_STEPS + LAYER_STEPS * l for l in range(DEPTH)]
STEPS = HEAD_STEPS + LAYER_STEPS * DEPTH + 1
TURN_Y, PROJECT, SCORES, TURN_COMB, EXPERT_BIAS = 1, 2, 3, 5, 6


class Plan:

    def __init__(self, up, down, top, attend, steps):
        self.up, self.down = up, down
        self.add = down
        self.top = top
        self.top_done = top[3::4]
        self.softmax = [k + 1 for k in self.top_done]
        self.combine = [k + 2 for k in self.top_done]
        self.p_turn = [k + 3 for k in self.top_done]
        self.attend = attend
        self.add_attention = [k + 1 for k in attend]
        self.steps = steps


L, M = BLOCK
WOVEN = Plan(up=[4, L, L + 4, L + 7, L + 11, M, M + 4, M + 11],
             down=[6, L + 2, L + 5, L + 10, L + 13, M + 2, M + 10, STEPS - 1],
             top=[4, 5, L + 3, L + 4, L + 6, L + 7, L + 8, L + 9, L + 12, L + 13, M + 3, M + 4, M + 6, M + 7, M + 8, M + 9],
             attend=[L + 13, M + 13], steps=STEPS)
ALONE = Plan(up=[4 + 3 * e for e in range(EXPERTS)], down=[6 + 3 * e for e in range(EXPERTS)], top=list(range(4, 20)),
             attend=[15, 26], steps=28)
LN_EXP = "natural_log_exp_and_others"
LN_SCALE = 2.0 ** 16


def count(i, per_pair, k):
    return (i - 1) * per_pair + k + 1


def build(nc, x_d, out_d, w):
    ctx = ExitStack()
    with ctx:
        def sb(name, shape, dt=F32):
            return ctx.enter_context(nc.sbuf_tensor(name, shape, dt))

        def sem(name):
            return ctx.enter_context(nc.semaphore(name))

        ident = sb("ident", [P, P])
        identb = sb("identb", [P, P], BF16)
        bandb = sb("bandb", [P, TILES, P], BF16)
        causal = sb("causal", [P, P])
        tab_cos = sb("tab_cos", [P, DEPTH, TILES, 2, DIM_HEAD])
        tab_sin = sb("tab_sin", [P, DEPTH, TILES, 2, DIM_HEAD])
        iota8 = sb("iota8", [P, EXPERTS])
        third = sb("third", [P, 3])
        fw_q = sb("fw_q", [P, P])
        fw_gate = sb("fw_gate", [P, P])
        fw_up = sb("fw_up", [P, P])
        fw_down = sb("fw_down", [P, 2, 2 * DH])
        q_norm = sb("q_norm", [P, P])
        wqkv = sb("wqkv", [P, DEPTH, 3 * INNER])
        wo = sb("wo", [P, DEPTH, INNER // P, P])
        w1 = sb("w1", [P, DEPTH, 2 * HID])
        w2 = sb("w2", [P, DEPTH, len(CH), P])
        a_wq = sb("a_wq", [P, P])
        a_wk = sb("a_wk", [P, P])
        a_wv = sb("a_wv", [P, P])
        a_wo = sb("a_wo", [P, P])
        a_bqs = sb("a_bqs", [P, 1])
        a_bv = sb("a_bv", [P, P])
        a_bo = sb("a_bo", [P, P])
        m_gate = sb("m_gate", [P, EXPERTS])
        m_w1 = sb("m_w1", [P, EXPERTS, HIDDEN])
        m_w2 = sb("m_w2", [P, EXPERTS, EC, P])
        m_b2 = sb("m_b2", [EXPERTS, P])
        cols = sb("cols", [P, 2 * DEPTH * len(CH) + 3 * DEPTH + 2 + EXPERTS * EC])
        b1a = cols[:, 0:6].rearrange("p (l c) -> p l c", l=DEPTH)
        b1g = cols[:, 6:12].rearrange("p (l c) -> p l c", l=DEPTH)
        b2, ln_g, ln_b = cols[:, 12:14], cols[:, 14:16], cols[:, 16:18]
        a_bq, a_bk = cols[:, 18:19], cols[:, 19:20]
        m_b1 = cols[:, 20:52].rearrange("p (e c) -> p e c", e=EXPERTS)

        x0 = sb("x0", [P, NT, P])
        stats = sb("stats", [P, NT, 6])
        meanvar = sb("meanvar", [P, NT, 2])
        rstd = sb("rstd", [P, NT])
        vareps = sb("vareps", [P, NT])
        newt = sb("newt", [P, NT, 16])
        ln_root = sb("ln_root", [P, 1])
        fw_n = sb("fw_n", [P, SLOTS, TILES + TILES * NH])
        fw_r = sb("fw_r", [P, SLOTS, TILES + TILES * NH])
        qk_n = sb("qk_n", [P, NT, 16])
        xn = sb("xn", [P, NT, P])
        xT = sb("xT", [P, SLOTS, S])
        x1T = sb("x1T", [P, SLOTS, S])
        hT = sb("hT", [P, SLOTS, S + 1])
        res = sb("res", [P, NT, P])
        ms0 = sb("ms0", [P, NT])
        hs0 = sb("hs0", [P, NT, NH])
        hr0 = sb("hr0", [P, NT, NH])
        bufA = sb("bufA", [P, NT, 16, DIM_HEAD])
        bufB = sb("bufB", [P, NT, 16, DIM_HEAD])
        bufC = sb("bufC", [P, NT, 16, DIM_HEAD])
        ssq = sb("ssq", [P, NT, 16])
        qkT = sb("qkT", [P, SLOTS, 8, S])
        v = sb("v", [P, SLOTS, TILES, INNER])
        hnT = sb("hnT", [P, SLOTS, S])
        ge = sb("ge", [P, SLOTS, len(CH), S])

        fw = bufC[:].rearrange("p n a b -> p (n a b)")
        q0 = fw[:, 0:NT * P].rearrange("p (n d) -> p n d", n=NT)
        q0s = fw[:, NT * P:2 * NT * P].rearrange("p (n d) -> p n d", n=NT)
        q0T = fw[:, 2 * NT * P:3 * NT * P].rearrange("p (s n) -> p s n", s=SLOTS)
        th = fw[:, 3 * NT * P:5 * NT * P].rearrange("p (s a n) -> p s a n", s=SLOTS, a=2)
        tmp = bufB[:].rearrange("p n a b -> p (n a b)")
        band = tmp[:, 0:256].rearrange("p (t n) -> p t n", t=TILES)
        rot_cos = tmp[:, 256:512].rearrange("p (t a n) -> p t a n", t=TILES, a=2)
        rot_sin = tmp[:, 512:768].rearrange("p (t a n) -> p t a n", t=TILES, a=2)
        qk_scale = tmp[:, 768:1024].rearrange("p (l a n) -> p l a n", l=DEPTH, a=2)
        oT = bufA[:].rearrange("p (s t) a b -> p s (t a b)", s=SLOTS)[:, :, 0:4 * S].rearrange("p s (k n) -> p s k n", k=4)
        vmix = ge[:].rearrange("p s c n -> p s (c n)")[:, :, 0:INNER]

        x1 = sb("x1", [P, NT, P])
        yn = sb("yn", [P, NT, P])
        y_out = sb("y_out", [P, NT, P])
        yT = sb("yT", [P, SLOTS, S])
        g_l = sb("g_l", [P, NT, EXPERTS])
        g_m = sb("g_m", [P, NT, EXPERTS])
        g_i = sb("g_i", [P, NT, EXPERTS], U32)
        g_f = sb("g_f", [P, NT, EXPERTS])
        g_e = sb("g_e", [P, NT, EXPERTS])
        g_s = sb("g_s", [P, NT])
        comb = sb("comb", [P, NT, EXPERTS])
        combT = sb("combT", [EXPERTS, NT * P])
        top8 = sb("top8", [P, NT, 8])
        nmax = sb("nmax", [P, NT, 3])
        lsum = sb("lsum", [P, NT, 3])
        kcs = sb("kcs", [P, SLOTS, SC])
        raw = sb("raw", [P, NT, S + SC])
        wrk = sb("wrk", [P, NT, S])
        csc = sb("csc", [P, NT, S])
        a_qT = sb("a_qT", [P, SLOTS, S])
        a_kT = sb("a_kT", [P, SLOTS, S + SC])
        a_v = sb("a_v", [P, SLOTS, TILES, P])
        a_pT = sb("a_pT", [P, SLOTS, TILES, S])
        a_oT = sb("a_oT", [P, SLOTS, S])
        hbuf = sb("hbuf", [P, EC, NT * P])

        ps0 = ctx.enter_context(nc.psum_tensor("ps0", [P, 4, 512], F32))
        ps1 = ctx.enter_context(nc.psum_tensor("ps1", [P, 4, 512], F32))
        MOE_OUT, MISC = 2, 3

        loaded = [sem("tables_loaded"), sem("first_loaded"), sem("second_loaded")]
        x_loaded = sem("x_loaded")
        x_used = sem("x_used")
        stored = sem("stored")
        consts = sem("consts_ready")
        prep_a = sem("dve_prep")
        dlink = [sem("dve_link_first"), sem("dve_link_second")]
        plink = [sem("pool_link_first"), sem("pool_link_second")]
        alink = sem("act_link")
        start_link = sem("dve_link_start")
        act_start_link = sem("act_link_start")
        names = """xn_ready xnT_done h0_ready q0_done q0_sq qn0_ready qT0_done qT0_ready gu_done th_ready hid_ready o0_done
        qk_done qk_sq qn_ready u_ready r_ready s_ready s1_ready vmix_ready qkT_done qkT_ready v_done v_ready sim_done max_ready p_ready rl_ready pn_ready pn1_ready x1b_ready
        pT_done pT_ready oT_done oT_ready x1T_done h2_ready h2tok_done hn_ready hnT_done hnT_ready gate_done w1_done gelu_ready
        u2_ready x2T_done h1_ready x2T_ready x2_done x1_ready y_ready yTp_done yT_ready proj_done qk1_ready kc_ready logit_ready
        e_ready comb_ready combT_done combT_ready b2_done acc0_ready sc_done raw_ready top_ready cm_ready cmax_ready
        sp_ready ex_ready pw_ready pwT_done pwT_ready at_done at_ready wo_done out_ready h_done relu_done eo_done
        acc_done half_ready var_ready rstd_ready fwn_ready fwr_ready qkn_ready qkr_ready""".split()
        g = {n: sem(n) for n in names}

        block = ctx.enter_context(nc.Block())
        n_load = [0, 0, 0]

        @block.sync
        def _(sp):
            def load(dst, src, part=0):
                n_load[part] += 1
                sp.dma_start(dst, src).then_inc(loaded[part], 16)

            xv = x_d.rearrange("b (t p) d -> p (b t) d", p=P)
            ov = out_d.rearrange("b (t p) d -> p (b t) d", p=P)
            sp.dma_start(x0[:], xv[:, 0:NT, :]).then_inc(x_loaded, 16)
            sp.wait_ge(consts, 1)
            load(ident[:], w["ident"])
            load(band, w["band"].rearrange("t p n -> p t n"))
            load(causal[:], w["causal"])
            load(rot_cos, w["rot_cos"].rearrange("(t p) a n -> p t a n", p=P))
            load(rot_sin, w["rot_sin"].rearrange("(t p) a n -> p t a n", p=P))
            load(qk_scale[:, :, 0, :], w["q_scale"].partition_broadcast(P))
            load(qk_scale[:, :, 1, :], w["k_scale"].partition_broadcast(P))
            load(iota8[:], w["iota8"].partition_broadcast(P))
            load(fw_q[:], w["fw_q"])
            load(q_norm[:], w["q_norm_w"].partition_broadcast(P))
            for h in range(NH):
                a, o = DH * h, DHID * (h % 2)
                load(fw_gate[a:a + DH, o:o + DHID], w["fw_w0"][h])
                load(fw_up[a:a + DH, o:o + DHID], w["fw_w2"][h])
                load(fw_down[o:o + DHID, h // 2, DH * (h % 2):DH * (h % 2 + 1)], w["fw_w1"][h])
            load(cols[:], w["cols"])
            for l in range(DEPTH):
                load(wqkv[:, l], w["wqkv"][l], 1)
            load(wo[:], w["wo"].rearrange("l (j p) n -> p l j n", p=P), 1)
            load(w1[:], w["w1"].rearrange("l p n -> p l n"), 1)
            for c, (o, n) in enumerate(CH):
                load(w2[0:n, :, c, :], w["w2"][:, o:o + n, :].rearrange("l p n -> p l n"), 1)
            for t, n in ((a_wq, "a_wq"), (a_wk, "a_wk"), (a_wv, "a_wv"), (a_wo, "a_wo"), (m_gate, "m_gate"),
                         (m_b2, "m_b2")):
                load(t[:], w[n], 2)
            load(a_bv[:], w["a_bv"].partition_broadcast(P), 2)
            load(a_bo[:], w["a_bo"].partition_broadcast(P), 2)
            load(m_w1[:], w["m_w1"], 2)
            load(m_w2[:], w["m_w2"], 2)
            sp.sem_inc(stored, 16)
            sp.wait_ge(x_used, count(1, SLOTS, SLOTS - 1))
            sp.dma_start(x0[:], xv[:, NT:2 * NT, :]).then_inc(x_loaded, 16)
            with sp.Fori(1, PAIRS - 1) as i:
                sp.wait_ge(x_used, count(i + 1, SLOTS, SLOTS - 1))
                sp.dma_start(x0[:], xv[:, bass.ds((i + 1) * NT, NT), :]).then_inc(x_loaded, 16)
                sp.wait_ge(g["out_ready"], count(i, 1, 0))
                sp.dma_start(ov[:, bass.ds((i - 1) * NT, NT), :], y_out[:]).then_inc(stored, 16)
            sp.wait_ge(x_used, count(PAIRS, SLOTS, SLOTS - 1))
            sp.dma_start(x0[:], xv[:, 0:NT, :]).then_inc(x_loaded, 16)
            for k in (PAIRS - 1, PAIRS):
                sp.wait_ge(g["out_ready"], k)
                sp.dma_start(ov[:, (k - 1) * NT:k * NT, :], y_out[:]).then_inc(stored, 16)
            sp.wait_ge(stored, 16 * (PAIRS + 1))

        slots = range(SLOTS)
        tiles = range(TILES)
        units = [(s, t) for s in slots for t in tiles]

        def tok(t):
            return slice(t * P, (t + 1) * P)

        weight_readers = (nc.tensor, nc.vector)

        def pipeline(eng, first, second):
            first(1, lambda k: None, None)
            if eng in weight_readers:
                eng.wait_ge(loaded[2], 16 * n_load[2])
            with eng.Fori(1, PAIRS) as i:
                first(i + 1, lambda k: second(i, k, i + 1), i)
            for k in range(ALONE.steps):
                second(PAIRS, k, None)

        @block.gpsimd
        def _(pool):
            def chain(part, per_pair):
                n = 0

                def link(i, ins):
                    nonlocal n
                    ins.then_inc(plink[part], 1)
                    pool.wait_ge(plink[part], count(i, per_pair, n % per_pair))
                    n += 1
                return link

            link0, link1 = chain(0, POOL_LINKS[0]), chain(1, POOL_LINKS[1])

            def first(i, side, before):
                for k in range(HEAD_STEPS):
                    side(k)
                for l in range(DEPTH):
                    step = BLOCK[l]
                    for j, (s, t) in enumerate(units):
                        pool.wait_ge(g["qn_ready"], count(i, 8, 4 * l + j))
                        for h in range(2):
                            src = bufB[:, j].rearrange("p (a h) n -> p a h n", a=2)[:, :, :, 32 * (1 - h):32 * (2 - h)]
                            dst = bufA[:, j].rearrange("p (a h) n -> p a h n", a=2)[:, :, :, 32 * h:32 * h + 32]
                            tab = tab_sin[:, l, t, :, 32 * h:32 * h + 32].unsqueeze(2).to_broadcast([P, 2, HEADS, 32])
                            last = nc.gpsimd.tensor_tensor(dst, src, tab, ALU.mult)
                        last.then_inc(g["r_ready"], 1)
                        if t == 0:
                            pool.wait_ge(g["r_ready"], count(i, 8, 4 * l + j))
                            pool.wait_ge(g["u_ready"], count(i, 8, 4 * l + j))
                            nc.gpsimd.tensor_tensor(bufC[:, j], bufC[:, j], bufA[:, j], ALU.add).then_inc(g["s_ready"], 1)
                    pool.wait_ge(g["r_ready"], count(i, 8, 4 * l + 3))
                    for s in slots:
                        pool.wait_ge(g["v_ready"], count(i, 8, 4 * l + 2 * s + 1))
                        pool.nop(nofuse=True)
                        link0(i, nc.gpsimd.tensor_copy(vmix[0:64, s, :], v[0:64, s, 1, :]))
                        pool.nop(nofuse=True)
                        nc.gpsimd.tensor_copy(vmix[64:128, s, :], v[64:128, s, 0, :]).then_inc(g["vmix_ready"], 1)
                        pool.wait_ge(g["vmix_ready"], count(i, 4, 2 * l + s))
                    for k in range(5):
                        side(step + k)
                    for j in (0, 2):
                        pool.wait_ge(g["rl_ready"], count(i, 8, 4 * l + j))
                        pv = bufB[:, j].rearrange("p a b -> p (a b)").rearrange("p (h n) -> p h n", h=HEADS)
                        nc.gpsimd.tensor_tensor(pv, pv, ssq[:, j, 0:8].unsqueeze(2).to_broadcast([P, HEADS, P]),
                                                ALU.mult).then_inc(g["pn_ready"], 1)
                    for k in range(5, LAYER_STEPS):
                        side(step + k)
                side(STEPS - 1)

            def second(i, k, after):
                plan = ALONE if after is None else WOVEN
                if k == SCORES:
                    for j, (s, t) in enumerate(units):
                        pool.wait_ge(g["raw_ready"], count(i, NT, j))
                        pool.nop(nofuse=True)
                        if t == 1:
                            nc.gpsimd.tensor_copy(csc[:, j, 0:P], raw[:, j, 0:P])
                        nc.gpsimd.tensor_tensor(csc[:, j, tok(t)], raw[:, j, tok(t)], causal[:], ALU.add).then_inc(g["cm_ready"], 1)
                if k in plan.top_done:
                    j = plan.top_done.index(k)
                    pool.wait_ge(g["top_ready"], count(i, NT, j))
                    link1(i, nc.gpsimd.tensor_tensor(wrk[:, j], wrk[:, j], raw[:, j, 0:S], ALU.subtract))
                    pool.nop(nofuse=True)
                    link1(i, nc.gpsimd.tensor_scalar(wrk[:, j], wrk[:, j], 0.0, None, ALU.is_lt))
                    nc.gpsimd.tensor_tensor(wrk[:, j], wrk[:, j], raw[:, j, 0:S], ALU.mult).then_inc(g["sp_ready"], 1)

            pipeline(pool, first, second)

        @block.scalar
        def _(act):
            nc.scalar.preload_act_table_set(LN_EXP)
            n_link = 0

            def rsqrt(i, out, x, scale, bias, ready):
                nonlocal n_link
                nc.scalar.activation(out, x, ACT.Ln, scale=scale).then_inc(alink, 1)
                act.wait_ge(alink, count(i, ACT_LINKS, n_link % ACT_LINKS))
                n_link += 1
                nc.scalar.activation(out, out, ACT.Exp, scale=-0.5, bias=bias).then_inc(ready, 1)

            def ln_root_of(i, k):
                s = k % 2
                act.wait_ge(g["var_ready"], count(i, 8, k))
                rsqrt(i, rstd[:, 2 * s:2 * s + 2], vareps[:, 2 * s:2 * s + 2], 1.0, 0.0, g["rstd_ready"])

            for s in slots:
                act.wait_ge(g["var_ready"], s + 1)
                js = slice(2 * s, 2 * s + 2)
                nc.scalar.activation(rstd[:, js], vareps[:, js], ACT.Ln).then_inc(act_start_link, 1)
                act.wait_ge(act_start_link, s + 1)
                nc.scalar.activation(rstd[:, js], rstd[:, js], ACT.Exp, scale=-0.5).then_inc(g["rstd_ready"], 1)
            act.wait_ge(prep_a, 3)

            def first(i, side, before):
                for s in slots:
                    act.wait_ge(g["xnT_done"], count(i, 2, s))
                    nc.scalar.copy(xT[:, s, :], ps0[:, 2 * s, 0:S])
                    nc.scalar.copy(hT[0:64, s, 0:S], ps0[0:64, 2 * s, 0:S])
                    nc.scalar.copy(hT[64:128, s, 1:S + 1], ps0[64:128, 2 * s, 0:S]).then_inc(g["h0_ready"], 1)
                for s in slots:
                    act.wait_ge(g["q0_done"], count(i, 2, s))
                    for t in tiles:
                        last = nc.scalar.activation(q0s[:, 2 * s + t], ps0[:, 2 * s + 1, tok(t)], ACT.Square,
                                                    scale=float(D) ** -0.5, accum_out=ms0[:, 2 * s + t:2 * s + t + 1])
                    last.then_inc(g["q0_sq"], 1)
                side(0)
                side(1)
                for s in slots:
                    act.wait_ge(g["fwn_ready"], count(i, 2, s))
                    rsqrt(i, fw_r[:, s], fw_n[:, s], LN_SCALE, ln_root[:], g["fwr_ready"])
                for s in slots:
                    act.wait_ge(g["qT0_done"], count(i, 2, s))
                    nc.scalar.copy(q0T[:, s, :], ps0[:, 2 * s, 0:S]).then_inc(g["qT0_ready"], 1)
                side(2)
                for s in slots:
                    act.wait_ge(g["gu_done"], count(i, 2, s))
                    for p in range(2):
                        last = nc.scalar.activation(th[:, s, p, :], ps0[:, 2 * s + p, 0:S], ACT.Tanh, scale=0.5)
                    last.then_inc(g["th_ready"], 1)
                nc.scalar.preload_act_table_set(LN_EXP)
                for k in range(3, HEAD_STEPS):
                    side(k)
                for l in range(DEPTH):
                    step = BLOCK[l]

                    def square(j):
                        t = j % 2
                        act.wait_ge(g["qk_done"], count(i, 8, 4 * l + j))
                        nc.scalar.activation(bufA[:, j].rearrange("p (a h) n -> p a (h n)", a=2),
                                             ps0[:, 2 * t:2 * t + 2, :], ACT.Square).then_inc(g["qk_sq"], 1)

                    def root(j):
                        act.wait_ge(g["qkn_ready"], count(i, 8, 4 * l + j))
                        rsqrt(i, ssq[:, j], qk_n[:, j], LN_SCALE, ln_root[:], g["qkr_ready"])

                    def values(s):
                        for t in tiles:
                            act.wait_ge(g["v_done"], count(i, 8, 4 * l + 2 * s + t))
                            nc.scalar.copy(v[:, s, t, :], ps1[:, t, :]).then_inc(g["v_ready"], 1)

                    def turned(j):
                        s, t = units[j]
                        act.wait_ge(g["qkT_done"], count(i, 8, 4 * l + j))
                        nc.scalar.copy(qkT[:, s, :, tok(t)], ps0[:, 2 * t:2 * t + 2, :].rearrange("p a (b n) -> p (a b) n", n=P)
                                       ).then_inc(g["qkT_ready"], 1)

                    def turned_p(j):
                        t = j % 2
                        act.wait_ge(g["pT_done"], count(i, 8, 4 * l + j))
                        nc.scalar.copy(bufC[:, j].rearrange("p (a h) n -> p a (h n)", a=2), ps0[:, 2 * t:2 * t + 2, :]
                                       ).then_inc(g["pT_ready"], 1)

                    square(0)
                    root(0)
                    square(1)
                    side(step)
                    root(1)
                    square(2)
                    values(0)
                    root(2)
                    side(step + 1)
                    square(3)
                    values(1)
                    root(3)
                    side(step + 2)
                    turned(0)
                    turned(1)
                    side(step + 3)
                    turned(2)
                    turned(3)
                    for j, (s, t) in enumerate(units):
                        act.wait_ge(g["max_ready"], count(i, 8, 4 * l + j))
                        for h in range(HEADS):
                            last = nc.scalar.activation(
                                bufB[:, j].rearrange("p a b -> p (a b)")[:, h * P:(h + 1) * P],
                                ps0[:, 2 * t + h // 4, P * (h % 4):P * (h % 4) + P], ACT.Exp, scale=8.0,
                                bias=ssq[:, j, 8 + h:9 + h], accum_out=ssq[:, j, h:h + 1])
                        last.then_inc(g["p_ready"], 1)
                        if j == 0:
                            side(step + 4)
                    side(step + 5)
                    turned_p(0)
                    turned_p(1)
                    side(step + 6)
                    turned_p(2)
                    turned_p(3)
                    side(step + 7)
                    for j, (s, t) in enumerate(units):
                        act.wait_ge(g["oT_done"], count(i, 8, 4 * l + j))
                        nc.scalar.copy(oT[:, s, :, tok(t)], ps0[:, 2 * t + s, :].rearrange("p (b n) -> p b n", n=P)
                                       ).then_inc(g["oT_ready"], 1)
                    side(step + 8)
                    side(step + 9)
                    for s in slots:
                        ln_root_of(i, 2 + 2 * l + s)
                    side(step + 10)
                    for s in slots:
                        act.wait_ge(g["hnT_done"], count(i, 4, 2 * l + s))
                        nc.scalar.activation(hnT[:, s, :], ps0[:, s, 0:S], ACT.Identity, bias=ln_b[:, l:l + 1],
                                             scale=ln_g[:, l:l + 1]).then_inc(g["hnT_ready"], 1)
                    if l == DEPTH - 1:
                        for s in slots:
                            ln_root_of(i, 6 + s)
                    for s in slots:
                        act.wait_ge(g["gate_done"], count(i, 4, 2 * l + s))
                        for c, (o, n) in enumerate(CH):
                            if c == 2:
                                act.wait_ge(g["w1_done"], count(i, 4, 2 * l + s))
                            src = ps0[0:n, s, c * S:(c + 1) * S] if c < 2 else ps0[0:n, 2, 0:S]
                            last = nc.scalar.activation(ge[0:n, s, c, :], src, ACT.Gelu, bias=b1g[0:n, l, c:c + 1])
                        last.then_inc(g["gelu_ready"], 1)
                        if s == 0:
                            side(step + 11)
                    nc.scalar.preload_act_table_set(LN_EXP)
                    side(step + 12)
                    side(step + 13)
                for s in slots:
                    ln_root_of(i, 8 + s)
                side(STEPS - 1)

            def second(i, k, after):
                plan = ALONE if after is None else WOVEN
                if k == TURN_Y:
                    act.wait_ge(g["yTp_done"], count(i, 1, 0))
                    nc.scalar.copy(yT[:], ps1[:, MISC, :].rearrange("p (s n) -> p s n", s=SLOTS)).then_inc(g["yT_ready"], 1)
                if k == PROJECT:
                    act.wait_ge(g["proj_done"], count(i, 1, 0))
                    for s in slots:
                        nc.scalar.activation(a_qT[:, s, :], ps1[:, s, 0:S], ACT.Identity, bias=a_bqs[:], scale=float(D) ** -0.5)
                        nc.scalar.activation(a_kT[:, s, 0:S], ps1[:, s, S:2 * S], ACT.Identity, bias=a_bk
                                             ).then_inc(g["qk1_ready"], 1)
                if k == SCORES:
                    act.wait_ge(g["logit_ready"], count(i, 1, 0))
                    nc.scalar.activation(g_e[:], g_l[:], ACT.Exp).then_inc(g["e_ready"], 1)
                    for j in range(NT):
                        act.wait_ge(g["sc_done"], count(i, NT, j))
                        nc.scalar.copy(raw[:, j, :], ps1[:, j % 2, 0:S + SC]).then_inc(g["raw_ready"], 1)
                if k == TURN_COMB:
                    act.wait_ge(g["combT_done"], count(i, 1, 0))
                    nc.scalar.copy(combT[:], ps1[0:EXPERTS, MISC, :]).then_inc(g["combT_ready"], 1)
                if k in plan.up:
                    e = plan.up.index(k)
                    for c in range(EC):
                        if c == 0 and e >= 1:
                            act.wait_ge(g["eo_done"], count(i, EXPERTS, e - 1))
                        act.wait_ge(g["h_done"], count(i, EXPERTS * EC, EC * e + c))
                        nc.scalar.activation(hbuf[:, c, :], ps1[:, c % 2, :], ACT.Relu, bias=m_b1[:, e, c:c + 1]
                                             ).then_inc(g["relu_done"], 1)
                if k in plan.softmax:
                    j = plan.softmax.index(k)
                    act.wait_ge(g["sp_ready"], count(i, NT, j))
                    act.wait_ge(g["cmax_ready"], count(i, NT, j))
                    n = P * (j % 2 + 1)
                    nc.scalar.activation(wrk[:, j], wrk[:, j], ACT.Exp, bias=nmax[:, j, 0:1], accum_out=lsum[:, j, 0:1])
                    nc.scalar.activation(csc[:, j, 0:n], csc[:, j, 0:n], ACT.Exp, bias=nmax[:, j, 1:2], accum_out=lsum[:, j, 1:2])
                    nc.scalar.activation(raw[:, j, S:], raw[:, j, S:], ACT.Exp, bias=nmax[:, j, 2:3], accum_out=lsum[:, j, 2:3]
                                         ).then_inc(g["ex_ready"], 1)
                if k in plan.p_turn:
                    j = plan.p_turn.index(k)
                    act.wait_ge(g["pwT_done"], count(i, NT, j))
                    nc.scalar.copy(a_pT[:, j // 2, :, tok(j % 2)], ps1[:, MISC, 0:S].rearrange("p (a n) -> p a n", n=P)
                                   ).then_inc(g["pwT_ready"], 1)
                if k in plan.attend:
                    s = plan.attend.index(k)
                    act.wait_ge(g["at_done"], count(i, 2, s))
                    nc.scalar.copy(a_oT[:, s, :], ps1[:, MISC, 0:S]).then_inc(g["at_ready"], 1)

            pipeline(act, first, second)

        @block.vector
        def _(dve):
            def vt(out, a, b, op):
                return nc.vector.tensor_tensor(out, a, b, op)

            nc.vector.memset(fw_gate[:], 0.0)
            nc.vector.memset(fw_up[:], 0.0)
            nc.vector.memset(fw_down[:], 0.0)
            nc.vector.memset(hT[64:128, :, 0:1], 0.0)
            nc.vector.memset(ln_root[:], 0.5 * math.log(LN_SCALE))
            nc.vector.memset(third[:, 0:2], 1.0 / 3.0)
            nc.vector.memset(third[:, 2:3], 1.0 / (3.0 * COMP)).then_inc(consts, 1)

            def newton(link, y, x, t):
                link(nc.vector.scalar_tensor_tensor(t, y, -0.5, y, ALU.mult, ALU.mult))
                link(vt(t, t, x, ALU.mult))
                return nc.vector.scalar_tensor_tensor(y, t, 1.5, y, ALU.add, ALU.mult)

            def after_wait(op, *args, **kw):
                dve.nop(nofuse=True)
                return op(*args, **kw)

            def moments(link, s, src):
                for t in tiles:
                    last = nc.vector.bn_stats(stats[:, 2 * s + t, :], src(t))
                link(last)
                for t in tiles:
                    last = after_wait(nc.vector.bn_aggr, meanvar[:, 2 * s + t, :], stats[:, 2 * s + t, :])
                link(last)
                nc.vector.tensor_scalar(vareps[:, 2 * s:2 * s + 2], meanvar[:, 2 * s:2 * s + 2, 1], 1e-5, None, ALU.add
                                        ).then_inc(g["var_ready"], 1)

            def normalise(link, s, src, dst, ready):
                js = slice(2 * s, 2 * s + 2)
                link(newton(link, rstd[:, js], vareps[:, js], newt[:, js, 0]))
                for t in tiles:
                    j = 2 * s + t
                    last = nc.vector.tensor_scalar(dst[:, j], src(t), meanvar[:, j, 0:1], rstd[:, j:j + 1],
                                                   ALU.subtract, ALU.mult)
                last.then_inc(ready, 1)

            def start_chain():
                n = 0

                def link(ins):
                    nonlocal n
                    n += 1
                    ins.then_inc(start_link, 1)
                    dve.wait_ge(start_link, n)
                return link

            link_start = start_chain()
            dve.wait_ge(x_loaded, 16)
            for s in slots:
                moments(link_start, s, lambda t: x0[:, 2 * s + t])
            for s in slots:
                dve.wait_ge(g["rstd_ready"], s + 1)
                normalise(link_start, s, lambda t: x0[:, 2 * s + t], xn, g["xn_ready"])

            dve.wait_ge(loaded[0], 16 * n_load[0])
            nc.vector.tensor_copy(identb[:], ident[:])
            nc.vector.tensor_copy(bandb[:], band)
            nc.vector.tensor_scalar_mul(a_bqs[:], a_bq, float(D) ** -0.5).then_inc(prep_a, 1)
            for l in range(DEPTH):
                for t in tiles:
                    vt(tab_cos[:, l, t], rot_cos[:, t], qk_scale[:, l], ALU.mult)
                    for h in range(2):
                        last = vt(tab_sin[:, l, t, :, 32 * h:32 * h + 32], rot_sin[:, t, :, 32 * h:32 * h + 32],
                                  qk_scale[:, l, :, 32 * (1 - h):32 * (2 - h)], ALU.mult)
                last.then_inc(prep_a, 1)
            dve.wait_ge(prep_a, 3)

            def chain(part, per_pair):
                n = 0

                def link(i, ins):
                    nonlocal n
                    ins.then_inc(dlink[part], 1)
                    dve.wait_ge(dlink[part], count(i, per_pair, n % per_pair))
                    n += 1

                def links():
                    return n
                return link, links

            link0, links0 = chain(0, DVE_LINKS[0])
            link1, links1 = chain(1, DVE_LINKS[1])

            def first(i, side, before):
                def link(ins):
                    link0(i, ins)

                side(0)
                side(1)
                for s in slots:
                    dve.wait_ge(g["q0_done"], count(i, 2, s))
                    dve.wait_ge(g["q0_sq"], count(i, 2, s))
                    js = slice(2 * s, 2 * s + 2)
                    link(vt(q0[:, js], ps0[:, 2 * s + 1, 0:S].rearrange("p (t n) -> p t n", t=2),
                            q_norm[:].unsqueeze(1).to_broadcast([P, 2, P]), ALU.mult))
                    link(vt(q0s[:, js], q0[:, js], q0[:, js], ALU.mult))
                    link(nc.vector.tensor_reduce(hs0[:, js], q0s[:, js].rearrange("p t (h n) -> p t h n", h=NH), AX_X, ALU.add))
                    nc.vector.tensor_scalar(fw_n[:, s, 0:TILES], ms0[:, js], 1e-6, None, ALU.add)
                    nc.vector.tensor_scalar(fw_n[:, s, TILES:], hs0[:, js].rearrange("p t h -> p (t h)"), 1e-24, None, ALU.max
                                            ).then_inc(g["fwn_ready"], 1)
                for s in slots:
                    js = slice(2 * s, 2 * s + 2)
                    dve.wait_ge(g["fwr_ready"], count(i, 2, s))
                    dve.wait_ge(g["fwn_ready"], count(i, 2, s))
                    link(newton(link, fw_r[:, s], fw_n[:, s], newt[:, 2 * s, 0:TILES + TILES * NH]))
                    rrb = fw_r[:, s, 0:TILES].unsqueeze(2).to_broadcast([P, 2, NH])
                    link(vt(hs0[:, js], hs0[:, js], fw_r[:, s, TILES:].rearrange("p (t h) -> p t h", t=TILES), ALU.mult))
                    link(vt(hs0[:, js], hs0[:, js], rrb, ALU.mult))
                    link(nc.vector.tensor_scalar(hs0[:, js], hs0[:, js], 1e-5, None, ALU.add))
                    link(after_wait(nc.vector.reciprocal, hr0[:, js], hs0[:, js]))
                    link(vt(hr0[:, js], hr0[:, js], rrb, ALU.mult))
                    vt(q0s[:, js].rearrange("p t (h n) -> p (t h) n", h=NH), q0[:, js].rearrange("p t (h n) -> p (t h) n", h=NH),
                       hr0[:, js].rearrange("p t h -> p (t h)").unsqueeze(2).to_broadcast([P, 2 * NH, DH]), ALU.mult
                       ).then_inc(g["qn0_ready"], 1)
                side(2)
                for s in slots:
                    dve.wait_ge(g["th_ready"], count(i, 2, s))
                    for p in range(2):
                        last = nc.vector.scalar_tensor_tensor(th[:, s, p], th[:, s, p], 1.0, ps0[:, 2 * s + p, 0:S], ALU.add, ALU.mult)
                    link(last)
                    for p in range(2):
                        last = nc.vector.scalar_tensor_tensor(th[:, s, p], th[:, s, p], 0.5, ps0[:, 2 * s + p, S:2 * S], ALU.mult, ALU.mult)
                    last.then_inc(g["hid_ready"], 1)
                side(3)
                for s in slots:
                    dve.wait_ge(g["o0_done"], count(i, 2, s))
                    vt(res[:, 2 * s:2 * s + 2], ps0[:, 2 * s + 1, 0:S].rearrange("p (t n) -> p t n", t=2), x0[:, 2 * s:2 * s + 2],
                       ALU.add).then_inc(x_used, 1)
                for k in range(4, HEAD_STEPS):
                    side(k)

                for l in range(DEPTH):
                    step = BLOCK[l]

                    def squared_norms(j):
                        dve.wait_ge(g["qk_sq"], count(i, 8, 4 * l + j))
                        link(nc.vector.tensor_reduce(qk_n[:, j], bufA[:, j], AX_X, ALU.add))
                        nc.vector.tensor_scalar(qk_n[:, j], qk_n[:, j], 1e-24, None, ALU.max).then_inc(g["qkn_ready"], 1)

                    def unit_norms(j):
                        t = j % 2
                        dve.wait_ge(g["qkr_ready"], count(i, 8, 4 * l + j))
                        dve.wait_ge(g["qkn_ready"], count(i, 8, 4 * l + j))
                        link(newton(link, ssq[:, j], qk_n[:, j], newt[:, j]))
                        vt(bufB[:, j], ps0[:, 2 * t:2 * t + 2, :].rearrange("p a (h n) -> p (a h) n", n=DIM_HEAD),
                           ssq[:, j].unsqueeze(2).to_broadcast([P, 16, DIM_HEAD]), ALU.mult).then_inc(g["qn_ready"], 1)

                    def cos_part(j):
                        t = j % 2
                        dve.wait_ge(g["qn_ready"], count(i, 8, 4 * l + j))
                        vt(bufC[:, j].rearrange("p (a h) n -> p a h n", a=2), bufB[:, j].rearrange("p (a h) n -> p a h n", a=2),
                           tab_cos[:, l, t].unsqueeze(2).to_broadcast([P, 2, HEADS, DIM_HEAD]), ALU.mult
                           ).then_inc(g["u_ready"], 1)

                    def rotated(j):
                        dve.wait_ge(g["r_ready"], count(i, 8, 4 * l + j))
                        dve.wait_ge(g["u_ready"], count(i, 8, 4 * l + j))
                        vt(bufC[:, j], bufC[:, j], bufA[:, j], ALU.add).then_inc(g["s1_ready"], 1)

                    squared_norms(0)
                    unit_norms(0)
                    squared_norms(1)
                    cos_part(0)
                    side(step)
                    unit_norms(1)
                    squared_norms(2)
                    cos_part(1)
                    side(step + 1)
                    unit_norms(2)
                    squared_norms(3)
                    cos_part(2)
                    unit_norms(3)
                    rotated(1)
                    cos_part(3)
                    rotated(3)
                    side(step + 2)
                    side(step + 3)

                    def row_maxima(j):
                        t = j % 2
                        dve.wait_ge(g["sim_done"], count(i, 8, 4 * l + j))
                        sim = ps0[:, 2 * t:2 * t + 2, :].rearrange("p a (h n) -> p (a h) n", n=P)
                        link(nc.vector.tensor_reduce(ssq[:, j, 8:16], sim, AX_X, ALU.max))
                        nc.vector.tensor_scalar_mul(ssq[:, j, 8:16], ssq[:, j, 8:16], -8.0).then_inc(g["max_ready"], 1)

                    def over_sums(j):
                        dve.wait_ge(g["p_ready"], count(i, 8, 4 * l + j))
                        after_wait(nc.vector.reciprocal, ssq[:, j, 0:8], ssq[:, j, 0:8]).then_inc(g["rl_ready"], 1)
                        if j % 2 == 1:
                            dve.wait_ge(g["rl_ready"], count(i, 8, 4 * l + j))
                            pv = bufB[:, j].rearrange("p a b -> p (a b)").rearrange("p (h n) -> p h n", h=HEADS)
                            vt(pv, pv, ssq[:, j, 0:8].unsqueeze(2).to_broadcast([P, HEADS, P]), ALU.mult
                               ).then_inc(g["pn1_ready"], 1)

                    row_maxima(0)
                    row_maxima(1)
                    side(step + 4)
                    over_sums(0)
                    row_maxima(2)
                    over_sums(1)
                    row_maxima(3)
                    over_sums(2)
                    over_sums(3)
                    for k in range(5, 9):
                        side(step + k)
                    for s in slots:
                        dve.wait_ge(g["x1T_done"], count(i, 4, 2 * l + s))
                        pr = ps0[:, s, 0:S]
                        vt(hT[0:64, s, 0:S], pr[0:64], xT[0:64, s], ALU.add)
                        vt(hT[64:128, s, 1:S + 1], pr[64:128], xT[64:128, s], ALU.add).then_inc(g["h2_ready"], 1)
                        vt(x1T[:, s], pr, xT[:, s], ALU.add)
                    side(step + 9)
                    for s in slots:
                        dve.wait_ge(g["h2tok_done"], count(i, 4, 2 * l + s))
                        moments(link, s, lambda t: ps0[:, 2 + s, tok(t)])
                    for s in slots:
                        dve.wait_ge(g["rstd_ready"], count(i, 8, 2 + 2 * l + s))
                        normalise(link, s, lambda t: ps0[:, 2 + s, tok(t)], xn, g["hn_ready"])
                    if l == DEPTH - 1:
                        dve.wait_ge(x_loaded, 16 * (i + 1))
                        dve.wait_ge(g["hn_ready"], count(i, 4, 2 * l + 1))
                        for s in slots:
                            moments(link, s, lambda t: x0[:, 2 * s + t])
                        for s in slots:
                            dve.wait_ge(g["rstd_ready"], count(i, 8, 6 + s))
                            dve.wait_ge(g["hnT_done"], count(i, 4, 2 * l + 1))
                            normalise(link, s, lambda t: x0[:, 2 * s + t], xn, g["xn_ready"])
                    side(step + 10)
                    for s in slots:
                        dve.wait_ge(g["w1_done"], count(i, 4, 2 * l + s))
                        dve.wait_ge(g["gelu_ready"], count(i, 4, 2 * l + s))
                        for c, (o, n) in enumerate(CH):
                            src = ps0[0:n, 3, c * S:(c + 1) * S] if c < 2 else ps0[0:n, 2, S:2 * S]
                            last = nc.vector.scalar_tensor_tensor(ge[0:n, s, c], src, b1a[0:n, l, c:c + 1], ge[0:n, s, c],
                                                                  ALU.add, ALU.mult)
                        last.then_inc(g["u2_ready"], 1)
                        if s == 0:
                            side(step + 11)
                    side(step + 12)
                    for s in slots:
                        dve.wait_ge(g["x2T_done"], count(i, 4, 2 * l + s))
                        pr = ps0[:, 3 * s, 0:S]
                        if l == 0:
                            nc.vector.scalar_tensor_tensor(hT[0:64, s, 0:S], pr[0:64], b2[0:64, l:l + 1], x1T[0:64, s],
                                                           ALU.add, ALU.add)
                            nc.vector.scalar_tensor_tensor(hT[64:128, s, 1:S + 1], pr[64:128], b2[64:128, l:l + 1],
                                                           x1T[64:128, s], ALU.add, ALU.add)
                        nc.vector.scalar_tensor_tensor(xT[:, s], pr, b2[:, l:l + 1], x1T[:, s], ALU.add, ALU.add
                                                       ).then_inc(g["x2T_ready" if l else "h1_ready"], 1)
                    side(step + 13)
                dve.wait_ge(g["x2_done"], count(i, 1, 0))
                dve.wait_ge(g["xn_ready"], count(i + 1, 2, 1))
                vt(x1[:], ps0[:, 1, :].rearrange("p (j n) -> p j n", n=P), res[:], ALU.add).then_inc(g["x1_ready"], 1)
                dve.wait_ge(g["x1_ready"], count(i, 1, 0))
                for s in slots:
                    moments(link, s, lambda t: x1[:, 2 * s + t])
                side(STEPS - 1)
                assert links0() % DVE_LINKS[0] == 0, links0()

            def second(i, k, after):
                plan = ALONE if after is None else WOVEN
                def link(ins):
                    link1(i, ins)

                if k == TURN_Y:
                    for s in slots:
                        dve.wait_ge(g["rstd_ready"], count(i, 8, 8 + s))
                        normalise(link, s, lambda t: x1[:, 2 * s + t], yn, g["y_ready"])
                if k == PROJECT:
                    dve.wait_ge(g["y_ready"], count(i, 2, 1))
                    vt(x1[:], x1[:], a_bo[:].unsqueeze(1).to_broadcast([P, NT, P]), ALU.add).then_inc(g["x1b_ready"], 1)
                    dve.wait_ge(g["proj_done"], count(i, 1, 0))
                    for s in slots:
                        vt(a_v[:, s], ps1[:, MOE_OUT, s * S:(s + 1) * S].rearrange("p (t n) -> p t n", t=2),
                           a_bv[:].unsqueeze(1).to_broadcast([P, 2, P]), ALU.add)
                    link(nc.vector.tensor_copy(g_l[:], ps1[:, MISC, 0:NT * EXPERTS].rearrange("p (t e) -> p t e", t=NT)))
                    for j in range(NT):
                        last = after_wait(nc.vector.max, g_m[:, j], g_l[:, j])
                    link(last)
                    for j in range(NT):
                        last = after_wait(nc.vector.max_index, g_i[:, j], g_m[:, j], g_l[:, j])
                    link(last)
                    nc.vector.tensor_copy(g_f[:], g_i[:])
                    vt(g_l[:], g_l[:], g_m[:, :, 0:1].to_broadcast([P, NT, EXPERTS]), ALU.subtract).then_inc(g["logit_ready"], 1)
                    for s in slots:
                        dve.wait_ge(g["qk1_ready"], count(i, 2, s))
                        link(nc.vector.tensor_reduce(kcs[:, s], a_kT[:, s, 0:S].rearrange("p (c n) -> p c n", n=COMP), AX_X, ALU.add))
                        nc.vector.tensor_scalar_mul(a_kT[:, s, S:S + SC], kcs[:, s], 1.0 / COMP).then_inc(g["kc_ready"], 1)
                if k == SCORES:
                    dve.wait_ge(g["e_ready"], count(i, 1, 0))
                    io = iota8[:].unsqueeze(1).to_broadcast([P, NT, EXPERTS])
                    vt(comb[:], io, g_f[:, :, 0:1].to_broadcast([P, NT, EXPERTS]), ALU.is_equal)
                    link(vt(g_m[:], io, g_f[:, :, 1:2].to_broadcast([P, NT, EXPERTS]), ALU.is_equal))
                    link(vt(comb[:], comb[:], g_m[:], ALU.add))
                    link(vt(comb[:], comb[:], g_e[:], ALU.mult))
                    link(nc.vector.tensor_reduce(g_s[:], comb[:], AX_X, ALU.add))
                    link(after_wait(nc.vector.reciprocal, g_s[:], g_s[:]))
                    vt(comb[:], comb[:], g_s[:].unsqueeze(2).to_broadcast([P, NT, EXPERTS]), ALU.mult).then_inc(g["comb_ready"], 1)
                if k == EXPERT_BIAS:
                    dve.wait_ge(g["b2_done"], count(i, 1, 0))
                    dve.wait_ge(g["x1b_ready"], count(i, 1, 0))
                    dve.wait_ge(stored, 16 * i)
                    vt(y_out[:], ps1[:, MISC, :].rearrange("p (j n) -> p j n", n=P), x1[:], ALU.add).then_inc(g["acc0_ready"], 1)
                if k in plan.add:
                    e = plan.add.index(k)
                    dve.wait_ge(g["eo_done"], count(i, EXPERTS, e))
                    if e == 0:
                        dve.wait_ge(g["acc0_ready"], count(i, 1, 0))
                    else:
                        dve.wait_ge(g["acc_done"], count(i, EXPERTS, e - 1))
                    for j in range(NT):
                        last = nc.vector.scalar_tensor_tensor(y_out[:, j], ps1[:, MOE_OUT, tok(j)], comb[:, j, e:e + 1], y_out[:, j],
                                                              ALU.mult, ALU.add)
                    last.then_inc(g["acc_done"], 1)
                if k in plan.top:
                    j, part = plan.top.index(k) // 4, plan.top.index(k) % 4
                    if part == 0:
                        dve.wait_ge(g["raw_ready"], count(i, NT, j))
                    for r in (2 * part, 2 * part + 1):
                        src = raw[:, j, 0:S] if r == 0 else wrk[:, j]
                        link(after_wait(nc.vector.max, top8[:, j], src))
                        if r == 0:
                            nc.vector.tensor_scalar(nmax[:, j, 0:1], top8[:, j, 0:1], 0.0, -1.0, ALU.max, ALU.mult)
                        last = after_wait(nc.vector.match_replace, wrk[:, j], top8[:, j], src, -BIG)
                        if r < TOP_K // 8 - 1:
                            link(last)
                    if part == 3:
                        last.then_inc(g["top_ready"], 1)
                        dve.wait_ge(g["cm_ready"], count(i, NT, j))
                        nc.vector.tensor_reduce(nmax[:, j, 1:2], csc[:, j, 0:P * (j % 2 + 1)], AX_X, ALU.max, negate=True)
                        nc.vector.tensor_reduce(nmax[:, j, 2:3], raw[:, j, S:], AX_X, ALU.max, negate=True
                                                ).then_inc(g["cmax_ready"], 1)
                if k in plan.combine:
                    j = plan.combine.index(k)
                    n = P * (j % 2 + 1)
                    dve.wait_ge(g["ex_ready"], count(i, NT, j))
                    link(after_wait(nc.vector.reciprocal, lsum[:, j], lsum[:, j]))
                    link(vt(lsum[:, j], lsum[:, j], third[:], ALU.mult))
                    link(nc.vector.tensor_scalar(wrk[:, j], wrk[:, j], lsum[:, j, 0:1], None, ALU.mult))
                    link(nc.vector.scalar_tensor_tensor(wrk[:, j, 0:n], csc[:, j, 0:n], lsum[:, j, 1:2], wrk[:, j, 0:n],
                                                        ALU.mult, ALU.add))
                    w4 = wrk[:, j].rearrange("p (c n) -> p c n", n=COMP)
                    nc.vector.scalar_tensor_tensor(w4, raw[:, j, S:].unsqueeze(2).to_broadcast([P, SC, COMP]),
                                                   lsum[:, j, 2:3], w4, ALU.mult, ALU.add).then_inc(g["pw_ready"], 1)
                if k in plan.add_attention:
                    s = plan.add_attention.index(k)
                    js = slice(2 * s, 2 * s + 2)
                    dve.wait_ge(g["wo_done"], count(i, 2, s))
                    dve.wait_ge(g["acc_done"], count(i, EXPERTS, max(e for e in range(EXPERTS) if plan.add[e] <= k)))
                    last = vt(y_out[:, js], ps1[:, MISC, 0:S].rearrange("p (t n) -> p t n", t=2), y_out[:, js], ALU.add)
                    last.then_inc(g[("half_ready", "out_ready")[s]], 1)
                    if s == 0:
                        dve.wait_ge(g["half_ready"], count(i, 1, 0))
                if k == plan.steps - 1:
                    assert links1() % DVE_LINKS[1] == 0, links1()

            pipeline(dve, first, second)

        @block.tensor
        def _(pe):
            def mm(out, a, b, start=True, stop=True):
                return nc.tensor.matmul(out, a, b, start=start, stop=stop)

            pe.wait_ge(prep_a, 3)

            def first(i, side, before):
                for s in slots:
                    pe.wait_ge(g["xn_ready"], count(i, 2, s))
                    for t in tiles:
                        last = nc.tensor.transpose(ps0[:, 2 * s, tok(t)], xn[:, 2 * s + t], ident[:])
                    last.then_inc(g["xnT_done"], 1)
                if before is not None:
                    pe.wait_ge(g["x1_ready"], count(before, 1, 0))
                for s in slots:
                    pe.wait_ge(g["h0_ready"], count(i, 2, s))
                    for t in tiles:
                        last = mm(ps0[:, 2 * s + 1, tok(t)], xT[:, s, tok(t)], fw_q[:])
                    last.then_inc(g["q0_done"], 1)
                side(0)
                side(1)
                side(2)
                for s in slots:
                    pe.wait_ge(g["qn0_ready"], count(i, 2, s))
                    for t in tiles:
                        last = nc.tensor.transpose(ps0[:, 2 * s, tok(t)], q0s[:, 2 * s + t], ident[:])
                    last.then_inc(g["qT0_done"], 1)
                for s in slots:
                    pe.wait_ge(g["qT0_ready"], count(i, 2, s))
                    for p in range(2):
                        r = slice(64 * p, 64 * p + 64)
                        mm(ps0[:, 2 * s + p, 0:S], fw_gate[r, :], q0T[r, s, :])
                        last = mm(ps0[:, 2 * s + p, S:2 * S], fw_up[r, :], q0T[r, s, :])
                    last.then_inc(g["gu_done"], 1)
                side(3)
                side(4)
                for s in slots:
                    pe.wait_ge(g["hid_ready"], count(i, 2, s))
                    for t in tiles:
                        for p in range(2):
                            last = mm(ps0[:, 2 * s + 1, P * t + 64 * p:P * t + 64 * p + 64], th[:, s, p, tok(t)], fw_down[:, p, :])
                    last.then_inc(g["o0_done"], 1)
                side(5)
                side(6)
                if before is None:
                    pe.wait_ge(loaded[1], 16 * n_load[1])

                for l in range(DEPTH):
                    step = BLOCK[l]

                    def q_and_k(j):
                        s, t = units[j]
                        if j < 2 and l == 0:
                            pe.wait_ge(x_used, count(i, 2, j))
                        if j < 2 and l == 1:
                            pe.wait_ge(g["h1_ready"], count(i, 2, j))
                        if j >= 2:
                            pe.wait_ge(g["qn_ready"], count(i, 8, 4 * l + j - 2))
                        mm(ps0[:, 2 * t, :], hT[:, s, tok(t)], wqkv[:, l, 0:INNER])
                        mm(ps0[:, 2 * t + 1, :], hT[:, s, tok(t)], wqkv[:, l, INNER:2 * INNER]).then_inc(g["qk_done"], 1)

                    def values(s):
                        for t in tiles:
                            if s == 1:
                                pe.wait_ge(g["v_ready"], count(i, 8, 4 * l + t))
                            elif before is not None:
                                e = max(e for e in range(EXPERTS) if WOVEN.up[e] <= step)
                                pe.wait_ge(g["relu_done"], count(before, EXPERTS * EC, EC * e + EC - 2 + t))
                            mm(ps1[:, t, :], hT[:, s, tok(t)], wqkv[:, l, 2 * INNER:3 * INNER]).then_inc(g["v_done"], 1)

                    def turn_qk(j):
                        s, t = units[j]
                        pe.wait_ge(g["s1_ready" if t else "s_ready"], count(i, 4, 2 * l + s))
                        if j < 2:
                            pe.wait_ge(g["qn_ready"], count(i, 8, 4 * l + j + 2))
                        else:
                            pe.wait_ge(g["qkT_ready"], count(i, 8, 4 * l + j - 2))
                        for a in range(8):
                            last = nc.tensor.transpose(ps0[:, 2 * t + a // 4, P * (a % 4):P * (a % 4) + P],
                                                       bufC[:, j].rearrange("p a b -> p (a b)")[:, a * P:(a + 1) * P], ident[:])
                        last.then_inc(g["qkT_done"], 1)

                    q_and_k(0)
                    q_and_k(1)
                    side(step)
                    q_and_k(2)
                    values(0)
                    side(step + 1)
                    q_and_k(3)
                    values(1)
                    side(step + 2)
                    turn_qk(0)
                    turn_qk(1)
                    side(step + 3)
                    turn_qk(2)
                    turn_qk(3)
                    for j, (s, t) in enumerate(units):
                        if j < 2:
                            pe.wait_ge(g["qkT_ready"], count(i, 8, 4 * l + j + 2))
                        else:
                            pe.wait_ge(g["p_ready"], count(i, 8, 4 * l + j - 2))
                        for h in range(2):
                            o = ps0[:, 2 * t + h, :]
                            mm(o, identb[:], bandb[:, t, :].unsqueeze(1).to_broadcast([P, 4, P]), stop=False)
                            r = slice(64 * h, 64 * h + 64)
                            for a in range(4):
                                c = a * P
                                q, kk = qkT[r, s, a], qkT[r, s, 4 + a]
                                if t == 0:
                                    last = mm(o[:, c:c + P], q[:, 0:P], kk[:, 0:P], start=False, stop=(a == 3))
                                else:
                                    mm(o[:, c:c + 64], q[:, P:2 * P], kk[:, P:P + 64], start=False, stop=False)
                                    mm(o[0:64, c + 64:c + P], q[:, P:P + 64], kk[:, 64:P], start=False, stop=(a == 3))
                                    last = mm(o[64:128, c + 64:c + P], q[:, P + 64:2 * P], kk[:, P + 64:2 * P],
                                              start=False, stop=(a == 3))
                        last.then_inc(g["sim_done"], 1)
                        if j == 1:
                            side(step + 4)
                    side(step + 5)
                    for j, (s, t) in enumerate(units):
                        pe.wait_ge(g["pn1_ready" if t else "pn_ready"], count(i, 4, 2 * l + s))
                        if j < 2:
                            pe.wait_ge(g["p_ready"], count(i, 8, 4 * l + j + 2))
                        else:
                            pe.wait_ge(g["pT_ready"], count(i, 8, 4 * l + j - 2))
                        for a in range(8):
                            last = nc.tensor.transpose(ps0[:, 2 * t + a // 4, P * (a % 4):P * (a % 4) + P],
                                                       bufB[:, j].rearrange("p a b -> p (a b)")[:, a * P:(a + 1) * P], ident[:])
                        last.then_inc(g["pT_done"], 1)
                        if j == 1:
                            side(step + 6)
                    side(step + 7)
                    for j, (s, t) in enumerate(units):
                        pe.wait_ge(g["pT_ready"], count(i, 8, 4 * l + max(j, 2 + t)))
                        if t == 1:
                            pe.wait_ge(g["vmix_ready"], count(i, 4, 2 * l + s))
                        pT = bufC[:, j].rearrange("p a b -> p (a b)").rearrange("p (h n) -> p h n", n=P)
                        for a in range(4):
                            for h in range(2):
                                o = ps0[64 * h:64 * h + 64, 2 * t + s, a * P:(a + 1) * P]
                                hd = slice(64 * (2 * a + h), 64 * (2 * a + h) + 64)
                                if t == 0:
                                    last = mm(o, v[:, s, 0, hd], pT[:, 4 * h + a, :])
                                else:
                                    mm(o[:, 0:64], vmix[:, s, hd], pT[:, 4 * h + a, 0:64])
                                    last = mm(o[:, 64:128], v[:, s, 1, hd], pT[:, 4 * h + a, 64:128])
                        last.then_inc(g["oT_done"], 1)
                    side(step + 8)
                    for s in slots:
                        pe.wait_ge(g["oT_ready"], count(i, 8, 4 * l + (3 if s else 2)))
                        for a in range(4):
                            last = mm(ps0[:, s, 0:S], wo[:, l, a, :], oT[:, s, a, :], start=(a == 0), stop=(a == 3))
                        last.then_inc(g["x1T_done"], 1)
                    side(step + 9)
                    for s in slots:
                        pe.wait_ge(g["h2_ready"], count(i, 4, 2 * l + s))
                        for t in tiles:
                            last = nc.tensor.transpose(ps0[:, 2 + s, tok(t)], hT[:, s, tok(t)], ident[:])
                        last.then_inc(g["h2tok_done"], 1)
                    side(step + 10)
                    for s in slots:
                        pe.wait_ge(g["hn_ready"], count(i, 4, 2 * l + s))
                        for t in tiles:
                            last = nc.tensor.transpose(ps0[:, s, tok(t)], xn[:, 2 * s + t], ident[:])
                        last.then_inc(g["hnT_done"], 1)

                    def hidden(s, half, c):
                        o, n = CH[c]
                        bank = 2 if c == 2 else (s if half else 3)
                        at = c * S if c < 2 else (1 - half) * S
                        return mm(ps0[0:n, bank, at:at + S], w1[:, l, half * HID + o:half * HID + o + n], hnT[:, s, :])

                    for s in slots:
                        pe.wait_ge(g["hnT_ready"], count(i, 4, 2 * l + s))
                        hidden(s, 1, 0)
                        hidden(s, 1, 1).then_inc(g["gate_done"], 1)
                        if s == 1:
                            side(step + 11)
                            pe.wait_ge(g["u2_ready"], count(i, 4, 2 * l))
                        hidden(s, 1, 2)
                        hidden(s, 0, 2)
                        hidden(s, 0, 0)
                        hidden(s, 0, 1).then_inc(g["w1_done"], 1)
                    side(step + 12)
                    for s in slots:
                        pe.wait_ge(g["u2_ready"], count(i, 4, 2 * l + s))
                        for c, (o, n) in enumerate(CH):
                            last = mm(ps0[:, 3 * s, 0:S], w2[0:n, l, c, :], ge[0:n, s, c, :], start=(c == 0), stop=(c == len(CH) - 1))
                        last.then_inc(g["x2T_done"], 1)
                    side(step + 13)
                for s in slots:
                    pe.wait_ge(g["x2T_ready"], count(i, 2, s))
                    for t in tiles:
                        last = nc.tensor.transpose(ps0[:, 1, tok(2 * s + t)], xT[:, s, tok(t)], ident[:])
                last.then_inc(g["x2_done"], 1)
                side(STEPS - 1)

            def second(i, k, after):
                plan = ALONE if after is None else WOVEN
                if k == TURN_Y:
                    for s in slots:
                        pe.wait_ge(g["y_ready"], count(i, 2, s))
                        for t in tiles:
                            last = nc.tensor.transpose(ps1[:, MISC, tok(2 * s + t)], yn[:, 2 * s + t], ident[:])
                    last.then_inc(g["yTp_done"], 1)
                if k == PROJECT:
                    pe.wait_ge(g["yT_ready"], count(i, 1, 0))
                    for s in slots:
                        mm(ps1[:, s, 0:S], a_wq[:], yT[:, s, :])
                        mm(ps1[:, s, S:2 * S], a_wk[:], yT[:, s, :])
                        for t in tiles:
                            mm(ps1[:, MOE_OUT, tok(2 * s + t)], yT[:, s, tok(t)], a_wv[:])
                    for j, (s, t) in enumerate(units):
                        last = mm(ps1[:, MISC, EXPERTS * j:EXPERTS * (j + 1)], yT[:, s, tok(t)], m_gate[:])
                    last.then_inc(g["proj_done"], 1)
                if k == SCORES:
                    for j, (s, t) in enumerate(units):
                        pe.wait_ge(g["kc_ready"], count(i, 2, s if j != 1 else 1))
                        if j >= 2:
                            pe.wait_ge(g["raw_ready"], count(i, NT, j - 2))
                        mm(ps1[:, j % 2, 0:S + SC], a_qT[:, s, tok(t)], a_kT[:, s, 0:S + SC]).then_inc(g["sc_done"], 1)
                if k == TURN_COMB:
                    pe.wait_ge(g["comb_ready"], count(i, 1, 0))
                    for j in range(NT):
                        last = nc.tensor.transpose(ps1[0:EXPERTS, MISC, tok(j)], comb[:, j, :], ident[:])
                    last.then_inc(g["combT_done"], 1)
                if k in plan.up:
                    e = plan.up.index(k)
                    for c in range(EC):
                        n = EC * e + c
                        if n >= 2:
                            pe.wait_ge(g["relu_done"], count(i, EXPERTS * EC, n - 2))
                        else:
                            pe.wait_ge(g["raw_ready"], count(i, NT, 2 + n))
                        for l in range(DEPTH):
                            if after is not None and c < 2 and plan.up[e] > BLOCK[l] + 1 and (e == 0 or plan.up[e - 1] <= BLOCK[l] + 1):
                                pe.wait_ge(g["v_ready"], count(after, 8, 4 * l + 2 + c))
                        mm(ps1[:, c % 2, :], m_w1[:, e, c * P:(c + 1) * P], yT[:].rearrange("p s n -> p (s n)")
                           ).then_inc(g["h_done"], 1)
                if k in plan.down:
                    e = plan.down.index(k)
                    pe.wait_ge(g["relu_done"], count(i, EXPERTS * EC, EC * e + EC - 1))
                    if e >= 1:
                        pe.wait_ge(g["acc_done"], count(i, EXPERTS, e - 1))
                    for j in range(NT):
                        for c in range(EC):
                            last = mm(ps1[:, MOE_OUT, tok(j)], hbuf[:, c, tok(j)], m_w2[:, e, c, :], start=(c == 0), stop=(c == EC - 1))
                    last.then_inc(g["eo_done"], 1)
                if k == EXPERT_BIAS:
                    pe.wait_ge(g["combT_ready"], count(i, 1, 0))
                    for j in range(NT):
                        last = mm(ps1[:, MISC, tok(j)], combT[:, tok(j)], m_b2[:])
                    last.then_inc(g["b2_done"], 1)
                if k in plan.p_turn:
                    j = plan.p_turn.index(k)
                    pe.wait_ge(g["pw_ready"], count(i, NT, j))
                    if j == 1 or j == 3:
                        pe.wait_ge(g["pwT_ready"], count(i, NT, j - 1))
                    if j == 2:
                        pe.wait_ge(g["half_ready"], count(i, 1, 0))
                    for a in range(2):
                        last = nc.tensor.transpose(ps1[:, MISC, a * P:(a + 1) * P], wrk[:, j, a * P:(a + 1) * P], ident[:])
                    last.then_inc(g["pwT_done"], 1)
                if k in plan.attend:
                    s = plan.attend.index(k)
                    pe.wait_ge(g["pwT_ready"], count(i, NT, 2 * s + 1))
                    for a in range(2):
                        last = mm(ps1[:, MISC, 0:S], a_v[:, s, a, :], a_pT[:, s, a, :], start=(a == 0), stop=(a == 1))
                    last.then_inc(g["at_done"], 1)
                    pe.wait_ge(g["at_ready"], count(i, 2, s))
                    for t in tiles:
                        last = mm(ps1[:, MISC, tok(t)], a_oT[:, s, tok(t)], a_wo[:])
                    last.then_inc(g["wo_done"], 1)

            pipeline(pe, first, second)


def shape_constants():
    import numpy as np
    f = np.float32
    half = np.arange(0, DIM_HEAD, 2, dtype=f)
    inv = (f(1.0) / f(10000.0) ** (half / f(DIM_HEAD))).astype(f)
    t = np.arange(S, dtype=f)
    fr = (t[:, None] * inv[None, :]).astype(f)
    fr = np.concatenate([fr, fr], -1)
    base = ((half + f(0.4 * DIM_HEAD)) / f(1.4 * DIM_HEAD)).astype(f)
    power = ((t - S // 2) / f(WINDOW // 2)).astype(f)
    sc = (base[None, :] ** power[:, None]).astype(f)
    sc = np.concatenate([sc, sc], -1)
    cos, sin = np.cos(fr).astype(f), np.sin(fr).astype(f)
    sgn = np.concatenate([-np.ones(DIM_HEAD // 2, f), np.ones(DIM_HEAD // 2, f)])
    rot_cos = np.stack([cos * sc, cos / sc], 1).astype(f)
    rot_sin = np.stack([sin * sc * sgn, sin / sc * sgn], 1).astype(f)
    q, c = np.arange(P)[:, None], np.arange(P)[None, :]
    ok0 = (c <= q) & (c >= q - WINDOW)
    qi, ci = q % WINDOW, c % WINDOW
    own = (q // WINDOW == 0) == (c // WINDOW == 0)
    ok1 = np.where(own, ci <= qi, ci >= qi)
    band = np.where(np.stack([ok0, ok1]), f(0), f(-1e30)).astype(f)
    causal = np.where(c <= q, f(0), f(-BIG)).astype(f)
    return {"ident": np.eye(P, dtype=f), "band": band, "causal": causal, "rot_cos": rot_cos, "rot_sin": rot_sin,
            "iota8": np.arange(EXPERTS, dtype=f)}


def kernel(**inputs):
    import numpy as np
    import concourse.bacc as bacc
    from concourse import mybir
    from concourse.bass_utils import run_bass_kernel_spmd as run

    a = {k: np.asarray(v) for k, v in inputs.items()}
    w = shape_constants()
    w["fw_q"] = a["L0_attn_qkv_w"][0:D].T
    w["q_norm_w"] = a["L0_attn_q_norm_w"]
    for n in ("w0", "w1", "w2"):
        w["fw_" + n] = a["L0_attn_" + n].transpose(0, 2, 1)
    for n in ("wqkv", "q_scale", "k_scale", "wo", "w1", "w2"):
        w[n] = a["L0_ffn_" + n]
    for n in ("Wq", "Wk", "Wv", "Wo", "bv", "bo"):
        w["a_" + n.lower()] = a["L1_attn_" + n]
    w["m_gate"] = a["L1_ffn_gate_w"].T
    w["m_w1"] = a["L1_ffn_w1"].transpose(2, 0, 1)
    w["m_w2"] = a["L1_ffn_w2"].reshape(EXPERTS, D, EC, P).transpose(3, 0, 2, 1)
    b1, columns = a["L0_ffn_b1"], np.zeros((P, 52), np.float32)
    for l in range(DEPTH):
        for c, (o, n) in enumerate(CH):
            columns[0:n, 3 * l + c] = b1[l, o:o + n]
            columns[0:n, 6 + 3 * l + c] = b1[l, HID + o:HID + o + n]
        columns[:, 12 + l], columns[:, 14 + l], columns[:, 16 + l] = (
            a["L0_ffn_b2"][l], a["L0_ffn_ln_g"][l], a["L0_ffn_ln_b"][l])
    columns[:, 18], columns[:, 19] = a["L1_attn_bq"], a["L1_attn_bk"]
    columns[:, 20:52] = a["L1_ffn_b1"].reshape(EXPERTS * EC, P).T
    w["cols"] = columns
    w["m_b2"] = a["L1_ffn_b2"]
    x = np.ascontiguousarray(a["L0_attn_hidden_states"])

    nc = bacc.Bacc("TRN2", target_bir_lowering=False, num_devices=1)
    arrays, aps = {"x": x}, {}
    for name, value in w.items():
        arrays["in_" + name] = np.ascontiguousarray(value)
        aps[name] = nc.dram_tensor("in_" + name, value.shape, mybir.dt.from_np(value.dtype), kind="ExternalInput").ap()
    x_d = nc.dram_tensor("x", x.shape, mybir.dt.float32, kind="ExternalInput").ap()
    out_d = nc.dram_tensor("out", x.shape, mybir.dt.float32, kind="ExternalOutput").ap()
    build(nc, x_d, out_d, aps)
    r = run(nc, [arrays], core_ids=[0])
    return r.results[0]["out"]
```

```python
import math
from contextlib import ExitStack

import concourse.bass as bass
from concourse import mybir

F32 = mybir.dt.float32
BF16 = mybir.dt.bfloat16
U32 = mybir.dt.uint32
ALU = mybir.AluOpType
ACT = mybir.ActivationFunctionType
AX_X = mybir.AxisListType.X

P = 128
B, S, D = 16, 256, 128
TILES = S // P
SLOTS = 2
PAIRS = B // SLOTS
NT = SLOTS * TILES
NH, DH, DHID = 4, 32, 64
DEPTH, HEADS, DIM_HEAD, WINDOW = 2, 8, 64, 64
INNER = HEADS * DIM_HEAD
HID = int(D * 4 * 2 / 3)
CH = [(c * P, min(P, HID - c * P)) for c in range((HID + P - 1) // P)]
EXPERTS, HIDDEN = 8, 512
EC = HIDDEN // P
COMP, TOP_K = 4, 64
SC = S // COMP
BIG = 3.0e38
DVE_LINKS = (84, 89)
POOL_LINKS = (4, 8)
ACT_LINKS = 15

HEAD_STEPS, LAYER_STEPS = 7, 15
BLOCK = [HEAD_STEPS + LAYER_STEPS * l for l in range(DEPTH)]
STEPS = HEAD_STEPS + LAYER_STEPS * DEPTH + 1
TURN_Y, PROJECT, SCORES, TURN_COMB, EXPERT_BIAS = 1, 2, 3, 5, 6


class Plan:

    def __init__(self, up, down, top, attend, steps):
        self.up, self.down = up, down
        self.add = down[1::2]
        self.top = top
        self.top_done = top[3::4]
        self.softmax = [k + 1 for k in self.top_done]
        self.combine = [k + 2 for k in self.top_done]
        self.p_turn = [k + 3 for k in self.top_done]
        self.attend = attend
        self.add_attention = [k + 1 for k in attend]
        self.steps = steps


L, M = BLOCK
WOVEN = Plan(up=[4, 4, 7, 8, 12, 12, 14, 15, 19, 19, 22, 23, 27, 28, 34, 34], down=[6, 6, 9, 9, 13, 13, 18, 18, 21, 21, 24, 24, 33, 33, 35, 37], top=[4, 5, 9, 12, 14, 15, 16, 17, 19, 20, 24, 27, 28, 30, 31, 32], attend=[21, 36], steps=STEPS)
ALONE = Plan(up=[4 + 3 * (n // 2) for n in range(2 * EXPERTS)], down=[6 + 3 * (n // 2) for n in range(2 * EXPERTS)], top=list(range(4, 20)),
             attend=[15, 26], steps=28)
LN_EXP = "natural_log_exp_and_others"
LN_SCALE = 2.0 ** 16


def count(i, per_pair, k):
    return (i - 1) * per_pair + k + 1


def build(nc, x_d, out_d, w):
    ctx = ExitStack()
    with ctx:
        def sb(name, shape, dt=F32):
            return ctx.enter_context(nc.sbuf_tensor(name, shape, dt))

        def sem(name):
            return ctx.enter_context(nc.semaphore(name))

        ident = sb("ident", [P, P])
        identb = sb("identb", [P, P], BF16)
        bandb = sb("bandb", [P, TILES, P], BF16)
        causal = sb("causal", [P, P])
        tab_cos = sb("tab_cos", [P, DEPTH, TILES, 2, DIM_HEAD])
        tab_sin = sb("tab_sin", [P, DEPTH, TILES, 2, DIM_HEAD])
        iota8 = sb("iota8", [P, EXPERTS])
        third = sb("third", [P, 3])
        fw_q = sb("fw_q", [P, P])
        fw_gate = sb("fw_gate", [P, P])
        fw_up = sb("fw_up", [P, P])
        fw_down = sb("fw_down", [P, 2, 2 * DH])
        q_norm = sb("q_norm", [P, P])
        wqkv = sb("wqkv", [P, DEPTH, 3 * INNER])
        wo = sb("wo", [P, DEPTH, INNER // P, P])
        w1 = sb("w1", [P, DEPTH, 2 * HID])
        w2 = sb("w2", [P, DEPTH, len(CH), P])
        a_wq = sb("a_wq", [P, P])
        a_wk = sb("a_wk", [P, P])
        a_wv = sb("a_wv", [P, P])
        a_wo = sb("a_wo", [P, P])
        a_bqs = sb("a_bqs", [P, 1])
        a_bv = sb("a_bv", [P, P])
        a_bo = sb("a_bo", [P, P])
        m_gate = sb("m_gate", [P, EXPERTS])
        m_w1 = sb("m_w1", [P, EXPERTS, HIDDEN])
        m_w2 = sb("m_w2", [P, EXPERTS, EC, P])
        m_b2 = sb("m_b2", [EXPERTS, P])
        cols = sb("cols", [P, 2 * DEPTH * len(CH) + 3 * DEPTH + 2 + EXPERTS * EC])
        b1a = cols[:, 0:6].rearrange("p (l c) -> p l c", l=DEPTH)
        b1g = cols[:, 6:12].rearrange("p (l c) -> p l c", l=DEPTH)
        b2, ln_g, ln_b = cols[:, 12:14], cols[:, 14:16], cols[:, 16:18]
        a_bq, a_bk = cols[:, 18:19], cols[:, 19:20]
        m_b1 = cols[:, 20:52].rearrange("p (e c) -> p e c", e=EXPERTS)

        x0 = sb("x0", [P, NT, P])
        stats = sb("stats", [P, NT, 6])
        meanvar = sb("meanvar", [P, NT, 2])
        rstd = sb("rstd", [P, NT])
        vareps = sb("vareps", [P, NT])
        newt = sb("newt", [P, NT, 16])
        ln_root = sb("ln_root", [P, 1])
        fw_n = sb("fw_n", [P, NT + NT * NH])
        fw_r = sb("fw_r", [P, NT + NT * NH])
        fw_t = sb("fw_t", [P, NT + NT * NH])
        qk_n = sb("qk_n", [P, NT, 16])
        xn = sb("xn", [P, NT, P])
        xT = sb("xT", [P, SLOTS, S])
        x1T = sb("x1T", [P, SLOTS, S])
        hT = sb("hT", [P, SLOTS, S + 1])
        res = sb("res", [P, NT, P])
        ms0 = sb("ms0", [P, NT])
        hs0 = sb("hs0", [P, NT, NH])
        hr0 = sb("hr0", [P, NT, NH])
        bufA = sb("bufA", [P, NT, 16, DIM_HEAD])
        bufB = sb("bufB", [P, NT, 16, DIM_HEAD])
        bufC = sb("bufC", [P, NT, 16, DIM_HEAD])
        ssq = sb("ssq", [P, NT, 16])
        q_factor = sb("q_factor", [P, NT, HEADS])
        qkT = sb("qkT", [P, SLOTS, 8, S])
        v = sb("v", [P, SLOTS, TILES, INNER])
        hnT = sb("hnT", [P, SLOTS, S])
        ge = sb("ge", [P, SLOTS, len(CH), S])

        fw = bufC[:].rearrange("p n a b -> p (n a b)")
        q0 = fw[:, 0:NT * P].rearrange("p (n d) -> p n d", n=NT)
        q0s = fw[:, NT * P:2 * NT * P].rearrange("p (n d) -> p n d", n=NT)
        q0T = fw[:, 2 * NT * P:3 * NT * P].rearrange("p (s n) -> p s n", s=SLOTS)
        th = fw[:, 3 * NT * P:5 * NT * P].rearrange("p (s a n) -> p s a n", s=SLOTS, a=2)
        tmp = bufB[:].rearrange("p n a b -> p (n a b)")
        band = tmp[:, 0:256].rearrange("p (t n) -> p t n", t=TILES)
        rot_cos = tmp[:, 256:512].rearrange("p (t a n) -> p t a n", t=TILES, a=2)
        rot_sin = tmp[:, 512:768].rearrange("p (t a n) -> p t a n", t=TILES, a=2)
        qk_scale = tmp[:, 768:1024].rearrange("p (l a n) -> p l a n", l=DEPTH, a=2)
        oT = bufA[:].rearrange("p (s t) a b -> p s (t a b)", s=SLOTS)[:, :, 0:4 * S].rearrange("p s (k n) -> p s k n", k=4)
        vmix = ge[:].rearrange("p s c n -> p s (c n)")[:, :, 0:INNER]

        x1 = sb("x1", [P, NT, P])
        yn = sb("yn", [P, NT, P])
        y_out = sb("y_out", [P, NT, P])
        yT = sb("yT", [P, SLOTS, S])
        g_l = sb("g_l", [P, NT, EXPERTS])
        g_m = sb("g_m", [P, NT, EXPERTS])
        g_i = sb("g_i", [P, NT, EXPERTS], U32)
        g_f = sb("g_f", [P, NT, EXPERTS])
        g_e = sb("g_e", [P, NT, EXPERTS])
        g_s = sb("g_s", [P, NT])
        comb = sb("comb", [P, NT, EXPERTS])
        combT = sb("combT", [EXPERTS, NT * P])
        top8 = sb("top8", [P, NT, 8])
        nmax = sb("nmax", [P, NT, 3])
        lsum = sb("lsum", [P, NT, 3])
        kcs = sb("kcs", [P, SLOTS, SC])
        raw = sb("raw", [P, NT, S + SC])
        wrk = sb("wrk", [P, NT, S])
        csc = sb("csc", [P, NT, S])
        a_qT = sb("a_qT", [P, SLOTS, S])
        a_kT = sb("a_kT", [P, SLOTS, S + SC])
        a_v = sb("a_v", [P, SLOTS, TILES, P])
        a_pT = sb("a_pT", [P, SLOTS, TILES, S])
        a_oT = sb("a_oT", [P, SLOTS, S])
        hbuf = sb("hbuf", [P, EC, NT * P])

        ps0 = ctx.enter_context(nc.psum_tensor("ps0", [P, 4, 512], F32))
        ps1 = ctx.enter_context(nc.psum_tensor("ps1", [P, 4, 512], F32))
        MOE_OUT, MISC = 2, 3

        loaded = [sem("tables_loaded"), sem("first_loaded"), sem("second_loaded")]
        x_loaded = sem("x_loaded")
        x_used = sem("x_used")
        stored = sem("stored")
        consts = sem("consts_ready")
        prep_a = sem("dve_prep")
        dlink = [sem("dve_link_first"), sem("dve_link_second")]
        plink = [sem("pool_link_first"), sem("pool_link_second")]
        alink = sem("act_link")
        start_link = sem("dve_link_start")
        act_start_link = sem("act_link_start")
        names = """xn_ready xnT_done xT_ready q0_done q0_sq qn0_ready qT0_done qT0_ready gu_done th_ready hid_ready o0_done
        qk_done qk_sq qc_ready qn_ready u_ready r_ready s_ready s1_ready vmix_ready qkT_done qkT_ready v_done v_ready sim_done max_ready p_ready rl_ready pn_ready pn1_ready x1b_ready
        pT_done pT_ready oT_done oT_ready x1T_done h2_ready h2tok_done hn_ready hnT_done hnT_ready gate_done w1_done gelu_ready
        u2_ready x2T_done h1_ready x2T_ready x2_done x1_ready y_ready yTp_done yT_ready proj_done qk1_ready kc_ready logit_ready
        e_ready comb_ready combT_done combT_ready b2_done acc0_ready sc_done raw_ready top_ready cm_ready cmax_ready
        sp_ready ex_ready pw_ready pwT_done pwT_ready at_done at_ready wo_done out_ready h_done relu_done eo_done
        acc_done half_ready var_ready rstd_ready fwn_ready fwr_ready qkn_ready qkr_ready""".split()
        g = {n: sem(n) for n in names}

        block = ctx.enter_context(nc.Block())
        n_load = [0, 0, 0]

        @block.sync
        def _(sp):
            def load(dst, src, part=0):
                n_load[part] += 1
                sp.dma_start(dst, src).then_inc(loaded[part], 16)

            xv = x_d.rearrange("b (t p) d -> p (b t) d", p=P)
            ov = out_d.rearrange("b (t p) d -> p (b t) d", p=P)
            sp.dma_start(x0[:], xv[:, 0:NT, :]).then_inc(x_loaded, 16)
            sp.wait_ge(consts, 1)
            load(ident[:], w["ident"])
            load(band, w["band"].rearrange("t p n -> p t n"))
            load(causal[:], w["causal"])
            load(rot_cos, w["rot_cos"].rearrange("(t p) a n -> p t a n", p=P))
            load(rot_sin, w["rot_sin"].rearrange("(t p) a n -> p t a n", p=P))
            load(qk_scale[:, :, 0, :], w["q_scale"].partition_broadcast(P))
            load(qk_scale[:, :, 1, :], w["k_scale"].partition_broadcast(P))
            load(iota8[:], w["iota8"].partition_broadcast(P))
            load(fw_q[:], w["fw_q"])
            load(q_norm[:], w["q_norm_w"].partition_broadcast(P))
            for h in range(NH):
                a, o = DH * h, DHID * (h % 2)
                load(fw_gate[a:a + DH, o:o + DHID], w["fw_w0"][h])
                load(fw_up[a:a + DH, o:o + DHID], w["fw_w2"][h])
                load(fw_down[o:o + DHID, h // 2, DH * (h % 2):DH * (h % 2 + 1)], w["fw_w1"][h])
            load(cols[:], w["cols"])
            for l in range(DEPTH):
                load(wqkv[:, l], w["wqkv"][l], 1)
            load(wo[:], w["wo"].rearrange("l (j p) n -> p l j n", p=P), 1)
            load(w1[:], w["w1"].rearrange("l p n -> p l n"), 1)
            for c, (o, n) in enumerate(CH):
                load(w2[0:n, :, c, :], w["w2"][:, o:o + n, :].rearrange("l p n -> p l n"), 1)
            for t, n in ((a_wq, "a_wq"), (a_wk, "a_wk"), (a_wv, "a_wv"), (a_wo, "a_wo"), (m_gate, "m_gate"),
                         (m_b2, "m_b2")):
                load(t[:], w[n], 2)
            load(a_bv[:], w["a_bv"].partition_broadcast(P), 2)
            load(a_bo[:], w["a_bo"].partition_broadcast(P), 2)
            load(m_w1[:], w["m_w1"], 2)
            load(m_w2[:], w["m_w2"], 2)
            sp.sem_inc(stored, 16)
            sp.wait_ge(x_used, count(1, SLOTS, SLOTS - 1))
            sp.dma_start(x0[:], xv[:, NT:2 * NT, :]).then_inc(x_loaded, 16)
            with sp.Fori(1, PAIRS - 1) as i:
                sp.wait_ge(x_used, count(i + 1, SLOTS, SLOTS - 1))
                sp.dma_start(x0[:], xv[:, bass.ds((i + 1) * NT, NT), :]).then_inc(x_loaded, 16)
                sp.wait_ge(g["out_ready"], count(i, 1, 0))
                sp.dma_start(ov[:, bass.ds((i - 1) * NT, NT), :], y_out[:]).then_inc(stored, 16)
            sp.wait_ge(x_used, count(PAIRS, SLOTS, SLOTS - 1))
            sp.dma_start(x0[:], xv[:, 0:NT, :]).then_inc(x_loaded, 16)
            for k in (PAIRS - 1, PAIRS):
                sp.wait_ge(g["out_ready"], k)
                sp.dma_start(ov[:, (k - 1) * NT:k * NT, :], y_out[:]).then_inc(stored, 16)
            sp.wait_ge(stored, 16 * (PAIRS + 1))

        slots = range(SLOTS)
        tiles = range(TILES)
        units = [(s, t) for s in slots for t in tiles]

        def tok(t):
            return slice(t * P, (t + 1) * P)

        weight_readers = (nc.tensor, nc.vector)

        def chunks(plan, k):
            return [(m // 2, 2 * (m % 2) + c) for m, at in enumerate(plan.up) if at == k for c in range(2)]

        def pipeline(eng, first, second):
            first(1, lambda k: None, None)
            if eng in weight_readers:
                eng.wait_ge(loaded[2], 16 * n_load[2])
            with eng.Fori(1, PAIRS) as i:
                first(i + 1, lambda k: second(i, k, i + 1), i)
            for k in range(ALONE.steps):
                second(PAIRS, k, None)

        @block.gpsimd
        def _(pool):
            def chain(part, per_pair):
                n = 0

                def link(i, ins):
                    nonlocal n
                    ins.then_inc(plink[part], 1)
                    pool.wait_ge(plink[part], count(i, per_pair, n % per_pair))
                    n += 1
                return link

            link0, link1 = chain(0, POOL_LINKS[0]), chain(1, POOL_LINKS[1])

            def first(i, side, before):
                for k in range(HEAD_STEPS):
                    side(k)
                for l in range(DEPTH):
                    step = BLOCK[l]
                    for j, (s, t) in enumerate(units):
                        for part in range(2):
                            if part == 0 and t == 0:
                                pool.wait_ge(g["qc_ready"], count(i, 4, 2 * l + s))
                                pool.wait_ge(g["qkn_ready"], count(i, 8, 4 * l + j))
                            else:
                                pool.wait_ge(g["qn_ready"], count(i, 8, 4 * l + j))
                            hs = slice(HEADS * part, HEADS * (part + 1))
                            for h in range(2):
                                tab = tab_sin[:, l, t, part, 32 * h:32 * h + 32].unsqueeze(1).to_broadcast([P, HEADS, 32])
                                last = nc.gpsimd.tensor_tensor(bufA[:, j, hs, 32 * h:32 * h + 32],
                                                               bufB[:, j, hs, 32 * (1 - h):32 * (2 - h)], tab, ALU.mult)
                        last.then_inc(g["r_ready"], 1)
                        if t == 0:
                            pool.wait_ge(g["r_ready"], count(i, 8, 4 * l + j))
                            pool.wait_ge(g["u_ready"], count(i, 8, 4 * l + j))
                            nc.gpsimd.tensor_tensor(bufC[:, j], bufC[:, j], bufA[:, j], ALU.add).then_inc(g["s_ready"], 1)
                    pool.wait_ge(g["r_ready"], count(i, 8, 4 * l + 3))
                    for s in slots:
                        pool.wait_ge(g["v_ready"], count(i, 8, 4 * l + 2 * s + 1))
                        pool.nop(nofuse=True)
                        link0(i, nc.gpsimd.tensor_copy(vmix[0:64, s, :], v[0:64, s, 1, :]))
                        pool.nop(nofuse=True)
                        nc.gpsimd.tensor_copy(vmix[64:128, s, :], v[64:128, s, 0, :]).then_inc(g["vmix_ready"], 1)
                        pool.wait_ge(g["vmix_ready"], count(i, 4, 2 * l + s))
                    for k in range(6):
                        side(step + k)
                    for j in (0, 2):
                        pool.wait_ge(g["rl_ready"], count(i, 8, 4 * l + j))
                        pv = bufB[:, j].rearrange("p a b -> p (a b)").rearrange("p (h n) -> p h n", h=HEADS)
                        nc.gpsimd.tensor_tensor(pv, pv, ssq[:, j, 0:8].unsqueeze(2).to_broadcast([P, HEADS, P]),
                                                ALU.mult).then_inc(g["pn_ready"], 1)
                    for k in range(6, LAYER_STEPS):
                        side(step + k)
                side(STEPS - 1)

            def second(i, k, after):
                plan = ALONE if after is None else WOVEN
                if k == SCORES:
                    for j, (s, t) in enumerate(units):
                        pool.wait_ge(g["raw_ready"], count(i, NT, j))
                        pool.nop(nofuse=True)
                        if t == 1:
                            nc.gpsimd.tensor_copy(csc[:, j, 0:P], raw[:, j, 0:P])
                        nc.gpsimd.tensor_tensor(csc[:, j, tok(t)], raw[:, j, tok(t)], causal[:], ALU.add).then_inc(g["cm_ready"], 1)
                if k in plan.top_done:
                    j = plan.top_done.index(k)
                    pool.wait_ge(g["top_ready"], count(i, NT, j))
                    link1(i, nc.gpsimd.tensor_tensor(wrk[:, j], wrk[:, j], raw[:, j, 0:S], ALU.subtract))
                    pool.nop(nofuse=True)
                    link1(i, nc.gpsimd.tensor_scalar(wrk[:, j], wrk[:, j], 0.0, None, ALU.is_lt))
                    nc.gpsimd.tensor_tensor(wrk[:, j], wrk[:, j], raw[:, j, 0:S], ALU.mult).then_inc(g["sp_ready"], 1)

            pipeline(pool, first, second)

        @block.scalar
        def _(act):
            nc.scalar.preload_act_table_set(LN_EXP)
            n_link = 0

            def rsqrt(i, out, x, scale, bias, ready):
                nonlocal n_link
                nc.scalar.activation(out, x, ACT.Ln, scale=scale).then_inc(alink, 1)
                act.wait_ge(alink, count(i, ACT_LINKS, n_link % ACT_LINKS))
                n_link += 1
                nc.scalar.activation(out, out, ACT.Exp, scale=-0.5, bias=bias).then_inc(ready, 1)

            def ln_root_of(i, k, js):
                act.wait_ge(g["var_ready"], count(i, 6, k))
                rsqrt(i, rstd[:, js], vareps[:, js], 1.0, 0.0, g["rstd_ready"])

            act.wait_ge(g["var_ready"], 1)
            nc.scalar.activation(rstd[:], vareps[:], ACT.Ln).then_inc(act_start_link, 1)
            act.wait_ge(act_start_link, 1)
            nc.scalar.activation(rstd[:], rstd[:], ACT.Exp, scale=-0.5).then_inc(g["rstd_ready"], 1)
            act.wait_ge(prep_a, 3)

            def first(i, side, before):
                for s in slots:
                    act.wait_ge(g["xnT_done"], count(i, 2, s))
                    nc.scalar.copy(xT[:, s, :], ps0[:, 2 * s, 0:S]).then_inc(g["xT_ready"], 1)
                for s in slots:
                    nc.scalar.copy(hT[0:64, s, 0:S], ps0[0:64, 2 * s, 0:S])
                    nc.scalar.copy(hT[64:128, s, 1:S + 1], ps0[64:128, 2 * s, 0:S])
                for s in slots:
                    act.wait_ge(g["q0_done"], count(i, 2, s))
                    for t in tiles:
                        last = nc.scalar.activation(q0s[:, 2 * s + t], ps0[:, 2 * s + 1, tok(t)], ACT.Square,
                                                    scale=float(D) ** -0.5, accum_out=ms0[:, 2 * s + t:2 * s + t + 1])
                    last.then_inc(g["q0_sq"], 1)
                side(0)
                side(1)
                act.wait_ge(g["fwn_ready"], count(i, 1, 0))
                rsqrt(i, fw_r[:], fw_n[:], LN_SCALE, ln_root[:], g["fwr_ready"])
                for s in slots:
                    act.wait_ge(g["qT0_done"], count(i, 2, s))
                    nc.scalar.copy(q0T[:, s, :], ps0[:, 2 * s, 0:S]).then_inc(g["qT0_ready"], 1)
                side(2)
                for s in slots:
                    act.wait_ge(g["gu_done"], count(i, 2, s))
                    for p in range(2):
                        last = nc.scalar.activation(th[:, s, p, :], ps0[:, 2 * s + p, 0:S], ACT.Tanh, scale=0.5)
                    last.then_inc(g["th_ready"], 1)
                nc.scalar.preload_act_table_set(LN_EXP)
                for k in range(3, HEAD_STEPS):
                    side(k)
                for l in range(DEPTH):
                    step = BLOCK[l]

                    def square(j):
                        t = j % 2
                        act.wait_ge(g["qk_done"], count(i, 8, 4 * l + j))
                        nc.scalar.activation(bufA[:, j].rearrange("p (a h) n -> p a (h n)", a=2),
                                             ps0[:, 2 * t:2 * t + 2, :], ACT.Square).then_inc(g["qk_sq"], 1)
                        if t == 0:
                            nc.scalar.copy(bufB[:, j, 0:HEADS].rearrange("p h n -> p (h n)"), ps0[:, 2 * t, :]).then_inc(g["qc_ready"], 1)

                    def root(j):
                        act.wait_ge(g["qkn_ready"], count(i, 8, 4 * l + j))
                        rsqrt(i, ssq[:, j], qk_n[:, j], LN_SCALE, ln_root[:], g["qkr_ready"])

                    def values(s):
                        for t in tiles:
                            act.wait_ge(g["v_done"], count(i, 8, 4 * l + 2 * s + t))
                            nc.scalar.copy(v[:, s, t, :], ps1[:, t, :]).then_inc(g["v_ready"], 1)

                    def turned(j):
                        s, t = units[j]
                        act.wait_ge(g["qkT_done"], count(i, 8, 4 * l + j))
                        nc.scalar.copy(qkT[:, s, :, tok(t)], ps0[:, 2 * t:2 * t + 2, :].rearrange("p a (b n) -> p (a b) n", n=P)
                                       ).then_inc(g["qkT_ready"], 1)

                    def turned_p(j):
                        t = j % 2
                        act.wait_ge(g["pT_done"], count(i, 8, 4 * l + j))
                        nc.scalar.copy(bufC[:, j].rearrange("p (a h) n -> p a (h n)", a=2), ps0[:, 2 * t:2 * t + 2, :]
                                       ).then_inc(g["pT_ready"], 1)

                    square(0)
                    root(0)
                    square(1)
                    side(step)
                    root(1)
                    square(2)
                    side(step + 1)
                    values(0)
                    root(2)
                    square(3)
                    values(1)
                    root(3)
                    side(step + 2)
                    turned(0)
                    side(step + 3)
                    turned(1)
                    side(step + 4)
                    turned(2)
                    turned(3)
                    for j, (s, t) in enumerate(units):
                        act.wait_ge(g["max_ready"], count(i, 8, 4 * l + j))
                        if t == 1:
                            last = nc.scalar.activation(bufB[:, j], bufA[:, j], ACT.Exp, scale=8.0)
                        else:
                            for h in range(HEADS):
                                last = nc.scalar.activation(
                                    bufB[:, j].rearrange("p a b -> p (a b)")[:, h * P:(h + 1) * P],
                                    ps0[:, 2 * t + h // 4, P * (h % 4):P * (h % 4) + P], ACT.Exp, scale=q_factor[:, j, h // 4 + 2 * (h % 4):h // 4 + 2 * (h % 4) + 1],
                                    bias=ssq[:, j, 8 + h:9 + h], accum_out=ssq[:, j, h:h + 1])
                        last.then_inc(g["p_ready"], 1)
                        if j == 0:
                            side(step + 5)
                    side(step + 6)
                    turned_p(0)
                    turned_p(1)
                    side(step + 7)
                    turned_p(2)
                    turned_p(3)
                    side(step + 8)
                    for j, (s, t) in enumerate(units):
                        act.wait_ge(g["oT_done"], count(i, 8, 4 * l + j))
                        nc.scalar.copy(oT[:, s, :, tok(t)], ps0[:, 2 * t + s, :].rearrange("p (b n) -> p b n", n=P)
                                       ).then_inc(g["oT_ready"], 1)
                    side(step + 9)
                    side(step + 10)
                    for s in slots:
                        ln_root_of(i, 1 + 2 * l + s, slice(2 * s, 2 * s + 2))
                    side(step + 11)
                    for s in slots:
                        act.wait_ge(g["hnT_done"], count(i, 4, 2 * l + s))
                        nc.scalar.activation(hnT[:, s, :], ps0[:, s, 0:S], ACT.Identity, bias=ln_b[:, l:l + 1],
                                             scale=ln_g[:, l:l + 1]).then_inc(g["hnT_ready"], 1)
                    if l == DEPTH - 1:
                        ln_root_of(i, 5, slice(0, NT))
                    for s in slots:
                        act.wait_ge(g["gate_done"], count(i, 4, 2 * l + s))
                        for c, (o, n) in enumerate(CH):
                            if c == 2:
                                act.wait_ge(g["w1_done"], count(i, 4, 2 * l + s))
                            src = ps0[0:n, s, c * S:(c + 1) * S] if c < 2 else ps0[0:n, 2, 0:S]
                            last = nc.scalar.activation(ge[0:n, s, c, :], src, ACT.Gelu, bias=b1g[0:n, l, c:c + 1])
                        last.then_inc(g["gelu_ready"], 1)
                        if s == 0:
                            side(step + 12)
                    nc.scalar.preload_act_table_set(LN_EXP)
                    side(step + 13)
                    side(step + 14)
                ln_root_of(i, 6, slice(0, NT))
                side(STEPS - 1)

            def second(i, k, after):
                plan = ALONE if after is None else WOVEN
                if k == TURN_Y:
                    act.wait_ge(g["yTp_done"], count(i, 1, 0))
                    nc.scalar.copy(yT[:], ps1[:, MISC, :].rearrange("p (s n) -> p s n", s=SLOTS)).then_inc(g["yT_ready"], 1)
                if k == PROJECT:
                    act.wait_ge(g["proj_done"], count(i, 1, 0))
                    for s in slots:
                        nc.scalar.activation(a_qT[:, s, :], ps1[:, s, 0:S], ACT.Identity, bias=a_bqs[:], scale=float(D) ** -0.5)
                        nc.scalar.activation(a_kT[:, s, 0:S], ps1[:, s, S:2 * S], ACT.Identity, bias=a_bk
                                             ).then_inc(g["qk1_ready"], 1)
                if k == SCORES:
                    act.wait_ge(g["logit_ready"], count(i, 1, 0))
                    nc.scalar.activation(g_e[:], g_l[:], ACT.Exp).then_inc(g["e_ready"], 1)
                    for j in range(NT):
                        act.wait_ge(g["sc_done"], count(i, NT, j))
                        nc.scalar.copy(raw[:, j, :], ps1[:, j % 2, 0:S + SC]).then_inc(g["raw_ready"], 1)
                if k == TURN_COMB:
                    act.wait_ge(g["combT_done"], count(i, 1, 0))
                    nc.scalar.copy(combT[:], ps1[0:EXPERTS, MISC, :]).then_inc(g["combT_ready"], 1)
                for e, c in chunks(plan, k):
                    if c == 0 and e >= 1:
                        act.wait_ge(g["eo_done"], count(i, EXPERTS, e - 1))
                    act.wait_ge(g["h_done"], count(i, EXPERTS * EC, EC * e + c))
                    nc.scalar.activation(hbuf[:, c, :], ps1[:, c % 2, :], ACT.Relu, bias=m_b1[:, e, c:c + 1]
                                         ).then_inc(g["relu_done"], 1)
                if k in plan.softmax:
                    j = plan.softmax.index(k)
                    act.wait_ge(g["sp_ready"], count(i, NT, j))
                    act.wait_ge(g["cmax_ready"], count(i, NT, j))
                    n = P * (j % 2 + 1)
                    nc.scalar.activation(wrk[:, j], wrk[:, j], ACT.Exp, bias=nmax[:, j, 0:1], accum_out=lsum[:, j, 0:1])
                    nc.scalar.activation(csc[:, j, 0:n], csc[:, j, 0:n], ACT.Exp, bias=nmax[:, j, 1:2], accum_out=lsum[:, j, 1:2])
                    nc.scalar.activation(raw[:, j, S:], raw[:, j, S:], ACT.Exp, bias=nmax[:, j, 2:3], accum_out=lsum[:, j, 2:3]
                                         ).then_inc(g["ex_ready"], 1)
                if k in plan.p_turn:
                    j = plan.p_turn.index(k)
                    act.wait_ge(g["pwT_done"], count(i, NT, j))
                    nc.scalar.copy(a_pT[:, j // 2, :, tok(j % 2)], ps1[:, MISC, 0:S].rearrange("p (a n) -> p a n", n=P)
                                   ).then_inc(g["pwT_ready"], 1)
                if k in plan.attend:
                    s = plan.attend.index(k)
                    act.wait_ge(g["at_done"], count(i, 2, s))
                    nc.scalar.copy(a_oT[:, s, :], ps1[:, MISC, 0:S]).then_inc(g["at_ready"], 1)

            pipeline(act, first, second)

        @block.vector
        def _(dve):
            def vt(out, a, b, op):
                return nc.vector.tensor_tensor(out, a, b, op)

            nc.vector.memset(fw_gate[:], 0.0)
            nc.vector.memset(fw_up[:], 0.0)
            nc.vector.memset(fw_down[:], 0.0)
            nc.vector.memset(hT[64:128, :, 0:1], 0.0)
            nc.vector.memset(ln_root[:], 0.5 * math.log(LN_SCALE))
            nc.vector.memset(third[:, 0:2], 1.0 / 3.0)
            nc.vector.memset(third[:, 2:3], 1.0 / (3.0 * COMP)).then_inc(consts, 1)

            def newton(link, y, x, t):
                link(nc.vector.scalar_tensor_tensor(t, y, -0.5, y, ALU.mult, ALU.mult))
                link(vt(t, t, x, ALU.mult))
                return nc.vector.scalar_tensor_tensor(y, t, 1.5, y, ALU.add, ALU.mult)

            def after_wait(op, *args, **kw):
                dve.nop(nofuse=True)
                return op(*args, **kw)

            def moments(link, js, src):
                for j in js:
                    last = nc.vector.bn_stats(stats[:, j, :], src(j))
                link(last)
                for j in js:
                    last = after_wait(nc.vector.bn_aggr, meanvar[:, j, :], stats[:, j, :])
                link(last)
                nc.vector.tensor_scalar(vareps[:, js[0]:js[-1] + 1], meanvar[:, js[0]:js[-1] + 1, 1], 1e-5, None, ALU.add
                                        ).then_inc(g["var_ready"], 1)

            def normalise(link, js, src, dst, ready):
                r = slice(js[0], js[-1] + 1)
                link(newton(link, rstd[:, r], vareps[:, r], newt[:, r, 0]))
                for j in js:
                    last = nc.vector.tensor_scalar(dst[:, j], src(j), meanvar[:, j, 0:1], rstd[:, j:j + 1],
                                                   ALU.subtract, ALU.mult)
                    if j % TILES == TILES - 1:
                        last.then_inc(ready, 1)

            def start_chain():
                n = 0

                def link(ins):
                    nonlocal n
                    n += 1
                    ins.then_inc(start_link, 1)
                    dve.wait_ge(start_link, n)
                return link

            link_start = start_chain()
            dve.wait_ge(x_loaded, 16)
            moments(link_start, range(NT), lambda j: x0[:, j])
            dve.wait_ge(g["rstd_ready"], 1)
            normalise(link_start, range(NT), lambda j: x0[:, j], xn, g["xn_ready"])

            dve.wait_ge(loaded[0], 16 * n_load[0])
            nc.vector.tensor_copy(identb[:], ident[:])
            nc.vector.tensor_copy(bandb[:], band)
            nc.vector.tensor_scalar_mul(a_bqs[:], a_bq, float(D) ** -0.5).then_inc(prep_a, 1)
            for l in range(DEPTH):
                for t in tiles:
                    vt(tab_cos[:, l, t], rot_cos[:, t], qk_scale[:, l], ALU.mult)
                    for h in range(2):
                        last = vt(tab_sin[:, l, t, :, 32 * h:32 * h + 32], rot_sin[:, t, :, 32 * h:32 * h + 32],
                                  qk_scale[:, l, :, 32 * (1 - h):32 * (2 - h)], ALU.mult)
                last.then_inc(prep_a, 1)
            dve.wait_ge(prep_a, 3)

            def chain(part, per_pair):
                n = 0

                def link(i, ins):
                    nonlocal n
                    ins.then_inc(dlink[part], 1)
                    dve.wait_ge(dlink[part], count(i, per_pair, n % per_pair))
                    n += 1

                def links():
                    return n
                return link, links

            link0, links0 = chain(0, DVE_LINKS[0])
            link1, links1 = chain(1, DVE_LINKS[1])

            def first(i, side, before):
                def link(ins):
                    link0(i, ins)

                side(0)
                side(1)
                for s in slots:
                    dve.wait_ge(g["q0_done"], count(i, 2, s))
                    dve.wait_ge(g["q0_sq"], count(i, 2, s))
                    js = slice(2 * s, 2 * s + 2)
                    last = vt(q0[:, js], ps0[:, 2 * s + 1, 0:S].rearrange("p (t n) -> p t n", t=2),
                              q_norm[:].unsqueeze(1).to_broadcast([P, 2, P]), ALU.mult)
                link(last)
                link(vt(q0s, q0, q0, ALU.mult))
                link(nc.vector.tensor_reduce(hs0[:], q0s.rearrange("p t (h n) -> p t h n", h=NH), AX_X, ALU.add))
                nc.vector.tensor_scalar(fw_n[:, 0:NT], ms0[:], 1e-6, None, ALU.add)
                nc.vector.tensor_scalar(fw_n[:, NT:], hs0[:].rearrange("p t h -> p (t h)"), 1e-24, None, ALU.max
                                        ).then_inc(g["fwn_ready"], 1)
                dve.wait_ge(g["fwr_ready"], count(i, 1, 0))
                dve.wait_ge(g["fwn_ready"], count(i, 1, 0))
                link(newton(link, fw_r[:], fw_n[:], fw_t[:]))
                rrb = fw_r[:, 0:NT].unsqueeze(2).to_broadcast([P, NT, NH])
                link(vt(hs0[:], hs0[:], fw_r[:, NT:].rearrange("p (t h) -> p t h", t=NT), ALU.mult))
                link(vt(hs0[:], hs0[:], rrb, ALU.mult))
                link(nc.vector.tensor_scalar(hs0[:], hs0[:], 1e-5, None, ALU.add))
                link(after_wait(nc.vector.reciprocal, hr0[:], hs0[:]))
                link(vt(hr0[:], hr0[:], rrb, ALU.mult))
                for s in slots:
                    js = slice(2 * s, 2 * s + 2)
                    vt(q0s[:, js].rearrange("p t (h n) -> p (t h) n", h=NH), q0[:, js].rearrange("p t (h n) -> p (t h) n", h=NH),
                       hr0[:, js].rearrange("p t h -> p (t h)").unsqueeze(2).to_broadcast([P, 2 * NH, DH]), ALU.mult
                       ).then_inc(g["qn0_ready"], 1)
                side(2)
                for s in slots:
                    dve.wait_ge(g["th_ready"], count(i, 2, s))
                    for p in range(2):
                        last = nc.vector.scalar_tensor_tensor(th[:, s, p], th[:, s, p], 1.0, ps0[:, 2 * s + p, 0:S], ALU.add, ALU.mult)
                    link(last)
                    for p in range(2):
                        last = nc.vector.scalar_tensor_tensor(th[:, s, p], th[:, s, p], 0.5, ps0[:, 2 * s + p, S:2 * S], ALU.mult, ALU.mult)
                    last.then_inc(g["hid_ready"], 1)
                side(3)
                for s in slots:
                    dve.wait_ge(g["o0_done"], count(i, 2, s))
                    vt(res[:, 2 * s:2 * s + 2], ps0[:, 2 * s + 1, 0:S].rearrange("p (t n) -> p t n", t=2), x0[:, 2 * s:2 * s + 2],
                       ALU.add).then_inc(x_used, 1)
                for k in range(4, HEAD_STEPS):
                    side(k)

                for l in range(DEPTH):
                    step = BLOCK[l]

                    def squared_norms(j):
                        dve.wait_ge(g["qk_sq"], count(i, 8, 4 * l + j))
                        link(nc.vector.tensor_reduce(qk_n[:, j], bufA[:, j], AX_X, ALU.add))
                        nc.vector.tensor_scalar(qk_n[:, j], qk_n[:, j], 1e-24, None, ALU.max).then_inc(g["qkn_ready"], 1)

                    def unit_norms(j):
                        t = j % 2
                        dve.wait_ge(g["qkr_ready"], count(i, 8, 4 * l + j))
                        dve.wait_ge(g["qkn_ready"], count(i, 8, 4 * l + j))
                        link(newton(link, ssq[:, j], qk_n[:, j], newt[:, j]))
                        if t == 1:
                            vt(bufB[:, j], ps0[:, 2:4, :].rearrange("p a (h n) -> p (a h) n", n=DIM_HEAD),
                               ssq[:, j].unsqueeze(2).to_broadcast([P, 16, DIM_HEAD]), ALU.mult).then_inc(g["qn_ready"], 1)
                        else:
                            vt(bufB[:, j, HEADS:], ps0[:, 1, :].rearrange("p (h n) -> p h n", n=DIM_HEAD),
                               ssq[:, j, HEADS:].unsqueeze(2).to_broadcast([P, HEADS, DIM_HEAD]), ALU.mult).then_inc(g["qn_ready"], 1)
                            nc.vector.tensor_scalar_mul(q_factor[:, j], ssq[:, j, 0:HEADS], 8.0)

                    def cos_part(j, part):
                        s, t = units[j]
                        if part == 0 and t == 1:
                            return
                        if part == 0:
                            dve.wait_ge(g["qc_ready"], count(i, 4, 2 * l + s))
                        else:
                            dve.wait_ge(g["qn_ready"], count(i, 8, 4 * l + j))
                        if t == 1:
                            last = vt(bufC[:, j].rearrange("p (a h) n -> p a h n", a=2), bufB[:, j].rearrange("p (a h) n -> p a h n", a=2),
                                      tab_cos[:, l, t].unsqueeze(2).to_broadcast([P, 2, HEADS, DIM_HEAD]), ALU.mult)
                        else:
                            hs = slice(HEADS * part, HEADS * (part + 1))
                            last = vt(bufC[:, j, hs], bufB[:, j, hs],
                                      tab_cos[:, l, t, part].unsqueeze(1).to_broadcast([P, HEADS, DIM_HEAD]), ALU.mult)
                        if part == 1:
                            last.then_inc(g["u_ready"], 1)

                    def rotated(j):
                        dve.wait_ge(g["r_ready"], count(i, 8, 4 * l + j))
                        dve.wait_ge(g["u_ready"], count(i, 8, 4 * l + j))
                        vt(bufC[:, j], bufC[:, j], bufA[:, j], ALU.add).then_inc(g["s1_ready"], 1)

                    squared_norms(0)
                    cos_part(0, 0)
                    unit_norms(0)
                    squared_norms(1)
                    cos_part(0, 1)
                    side(step)
                    cos_part(1, 0)
                    unit_norms(1)
                    squared_norms(2)
                    cos_part(1, 1)
                    side(step + 1)
                    cos_part(2, 0)
                    unit_norms(2)
                    squared_norms(3)
                    cos_part(2, 1)
                    cos_part(3, 0)
                    unit_norms(3)
                    rotated(1)
                    cos_part(3, 1)
                    rotated(3)
                    side(step + 2)
                    side(step + 3)
                    side(step + 4)

                    def row_maxima(j):
                        t = j % 2
                        dve.wait_ge(g["sim_done"], count(i, 8, 4 * l + j))
                        sim = ps0[:, 2 * t:2 * t + 2, :].rearrange("p a (h n) -> p (a h) n", n=P)
                        link(nc.vector.tensor_reduce(ssq[:, j, 8:16], sim, AX_X, ALU.max))
                        if t == 1:
                            vt(bufA[:, j].rearrange("p a b -> p (a b)").rearrange("p (h n) -> p h n", h=HEADS), sim,
                               ssq[:, j, 8:16].unsqueeze(2).to_broadcast([P, HEADS, P]), ALU.subtract).then_inc(g["max_ready"], 1)
                        else:
                            nc.vector.scalar_tensor_tensor(ssq[:, j, 8:16].rearrange("p (h a) -> p h a", h=2),
                                                           ssq[:, j, 8:16].rearrange("p (h a) -> p h a", h=2), -1.0,
                                                           q_factor[:, j].rearrange("p (a h) -> p h a", h=2), ALU.mult, ALU.mult
                                                           ).then_inc(g["max_ready"], 1)

                    def over_sums(j):
                        dve.wait_ge(g["p_ready"], count(i, 8, 4 * l + j))
                        if j % 2 == 1:
                            link(nc.vector.tensor_reduce(ssq[:, j, 0:8], bufB[:, j].rearrange("p a b -> p (a b)").rearrange(
                                "p (h n) -> p h n", h=HEADS), AX_X, ALU.add))
                        after_wait(nc.vector.reciprocal, ssq[:, j, 0:8], ssq[:, j, 0:8]).then_inc(g["rl_ready"], 1)
                        if j % 2 == 1:
                            dve.wait_ge(g["rl_ready"], count(i, 8, 4 * l + j))
                            pv = bufB[:, j].rearrange("p a b -> p (a b)").rearrange("p (h n) -> p h n", h=HEADS)
                            vt(pv, pv, ssq[:, j, 0:8].unsqueeze(2).to_broadcast([P, HEADS, P]), ALU.mult
                               ).then_inc(g["pn1_ready"], 1)

                    row_maxima(0)
                    row_maxima(1)
                    side(step + 5)
                    over_sums(0)
                    row_maxima(2)
                    over_sums(1)
                    row_maxima(3)
                    over_sums(2)
                    over_sums(3)
                    for k in range(6, 10):
                        side(step + k)
                    for s in slots:
                        dve.wait_ge(g["x1T_done"], count(i, 4, 2 * l + s))
                        pr = ps0[:, s, 0:S]
                        vt(hT[0:64, s, 0:S], pr[0:64], xT[0:64, s], ALU.add)
                        vt(hT[64:128, s, 1:S + 1], pr[64:128], xT[64:128, s], ALU.add).then_inc(g["h2_ready"], 1)
                        vt(x1T[:, s], pr, xT[:, s], ALU.add)
                    side(step + 10)
                    for s in slots:
                        dve.wait_ge(g["h2tok_done"], count(i, 4, 2 * l + s))
                        moments(link, range(2 * s, 2 * s + 2), lambda j: ps0[:, 2 + j // 2, tok(j % 2)])
                    for s in slots:
                        dve.wait_ge(g["rstd_ready"], count(i, 6, 1 + 2 * l + s))
                        normalise(link, range(2 * s, 2 * s + 2), lambda j: ps0[:, 2 + j // 2, tok(j % 2)], xn, g["hn_ready"])
                    if l == DEPTH - 1:
                        dve.wait_ge(x_loaded, 16 * (i + 1))
                        dve.wait_ge(g["hn_ready"], count(i, 4, 2 * l + 1))
                        moments(link, range(NT), lambda j: x0[:, j])
                        dve.wait_ge(g["rstd_ready"], count(i, 6, 5))
                        dve.wait_ge(g["hnT_done"], count(i, 4, 2 * l + 1))
                        normalise(link, range(NT), lambda j: x0[:, j], xn, g["xn_ready"])
                    side(step + 11)
                    for s in slots:
                        dve.wait_ge(g["w1_done"], count(i, 4, 2 * l + s))
                        dve.wait_ge(g["gelu_ready"], count(i, 4, 2 * l + s))
                        for c, (o, n) in enumerate(CH):
                            src = ps0[0:n, 3, c * S:(c + 1) * S] if c < 2 else ps0[0:n, 2, S:2 * S]
                            last = nc.vector.scalar_tensor_tensor(ge[0:n, s, c], src, b1a[0:n, l, c:c + 1], ge[0:n, s, c],
                                                                  ALU.add, ALU.mult)
                        last.then_inc(g["u2_ready"], 1)
                        if s == 0:
                            side(step + 12)
                    side(step + 13)
                    for s in slots:
                        dve.wait_ge(g["x2T_done"], count(i, 4, 2 * l + s))
                        pr = ps0[:, 3 * s, 0:S]
                        if l == 0:
                            nc.vector.scalar_tensor_tensor(hT[0:64, s, 0:S], pr[0:64], b2[0:64, l:l + 1], x1T[0:64, s],
                                                           ALU.add, ALU.add)
                            nc.vector.scalar_tensor_tensor(hT[64:128, s, 1:S + 1], pr[64:128], b2[64:128, l:l + 1],
                                                           x1T[64:128, s], ALU.add, ALU.add)
                        nc.vector.scalar_tensor_tensor(xT[:, s], pr, b2[:, l:l + 1], x1T[:, s], ALU.add, ALU.add
                                                       ).then_inc(g["x2T_ready" if l else "h1_ready"], 1)
                    side(step + 14)
                dve.wait_ge(g["x2_done"], count(i, 1, 0))
                dve.wait_ge(g["xn_ready"], count(i + 1, 2, 1))
                vt(x1[:], ps0[:, 1, :].rearrange("p (j n) -> p j n", n=P), res[:], ALU.add).then_inc(g["x1_ready"], 1)
                dve.wait_ge(g["x1_ready"], count(i, 1, 0))
                moments(link, range(NT), lambda j: x1[:, j])
                side(STEPS - 1)
                assert links0() % DVE_LINKS[0] == 0, links0()

            def second(i, k, after):
                plan = ALONE if after is None else WOVEN
                def link(ins):
                    link1(i, ins)

                if k == TURN_Y:
                    dve.wait_ge(g["rstd_ready"], count(i, 6, 6))
                    normalise(link, range(NT), lambda j: x1[:, j], yn, g["y_ready"])
                if k == PROJECT:
                    dve.wait_ge(g["y_ready"], count(i, 2, 1))
                    vt(x1[:], x1[:], a_bo[:].unsqueeze(1).to_broadcast([P, NT, P]), ALU.add).then_inc(g["x1b_ready"], 1)
                    dve.wait_ge(g["proj_done"], count(i, 1, 0))
                    for s in slots:
                        vt(a_v[:, s], ps1[:, MOE_OUT, s * S:(s + 1) * S].rearrange("p (t n) -> p t n", t=2),
                           a_bv[:].unsqueeze(1).to_broadcast([P, 2, P]), ALU.add)
                    link(nc.vector.tensor_copy(g_l[:], ps1[:, MISC, 0:NT * EXPERTS].rearrange("p (t e) -> p t e", t=NT)))
                    for j in range(NT):
                        last = after_wait(nc.vector.max, g_m[:, j], g_l[:, j])
                    link(last)
                    for j in range(NT):
                        last = after_wait(nc.vector.max_index, g_i[:, j], g_m[:, j], g_l[:, j])
                    link(last)
                    nc.vector.tensor_copy(g_f[:], g_i[:])
                    vt(g_l[:], g_l[:], g_m[:, :, 0:1].to_broadcast([P, NT, EXPERTS]), ALU.subtract).then_inc(g["logit_ready"], 1)
                    for s in slots:
                        dve.wait_ge(g["qk1_ready"], count(i, 2, s))
                        link(nc.vector.tensor_reduce(kcs[:, s], a_kT[:, s, 0:S].rearrange("p (c n) -> p c n", n=COMP), AX_X, ALU.add))
                        nc.vector.tensor_scalar_mul(a_kT[:, s, S:S + SC], kcs[:, s], 1.0 / COMP).then_inc(g["kc_ready"], 1)
                if k == SCORES:
                    dve.wait_ge(g["e_ready"], count(i, 1, 0))
                    io = iota8[:].unsqueeze(1).to_broadcast([P, NT, EXPERTS])
                    vt(comb[:], io, g_f[:, :, 0:1].to_broadcast([P, NT, EXPERTS]), ALU.is_equal)
                    link(vt(g_m[:], io, g_f[:, :, 1:2].to_broadcast([P, NT, EXPERTS]), ALU.is_equal))
                    link(vt(comb[:], comb[:], g_m[:], ALU.add))
                    link(vt(comb[:], comb[:], g_e[:], ALU.mult))
                    link(nc.vector.tensor_reduce(g_s[:], comb[:], AX_X, ALU.add))
                    link(after_wait(nc.vector.reciprocal, g_s[:], g_s[:]))
                    vt(comb[:], comb[:], g_s[:].unsqueeze(2).to_broadcast([P, NT, EXPERTS]), ALU.mult).then_inc(g["comb_ready"], 1)
                if k == EXPERT_BIAS:
                    dve.wait_ge(g["b2_done"], count(i, 1, 0))
                    dve.wait_ge(g["x1b_ready"], count(i, 1, 0))
                    dve.wait_ge(stored, 16 * i)
                    vt(y_out[:], ps1[:, MISC, :].rearrange("p (j n) -> p j n", n=P), x1[:], ALU.add).then_inc(g["acc0_ready"], 1)
                if k in plan.add:
                    e = plan.add.index(k)
                    dve.wait_ge(g["eo_done"], count(i, EXPERTS, e))
                    if e == 0:
                        dve.wait_ge(g["acc0_ready"], count(i, 1, 0))
                    else:
                        dve.wait_ge(g["acc_done"], count(i, EXPERTS, e - 1))
                    for j in range(NT):
                        last = nc.vector.scalar_tensor_tensor(y_out[:, j], ps1[:, MOE_OUT, tok(j)], comb[:, j, e:e + 1], y_out[:, j],
                                                              ALU.mult, ALU.add)
                    last.then_inc(g["acc_done"], 1)
                if k in plan.top:
                    j, part = plan.top.index(k) // 4, plan.top.index(k) % 4
                    if part == 0:
                        dve.wait_ge(g["raw_ready"], count(i, NT, j))
                    for r in (2 * part, 2 * part + 1):
                        src = raw[:, j, 0:S] if r == 0 else wrk[:, j]
                        link(after_wait(nc.vector.max, top8[:, j], src))
                        if r == 0:
                            nc.vector.tensor_scalar(nmax[:, j, 0:1], top8[:, j, 0:1], 0.0, -1.0, ALU.max, ALU.mult)
                        last = after_wait(nc.vector.match_replace, wrk[:, j], top8[:, j], src, -BIG)
                        if r < TOP_K // 8 - 1:
                            link(last)
                    if part == 3:
                        last.then_inc(g["top_ready"], 1)
                        dve.wait_ge(g["cm_ready"], count(i, NT, j))
                        nc.vector.tensor_reduce(nmax[:, j, 1:2], csc[:, j, 0:P * (j % 2 + 1)], AX_X, ALU.max, negate=True)
                        nc.vector.tensor_reduce(nmax[:, j, 2:3], raw[:, j, S:], AX_X, ALU.max, negate=True
                                                ).then_inc(g["cmax_ready"], 1)
                if k in plan.combine:
                    j = plan.combine.index(k)
                    n = P * (j % 2 + 1)
                    dve.wait_ge(g["ex_ready"], count(i, NT, j))
                    link(after_wait(nc.vector.reciprocal, lsum[:, j], lsum[:, j]))
                    link(vt(lsum[:, j], lsum[:, j], third[:], ALU.mult))
                    link(nc.vector.tensor_scalar(wrk[:, j], wrk[:, j], lsum[:, j, 0:1], None, ALU.mult))
                    link(nc.vector.scalar_tensor_tensor(wrk[:, j, 0:n], csc[:, j, 0:n], lsum[:, j, 1:2], wrk[:, j, 0:n],
                                                        ALU.mult, ALU.add))
                    w4 = wrk[:, j].rearrange("p (c n) -> p c n", n=COMP)
                    nc.vector.scalar_tensor_tensor(w4, raw[:, j, S:].unsqueeze(2).to_broadcast([P, SC, COMP]),
                                                   lsum[:, j, 2:3], w4, ALU.mult, ALU.add).then_inc(g["pw_ready"], 1)
                if k in plan.add_attention:
                    s = plan.add_attention.index(k)
                    js = slice(2 * s, 2 * s + 2)
                    dve.wait_ge(g["wo_done"], count(i, 2, s))
                    dve.wait_ge(g["acc_done"], count(i, EXPERTS, max(e for e in range(EXPERTS) if plan.add[e] <= k)))
                    last = vt(y_out[:, js], ps1[:, MISC, 0:S].rearrange("p (t n) -> p t n", t=2), y_out[:, js], ALU.add)
                    last.then_inc(g[("half_ready", "out_ready")[s]], 1)
                    if s == 0:
                        dve.wait_ge(g["half_ready"], count(i, 1, 0))
                if k == plan.steps - 1:
                    assert links1() % DVE_LINKS[1] == 0, links1()

            pipeline(dve, first, second)

        @block.tensor
        def _(pe):
            def mm(out, a, b, start=True, stop=True):
                return nc.tensor.matmul(out, a, b, start=start, stop=stop)

            pe.wait_ge(prep_a, 3)

            def first(i, side, before):
                for s in slots:
                    pe.wait_ge(g["xn_ready"], count(i, 2, s))
                    for t in tiles:
                        last = nc.tensor.transpose(ps0[:, 2 * s, tok(t)], xn[:, 2 * s + t], ident[:])
                    last.then_inc(g["xnT_done"], 1)
                if before is not None:
                    pe.wait_ge(g["x1_ready"], count(before, 1, 0))
                for s in slots:
                    pe.wait_ge(g["xT_ready"], count(i, 2, s))
                    for t in tiles:
                        last = mm(ps0[:, 2 * s + 1, tok(t)], xT[:, s, tok(t)], fw_q[:])
                    last.then_inc(g["q0_done"], 1)
                side(0)
                side(1)
                side(2)
                for s in slots:
                    pe.wait_ge(g["qn0_ready"], count(i, 2, s))
                    for t in tiles:
                        last = nc.tensor.transpose(ps0[:, 2 * s, tok(t)], q0s[:, 2 * s + t], ident[:])
                    last.then_inc(g["qT0_done"], 1)
                for s in slots:
                    pe.wait_ge(g["qT0_ready"], count(i, 2, s))
                    for p in range(2):
                        r = slice(64 * p, 64 * p + 64)
                        mm(ps0[:, 2 * s + p, 0:S], fw_gate[r, :], q0T[r, s, :])
                        last = mm(ps0[:, 2 * s + p, S:2 * S], fw_up[r, :], q0T[r, s, :])
                    last.then_inc(g["gu_done"], 1)
                side(3)
                side(4)
                for s in slots:
                    pe.wait_ge(g["hid_ready"], count(i, 2, s))
                    for t in tiles:
                        for p in range(2):
                            last = mm(ps0[:, 2 * s + 1, P * t + 64 * p:P * t + 64 * p + 64], th[:, s, p, tok(t)], fw_down[:, p, :])
                    last.then_inc(g["o0_done"], 1)
                side(5)
                side(6)
                if before is None:
                    pe.wait_ge(loaded[1], 16 * n_load[1])

                for l in range(DEPTH):
                    step = BLOCK[l]

                    def q_and_k(j):
                        s, t = units[j]
                        if j < 2 and l == 0:
                            pe.wait_ge(x_used, count(i, 2, j))
                        if j < 2 and l == 1:
                            pe.wait_ge(g["h1_ready"], count(i, 2, j))
                        if j >= 2:
                            pe.wait_ge(g["qn_ready"], count(i, 8, 4 * l + j - 2))
                        mm(ps0[:, 2 * t, :], hT[:, s, tok(t)], wqkv[:, l, 0:INNER])
                        mm(ps0[:, 2 * t + 1, :], hT[:, s, tok(t)], wqkv[:, l, INNER:2 * INNER]).then_inc(g["qk_done"], 1)

                    def values(s):
                        for t in tiles:
                            if s == 1:
                                pe.wait_ge(g["v_ready"], count(i, 8, 4 * l + t))
                            elif before is not None:
                                m = max(m for m in range(2 * EXPERTS) if WOVEN.up[m] <= step + 1)
                                pe.wait_ge(g["relu_done"], count(before, EXPERTS * EC, 2 * m + t))
                            mm(ps1[:, t, :], hT[:, s, tok(t)], wqkv[:, l, 2 * INNER:3 * INNER]).then_inc(g["v_done"], 1)

                    def turn_qk(j):
                        s, t = units[j]
                        pe.wait_ge(g["s1_ready" if t else "s_ready"], count(i, 4, 2 * l + s))
                        if j < 2:
                            pe.wait_ge(g["qn_ready"], count(i, 8, 4 * l + j + 2))
                        else:
                            pe.wait_ge(g["qkT_ready"], count(i, 8, 4 * l + j - 2))
                        for a in range(8):
                            last = nc.tensor.transpose(ps0[:, 2 * t + a // 4, P * (a % 4):P * (a % 4) + P],
                                                       bufC[:, j].rearrange("p a b -> p (a b)")[:, a * P:(a + 1) * P], ident[:])
                        last.then_inc(g["qkT_done"], 1)

                    q_and_k(0)
                    q_and_k(1)
                    side(step)
                    q_and_k(2)
                    side(step + 1)
                    values(0)
                    q_and_k(3)
                    values(1)
                    side(step + 2)
                    turn_qk(0)
                    side(step + 3)
                    turn_qk(1)
                    side(step + 4)
                    turn_qk(2)
                    turn_qk(3)
                    for j, (s, t) in enumerate(units):
                        if j < 2:
                            pe.wait_ge(g["qkT_ready"], count(i, 8, 4 * l + j + 2))
                        else:
                            pe.wait_ge(g["max_ready" if t else "p_ready"], count(i, 8, 4 * l + j - 2))
                        for h in range(2):
                            o = ps0[:, 2 * t + h, :]
                            mm(o, identb[:], bandb[:, t, :].unsqueeze(1).to_broadcast([P, 4, P]), stop=False)
                            r = slice(64 * h, 64 * h + 64)
                            for a in range(4):
                                c = a * P
                                q, kk = qkT[r, s, a], qkT[r, s, 4 + a]
                                if t == 0:
                                    last = mm(o[:, c:c + P], q[:, 0:P], kk[:, 0:P], start=False, stop=(a == 3))
                                else:
                                    mm(o[:, c:c + 64], q[:, P:2 * P], kk[:, P:P + 64], start=False, stop=False)
                                    mm(o[0:64, c + 64:c + P], q[:, P:P + 64], kk[:, 64:P], start=False, stop=(a == 3))
                                    last = mm(o[64:128, c + 64:c + P], q[:, P + 64:2 * P], kk[:, P + 64:2 * P],
                                              start=False, stop=(a == 3))
                        last.then_inc(g["sim_done"], 1)
                        if j == 1:
                            side(step + 5)
                    side(step + 6)
                    for j, (s, t) in enumerate(units):
                        pe.wait_ge(g["pn1_ready" if t else "pn_ready"], count(i, 4, 2 * l + s))
                        if j < 2:
                            pe.wait_ge(g["max_ready" if t else "p_ready"], count(i, 8, 4 * l + j + 2))
                        else:
                            pe.wait_ge(g["pT_ready"], count(i, 8, 4 * l + j - 2))
                        for a in range(8):
                            last = nc.tensor.transpose(ps0[:, 2 * t + a // 4, P * (a % 4):P * (a % 4) + P],
                                                       bufB[:, j].rearrange("p a b -> p (a b)")[:, a * P:(a + 1) * P], ident[:])
                        last.then_inc(g["pT_done"], 1)
                        if j == 1:
                            side(step + 7)
                    side(step + 8)
                    for j, (s, t) in enumerate(units):
                        pe.wait_ge(g["pT_ready"], count(i, 8, 4 * l + max(j, 2 + t)))
                        if t == 1:
                            pe.wait_ge(g["vmix_ready"], count(i, 4, 2 * l + s))
                        pT = bufC[:, j].rearrange("p a b -> p (a b)").rearrange("p (h n) -> p h n", n=P)
                        for a in range(4):
                            for h in range(2):
                                o = ps0[64 * h:64 * h + 64, 2 * t + s, a * P:(a + 1) * P]
                                hd = slice(64 * (2 * a + h), 64 * (2 * a + h) + 64)
                                if t == 0:
                                    last = mm(o, v[:, s, 0, hd], pT[:, 4 * h + a, :])
                                else:
                                    mm(o[:, 0:64], vmix[:, s, hd], pT[:, 4 * h + a, 0:64])
                                    last = mm(o[:, 64:128], v[:, s, 1, hd], pT[:, 4 * h + a, 64:128])
                        last.then_inc(g["oT_done"], 1)
                    side(step + 9)
                    for s in slots:
                        pe.wait_ge(g["oT_ready"], count(i, 8, 4 * l + (3 if s else 2)))
                        for a in range(4):
                            last = mm(ps0[:, s, 0:S], wo[:, l, a, :], oT[:, s, a, :], start=(a == 0), stop=(a == 3))
                        last.then_inc(g["x1T_done"], 1)
                    side(step + 10)
                    for s in slots:
                        pe.wait_ge(g["h2_ready"], count(i, 4, 2 * l + s))
                        for t in tiles:
                            last = nc.tensor.transpose(ps0[:, 2 + s, tok(t)], hT[:, s, tok(t)], ident[:])
                        last.then_inc(g["h2tok_done"], 1)
                    side(step + 11)
                    for s in slots:
                        pe.wait_ge(g["hn_ready"], count(i, 4, 2 * l + s))
                        for t in tiles:
                            last = nc.tensor.transpose(ps0[:, s, tok(t)], xn[:, 2 * s + t], ident[:])
                        last.then_inc(g["hnT_done"], 1)

                    def hidden(s, half, c):
                        o, n = CH[c]
                        bank = 2 if c == 2 else (s if half else 3)
                        at = c * S if c < 2 else (1 - half) * S
                        return mm(ps0[0:n, bank, at:at + S], w1[:, l, half * HID + o:half * HID + o + n], hnT[:, s, :])

                    for s in slots:
                        pe.wait_ge(g["hnT_ready"], count(i, 4, 2 * l + s))
                        hidden(s, 1, 0)
                        hidden(s, 1, 1).then_inc(g["gate_done"], 1)
                        if s == 1:
                            side(step + 12)
                            pe.wait_ge(g["u2_ready"], count(i, 4, 2 * l))
                        hidden(s, 1, 2)
                        hidden(s, 0, 2)
                        hidden(s, 0, 0)
                        hidden(s, 0, 1).then_inc(g["w1_done"], 1)
                    side(step + 13)
                    for s in slots:
                        pe.wait_ge(g["u2_ready"], count(i, 4, 2 * l + s))
                        for c, (o, n) in enumerate(CH):
                            last = mm(ps0[:, 3 * s, 0:S], w2[0:n, l, c, :], ge[0:n, s, c, :], start=(c == 0), stop=(c == len(CH) - 1))
                        last.then_inc(g["x2T_done"], 1)
                    side(step + 14)
                for s in slots:
                    pe.wait_ge(g["x2T_ready"], count(i, 2, s))
                    for t in tiles:
                        last = nc.tensor.transpose(ps0[:, 1, tok(2 * s + t)], xT[:, s, tok(t)], ident[:])
                last.then_inc(g["x2_done"], 1)
                side(STEPS - 1)

            def second(i, k, after):
                plan = ALONE if after is None else WOVEN
                if k == TURN_Y:
                    for s in slots:
                        pe.wait_ge(g["y_ready"], count(i, 2, s))
                        for t in tiles:
                            last = nc.tensor.transpose(ps1[:, MISC, tok(2 * s + t)], yn[:, 2 * s + t], ident[:])
                    last.then_inc(g["yTp_done"], 1)
                if k == PROJECT:
                    pe.wait_ge(g["yT_ready"], count(i, 1, 0))
                    for s in slots:
                        mm(ps1[:, s, 0:S], a_wq[:], yT[:, s, :])
                        mm(ps1[:, s, S:2 * S], a_wk[:], yT[:, s, :])
                        for t in tiles:
                            mm(ps1[:, MOE_OUT, tok(2 * s + t)], yT[:, s, tok(t)], a_wv[:])
                    for j, (s, t) in enumerate(units):
                        last = mm(ps1[:, MISC, EXPERTS * j:EXPERTS * (j + 1)], yT[:, s, tok(t)], m_gate[:])
                    last.then_inc(g["proj_done"], 1)
                if k == SCORES:
                    for j, (s, t) in enumerate(units):
                        pe.wait_ge(g["kc_ready"], count(i, 2, s if j != 1 else 1))
                        if j >= 2:
                            pe.wait_ge(g["raw_ready"], count(i, NT, j - 2))
                        mm(ps1[:, j % 2, 0:S + SC], a_qT[:, s, tok(t)], a_kT[:, s, 0:S + SC]).then_inc(g["sc_done"], 1)
                if k == TURN_COMB:
                    pe.wait_ge(g["comb_ready"], count(i, 1, 0))
                    for j in range(NT):
                        last = nc.tensor.transpose(ps1[0:EXPERTS, MISC, tok(j)], comb[:, j, :], ident[:])
                    last.then_inc(g["combT_done"], 1)
                for e, c in chunks(plan, k):
                    n = EC * e + c
                    if n >= 2:
                        pe.wait_ge(g["relu_done"], count(i, EXPERTS * EC, n - 2))
                    else:
                        pe.wait_ge(g["raw_ready"], count(i, NT, 2 + n))
                    for l in range(DEPTH):
                        m, taken = n // 2, BLOCK[l] + 1
                        if after is not None and plan.up[m] > taken and (m == 0 or plan.up[m - 1] <= taken):
                            pe.wait_ge(g["v_ready"], count(after, 8, 4 * l + 2 + c % 2))
                    mm(ps1[:, c % 2, :], m_w1[:, e, c * P:(c + 1) * P], yT[:].rearrange("p s n -> p (s n)")
                       ).then_inc(g["h_done"], 1)
                for m in [m for m, at in enumerate(plan.down) if at == k]:
                    e = m // 2
                    pe.wait_ge(g["relu_done"], count(i, EXPERTS * EC, EC * e + EC - 1))
                    if e >= 1:
                        pe.wait_ge(g["acc_done"], count(i, EXPERTS, e - 1))
                    for j in (2 * (m % 2), 2 * (m % 2) + 1):
                        for c in range(EC):
                            last = mm(ps1[:, MOE_OUT, tok(j)], hbuf[:, c, tok(j)], m_w2[:, e, c, :], start=(c == 0), stop=(c == EC - 1))
                    if m % 2 == 1:
                        last.then_inc(g["eo_done"], 1)
                if k == EXPERT_BIAS:
                    pe.wait_ge(g["combT_ready"], count(i, 1, 0))
                    for j in range(NT):
                        last = mm(ps1[:, MISC, tok(j)], combT[:, tok(j)], m_b2[:])
                    last.then_inc(g["b2_done"], 1)
                if k in plan.p_turn:
                    j = plan.p_turn.index(k)
                    pe.wait_ge(g["pw_ready"], count(i, NT, j))
                    if j == 1 or j == 3:
                        pe.wait_ge(g["pwT_ready"], count(i, NT, j - 1))
                    if j == 2:
                        pe.wait_ge(g["half_ready"], count(i, 1, 0))
                    for a in range(2):
                        last = nc.tensor.transpose(ps1[:, MISC, a * P:(a + 1) * P], wrk[:, j, a * P:(a + 1) * P], ident[:])
                    last.then_inc(g["pwT_done"], 1)
                if k in plan.attend:
                    s = plan.attend.index(k)
                    pe.wait_ge(g["pwT_ready"], count(i, NT, 2 * s + 1))
                    for a in range(2):
                        last = mm(ps1[:, MISC, 0:S], a_v[:, s, a, :], a_pT[:, s, a, :], start=(a == 0), stop=(a == 1))
                    last.then_inc(g["at_done"], 1)
                    pe.wait_ge(g["at_ready"], count(i, 2, s))
                    for t in tiles:
                        last = mm(ps1[:, MISC, tok(t)], a_oT[:, s, tok(t)], a_wo[:])
                    last.then_inc(g["wo_done"], 1)

            pipeline(pe, first, second)


def shape_constants():
    import numpy as np
    f = np.float32
    half = np.arange(0, DIM_HEAD, 2, dtype=f)
    inv = (f(1.0) / f(10000.0) ** (half / f(DIM_HEAD))).astype(f)
    t = np.arange(S, dtype=f)
    fr = (t[:, None] * inv[None, :]).astype(f)
    fr = np.concatenate([fr, fr], -1)
    base = ((half + f(0.4 * DIM_HEAD)) / f(1.4 * DIM_HEAD)).astype(f)
    power = ((t - S // 2) / f(WINDOW // 2)).astype(f)
    sc = (base[None, :] ** power[:, None]).astype(f)
    sc = np.concatenate([sc, sc], -1)
    cos, sin = np.cos(fr).astype(f), np.sin(fr).astype(f)
    sgn = np.concatenate([-np.ones(DIM_HEAD // 2, f), np.ones(DIM_HEAD // 2, f)])
    rot_cos = np.stack([cos * sc, cos / sc], 1).astype(f)
    rot_sin = np.stack([sin * sc * sgn, sin / sc * sgn], 1).astype(f)
    q, c = np.arange(P)[:, None], np.arange(P)[None, :]
    ok0 = (c <= q) & (c >= q - WINDOW)
    qi, ci = q % WINDOW, c % WINDOW
    own = (q // WINDOW == 0) == (c // WINDOW == 0)
    ok1 = np.where(own, ci <= qi, ci >= qi)
    band = np.where(np.stack([ok0, ok1]), f(0), f(-1e30)).astype(f)
    causal = np.where(c <= q, f(0), f(-BIG)).astype(f)
    return {"ident": np.eye(P, dtype=f), "band": band, "causal": causal, "rot_cos": rot_cos, "rot_sin": rot_sin,
            "iota8": np.arange(EXPERTS, dtype=f)}


def kernel(**inputs):
    import numpy as np
    import concourse.bacc as bacc
    from concourse import mybir
    from concourse.bass_utils import run_bass_kernel_spmd as run

    a = {k: np.asarray(v) for k, v in inputs.items()}
    w = shape_constants()
    w["fw_q"] = a["L0_attn_qkv_w"][0:D].T
    w["q_norm_w"] = a["L0_attn_q_norm_w"]
    for n in ("w0", "w1", "w2"):
        w["fw_" + n] = a["L0_attn_" + n].transpose(0, 2, 1)
    for n in ("wqkv", "q_scale", "k_scale", "wo", "w1", "w2"):
        w[n] = a["L0_ffn_" + n]
    for n in ("Wq", "Wk", "Wv", "Wo", "bv", "bo"):
        w["a_" + n.lower()] = a["L1_attn_" + n]
    w["m_gate"] = a["L1_ffn_gate_w"].T
    w["m_w1"] = a["L1_ffn_w1"].transpose(2, 0, 1)
    w["m_w2"] = a["L1_ffn_w2"].reshape(EXPERTS, D, EC, P).transpose(3, 0, 2, 1)
    b1, columns = a["L0_ffn_b1"], np.zeros((P, 52), np.float32)
    for l in range(DEPTH):
        for c, (o, n) in enumerate(CH):
            columns[0:n, 3 * l + c] = b1[l, o:o + n]
            columns[0:n, 6 + 3 * l + c] = b1[l, HID + o:HID + o + n]
        columns[:, 12 + l], columns[:, 14 + l], columns[:, 16 + l] = (
            a["L0_ffn_b2"][l], a["L0_ffn_ln_g"][l], a["L0_ffn_ln_b"][l])
    columns[:, 18], columns[:, 19] = a["L1_attn_bq"], a["L1_attn_bk"]
    columns[:, 20:52] = a["L1_ffn_b1"].reshape(EXPERTS * EC, P).T
    w["cols"] = columns
    w["m_b2"] = a["L1_ffn_b2"]
    x = np.ascontiguousarray(a["L0_attn_hidden_states"])

    nc = bacc.Bacc("TRN2", target_bir_lowering=False, num_devices=1)
    arrays, aps = {"x": x}, {}
    for name, value in w.items():
        arrays["in_" + name] = np.ascontiguousarray(value)
        aps[name] = nc.dram_tensor("in_" + name, value.shape, mybir.dt.from_np(value.dtype), kind="ExternalInput").ap()
    x_d = nc.dram_tensor("x", x.shape, mybir.dt.float32, kind="ExternalInput").ap()
    out_d = nc.dram_tensor("out", x.shape, mybir.dt.float32, kind="ExternalOutput").ap()
    build(nc, x_d, out_d, aps)
    r = run(nc, [arrays], core_ids=[0])
    return r.results[0]["out"]
```
